# Optimizing a Trainium2 kernel written in Bass

```python
import numpy as np
import jax
import jax.numpy as jnp

def _softmax(x, axis=-1):
    return jax.nn.softmax(x, axis=axis)

def _gelu(x):
    return jax.nn.gelu(x, approximate=True)

def _silu(x):
    return jax.nn.silu(x)

def _sigmoid(x):
    return jax.nn.sigmoid(x)

def _layernorm(x, axis=-1, eps=1e-05):
    m = jnp.mean(x, axis=axis, keepdims=True)
    v = jnp.var(x, axis=axis, keepdims=True)
    return (x - m) / jnp.sqrt(v + eps)

def _scatter_add(tgt, idx, src, axis=0):
    return tgt.at[idx].add(src)

def _segment_sum(src, seg, n):
    return jax.ops.segment_sum(src, seg, n)
kernel_name = 'mk_gnn_resnorm_d2_gnn_r32_6c8cea'

def setup_inputs(seed: int=0):
    np.random.seed(seed)
    _w = jnp.asarray

    def _rec_inputs():
        import jax
        import jax.numpy as jnp
        _gk = jax.random.key(seed)
        x = -0.0003713 + 1 * jax.random.normal(jax.random.fold_in(_gk, 1), (3125, 128), jnp.float32)
        _s = jax.random.randint(jax.random.fold_in(_gk, 2), (50000,), 0, 3125, jnp.int32)
        _d = jax.random.randint(jax.random.fold_in(_gk, 3), (50000,), 0, 3125, jnp.int32)
        _loop = jnp.arange(3125, dtype=jnp.int32)
        src = jnp.concatenate([_s, _d, _loop])
        dst = jnp.concatenate([_d, _s, _loop])
        _o = jnp.argsort(dst, stable=True)
        src = src[_o]
        dst = dst[_o]
        edge_attr_3 = -0.000451519 + 1.00018 * jax.random.normal(jax.random.fold_in(_gk, 12), (103125, 3), jnp.float32)
        edge_weight = jax.random.uniform(jax.random.fold_in(_gk, 14), (103125,), jnp.float32, 0.0, 0.999998)
        return (x, src, dst, edge_attr_3, edge_weight)
    x, src, dst, edge_attr_3, edge_weight = _rec_inputs()

    def _L0_gnn_setup():
        import jax, jax.numpy as jnp
        import numpy as np
        N = 3125
        E = 15625
        D = 128
        H = 4
        C = 32
        HID = 512
        EPS = 1e-05

        def _layer_norm(x, w, b):
            mu = jnp.mean(x, axis=-1, keepdims=True)
            var = jnp.mean(jnp.square(x - mu), axis=-1, keepdims=True)
            return (x - mu) * jax.lax.rsqrt(var + EPS) * w + b

        def _transformer_conv(x, src, dst, Wq, bq, Wk, bk, Wv, bv, Wskip, bskip):
            q = (x @ Wq.T + bq).reshape(N, H, C)
            k = (x @ Wk.T + bk).reshape(N, H, C)
            v = (x @ Wv.T + bv).reshape(N, H, C)
            alpha = jnp.sum(q[dst] * k[src], axis=-1) / np.sqrt(C)
            m = jax.ops.segment_max(alpha, dst, num_segments=N)
            e = jnp.exp(alpha - m[dst])
            z = jax.ops.segment_sum(e, dst, num_segments=N)
            a = e / z[dst]
            msg = a[:, :, None] * v[src]
            out = jax.ops.segment_sum(msg, dst, num_segments=N)
            return out.reshape(N, H * C) + x @ Wskip.T + bskip
        key = jax.random.key(seed)
        ks = jax.random.split(key, 16)
        s = 1.0 / np.sqrt(D)
        inp = {'x': jax.random.normal(ks[0], (N, D), dtype=jnp.float32), 'edge_index': jax.random.randint(ks[1], (2, E), 0, N, dtype=jnp.int64), 'Wq': jax.random.normal(ks[2], (D, D), dtype=jnp.float32) * s, 'bq': jnp.zeros((D,), jnp.float32), 'Wk': jax.random.normal(ks[3], (D, D), dtype=jnp.float32) * s, 'bk': jnp.zeros((D,), jnp.float32), 'Wv': jax.random.normal(ks[4], (D, D), dtype=jnp.float32) * s, 'bv': jnp.zeros((D,), jnp.float32), 'Wskip': jax.random.normal(ks[5], (D, D), dtype=jnp.float32) * s, 'bskip': jnp.zeros((D,), jnp.float32), 'Wout': jax.random.normal(ks[6], (D, D), dtype=jnp.float32) * s, 'bout': jnp.zeros((D,), jnp.float32), 'ln1_w': jnp.ones((D,), jnp.float32), 'ln1_b': jnp.zeros((D,), jnp.float32), 'ln2_w': jnp.ones((D,), jnp.float32), 'ln2_b': jnp.zeros((D,), jnp.float32), 'W1': jax.random.normal(ks[7], (HID, D), dtype=jnp.float32) * s, 'b1': jnp.zeros((HID,), jnp.float32), 'W2': jax.random.normal(ks[8], (D, HID), dtype=jnp.float32) * (1.0 / np.sqrt(HID)), 'b2': jnp.zeros((D,), jnp.float32)}
        return inp
    _L0_gnn_all = _L0_gnn_setup()
    _L0_gnn_in = {k: v for k, v in _L0_gnn_all.items() if k in ('Wq', 'bq', 'Wk', 'bk', 'Wv', 'bv', 'Wskip', 'bskip', 'Wout', 'bout', 'ln1_w', 'ln1_b', 'W1', 'b1', 'W2', 'b2', 'ln2_w', 'ln2_b')}
    del _L0_gnn_all

    def _L1_gnn_setup():
        import jax, jax.numpy as jnp
        import numpy as np
        N = 50000
        E = 25000
        MUL = 32
        NB = 8
        R_MAX = 1.0
        AVG = 16.0
        SQ3 = 3.0 ** 0.5

        def _radial_embedding(r):
            x = jnp.clip(r / R_MAX, 0.0, 1.0)
            centers = jnp.arange(NB, dtype=jnp.float32) / (NB - 1)
            sigma = 1.0 / (NB - 1)
            emb = jnp.exp(-0.5 * ((x[:, None] - centers[None, :]) / sigma) ** 2)
            emb = emb * NB ** 0.5 * (r <= R_MAX).astype(jnp.float32)[:, None]
            return emb
        key = jax.random.key(seed)
        k = jax.random.split(key, 12)
        inp = {'node_feats': jax.random.normal(k[0], (N, 4 * MUL), dtype=jnp.float32), 'edge_vec': jax.random.normal(k[1], (E, 3), dtype=jnp.float32), 'edge_length': jax.random.uniform(k[2], (E,), dtype=jnp.float32), 'senders': jax.random.randint(k[3], (E,), 0, N, dtype=jnp.int32), 'receivers': jax.random.randint(k[4], (E,), 0, N, dtype=jnp.int32), 'num_nodes': N, 'W_up0': jax.random.normal(k[5], (MUL, MUL), dtype=jnp.float32), 'W_up1': jax.random.normal(k[6], (MUL, MUL), dtype=jnp.float32), 'mlp_w0': jax.random.normal(k[7], (NB, 64), dtype=jnp.float32) / NB ** 0.5, 'mlp_b0': jnp.zeros((64,), dtype=jnp.float32), 'mlp_w1': jax.random.normal(k[8], (64, 64), dtype=jnp.float32) / 8.0, 'mlp_b1': jnp.zeros((64,), dtype=jnp.float32), 'mlp_w2': jax.random.normal(k[9], (64, 4 * MUL), dtype=jnp.float32) / 8.0, 'mlp_b2': jnp.zeros((4 * MUL,), dtype=jnp.float32), 'W_out0': jax.random.normal(k[10], (2 * MUL, MUL), dtype=jnp.float32), 'W_out1': jax.random.normal(k[11], (2 * MUL, MUL), dtype=jnp.float32)}
        return inp
    _L1_gnn_all = _L1_gnn_setup()
    _L1_gnn_in = {k: v for k, v in _L1_gnn_all.items() if k in ('W_up0', 'W_up1', 'mlp_w0', 'mlp_b0', 'mlp_w1', 'mlp_b1', 'mlp_w2', 'mlp_b2', 'W_out0', 'W_out1')}
    del _L1_gnn_all
    return {'x': x, 'src': src, 'dst': dst, 'edge_attr_3': edge_attr_3, 'edge_weight': edge_weight, 'L0_gnn_Wq': _L0_gnn_in['Wq'], 'L0_gnn_bq': _L0_gnn_in['bq'], 'L0_gnn_Wk': _L0_gnn_in['Wk'], 'L0_gnn_bk': _L0_gnn_in['bk'], 'L0_gnn_Wv': _L0_gnn_in['Wv'], 'L0_gnn_bv': _L0_gnn_in['bv'], 'L0_gnn_Wskip': _L0_gnn_in['Wskip'], 'L0_gnn_bskip': _L0_gnn_in['bskip'], 'L0_gnn_Wout': _L0_gnn_in['Wout'], 'L0_gnn_bout': _L0_gnn_in['bout'], 'L0_gnn_ln1_w': _L0_gnn_in['ln1_w'], 'L0_gnn_ln1_b': _L0_gnn_in['ln1_b'], 'L0_gnn_W1': _L0_gnn_in['W1'], 'L0_gnn_b1': _L0_gnn_in['b1'], 'L0_gnn_W2': _L0_gnn_in['W2'], 'L0_gnn_b2': _L0_gnn_in['b2'], 'L0_gnn_ln2_w': _L0_gnn_in['ln2_w'], 'L0_gnn_ln2_b': _L0_gnn_in['ln2_b'], 'L1_gnn_W_up0': _L1_gnn_in['W_up0'], 'L1_gnn_W_up1': _L1_gnn_in['W_up1'], 'L1_gnn_mlp_w0': _L1_gnn_in['mlp_w0'], 'L1_gnn_mlp_b0': _L1_gnn_in['mlp_b0'], 'L1_gnn_mlp_w1': _L1_gnn_in['mlp_w1'], 'L1_gnn_mlp_b1': _L1_gnn_in['mlp_b1'], 'L1_gnn_mlp_w2': _L1_gnn_in['mlp_w2'], 'L1_gnn_mlp_b2': _L1_gnn_in['mlp_b2'], 'L1_gnn_W_out0': _L1_gnn_in['W_out0'], 'L1_gnn_W_out1': _L1_gnn_in['W_out1']}

def reference(x, src, dst, edge_attr_3, edge_weight, L0_gnn_Wq, L0_gnn_bq, L0_gnn_Wk, L0_gnn_bk, L0_gnn_Wv, L0_gnn_bv, L0_gnn_Wskip, L0_gnn_bskip, L0_gnn_Wout, L0_gnn_bout, L0_gnn_ln1_w, L0_gnn_ln1_b, L0_gnn_W1, L0_gnn_b1, L0_gnn_W2, L0_gnn_b2, L0_gnn_ln2_w, L0_gnn_ln2_b, L1_gnn_W_up0, L1_gnn_W_up1, L1_gnn_mlp_w0, L1_gnn_mlp_b0, L1_gnn_mlp_w1, L1_gnn_mlp_b1, L1_gnn_mlp_w2, L1_gnn_mlp_b2, L1_gnn_W_out0, L1_gnn_W_out1):
    import jax
    import jax.numpy as jnp

    def _L0_gnn_ref(x, Wq, bq, Wk, bk, Wv, bv, Wskip, bskip, Wout, bout, ln1_w, ln1_b, W1, b1, W2, b2, ln2_w, ln2_b, edge_index):
        import jax, jax.numpy as jnp
        import numpy as np
        N = 3125
        E = 15625
        D = 128
        H = 4
        C = 32
        HID = 512
        EPS = 1e-05

        def _layer_norm(x, w, b):
            mu = jnp.mean(x, axis=-1, keepdims=True)
            var = jnp.mean(jnp.square(x - mu), axis=-1, keepdims=True)
            return (x - mu) * jax.lax.rsqrt(var + EPS) * w + b

        def _transformer_conv(x, src, dst, Wq, bq, Wk, bk, Wv, bv, Wskip, bskip):
            q = (x @ Wq.T + bq).reshape(N, H, C)
            k = (x @ Wk.T + bk).reshape(N, H, C)
            v = (x @ Wv.T + bv).reshape(N, H, C)
            alpha = jnp.sum(q[dst] * k[src], axis=-1) / np.sqrt(C)
            m = jax.ops.segment_max(alpha, dst, num_segments=N)
            e = jnp.exp(alpha - m[dst])
            z = jax.ops.segment_sum(e, dst, num_segments=N)
            a = e / z[dst]
            msg = a[:, :, None] * v[src]
            out = jax.ops.segment_sum(msg, dst, num_segments=N)
            return out.reshape(N, H * C) + x @ Wskip.T + bskip
        src = edge_index[0]
        dst = edge_index[1]
        conv = _transformer_conv(x, src, dst, Wq, bq, Wk, bk, Wv, bv, Wskip, bskip)
        out1 = conv @ Wout.T + bout
        out2 = _layer_norm(out1 + x, ln1_w, ln1_b)
        h = jax.nn.relu(out2 @ W1.T + b1)
        out3 = h @ W2.T + b2
        out4 = _layer_norm(out3 + out2, ln2_w, ln2_b)
        return out4

    def _L1_gnn_ref(node_feats, edge_vec, edge_length, senders, receivers, num_nodes, W_up0, W_up1, mlp_w0, mlp_b0, mlp_w1, mlp_b1, mlp_w2, mlp_b2, W_out0, W_out1):
        import jax, jax.numpy as jnp
        import numpy as np
        N = 50000
        E = 25000
        MUL = 32
        NB = 8
        R_MAX = 1.0
        AVG = 16.0
        SQ3 = 3.0 ** 0.5

        def _radial_embedding(r):
            x = jnp.clip(r / R_MAX, 0.0, 1.0)
            centers = jnp.arange(NB, dtype=jnp.float32) / (NB - 1)
            sigma = 1.0 / (NB - 1)
            emb = jnp.exp(-0.5 * ((x[:, None] - centers[None, :]) / sigma) ** 2)
            emb = emb * NB ** 0.5 * (r <= R_MAX).astype(jnp.float32)[:, None]
            return emb
        f32 = jnp.float32
        rhat = edge_vec / (jnp.linalg.norm(edge_vec, axis=-1, keepdims=True) + 1e-12)
        Y1 = SQ3 * rhat
        emb = _radial_embedding(edge_length)
        h = jax.nn.silu(emb @ mlp_w0 + mlp_b0)
        h = jax.nn.silu(h @ mlp_w1 + mlp_b1)
        w = (h @ mlp_w2 + mlp_b2).reshape(-1, 4, MUL)
        s = node_feats[:, :MUL]
        v = node_feats[:, MUL:].reshape(-1, MUL, 3)
        xs = s @ W_up0 / f32(MUL) ** 0.5
        xv = jnp.einsum('nmc,mk->nkc', v, W_up1) / f32(MUL) ** 0.5
        ss = xs[senders]
        vv = xv[senders]
        m0 = w[:, 0] * ss
        m1 = w[:, 1][:, :, None] * ss[:, :, None] * Y1[:, None, :]
        m2 = w[:, 2][:, :, None] * vv
        m3 = w[:, 3] * (jnp.einsum('emc,ec->em', vv, Y1) / SQ3)
        mid_s = jnp.concatenate([m0, m3], axis=1)
        mid_v = jnp.concatenate([m1, m2], axis=1)
        msg_s = jax.ops.segment_sum(mid_s, receivers, num_segments=num_nodes)
        msg_v = jax.ops.segment_sum(mid_v, receivers, num_segments=num_nodes)
        out_s = msg_s @ W_out0 / f32(2 * MUL) ** 0.5
        out_v = jnp.einsum('nmc,mk->nkc', msg_v, W_out1) / f32(2 * MUL) ** 0.5
        out = jnp.concatenate([out_s, out_v.reshape(-1, 3 * MUL)], axis=1)
        return out / max(AVG, 1e-08)
    edge_index = jnp.stack([src, dst])
    x = _layernorm(x + _L0_gnn_ref(x, L0_gnn_Wq, L0_gnn_bq, L0_gnn_Wk, L0_gnn_bk, L0_gnn_Wv, L0_gnn_bv, L0_gnn_Wskip, L0_gnn_bskip, L0_gnn_Wout, L0_gnn_bout, L0_gnn_ln1_w, L0_gnn_ln1_b, L0_gnn_W1, L0_gnn_b1, L0_gnn_W2, L0_gnn_b2, L0_gnn_ln2_w, L0_gnn_ln2_b, edge_index), axis=-1)
    x = _layernorm(x + _L1_gnn_ref(x, edge_attr_3, edge_weight, src, dst, 3125, L1_gnn_W_up0, L1_gnn_W_up1, L1_gnn_mlp_w0, L1_gnn_mlp_b0, L1_gnn_mlp_w1, L1_gnn_mlp_b1, L1_gnn_mlp_w2, L1_gnn_mlp_b2, L1_gnn_W_out0, L1_gnn_W_out1), axis=-1)
    return x

_drawn_inputs = setup_inputs


def setup_inputs(seed=0):
    import zlib

    import numpy as np

    out = dict(_drawn_inputs(seed))
    spreads = {'L0_gnn_bq': (0.0, 0.8),
     'L0_gnn_bk': (0.0, 0.8),
     'L0_gnn_bv': (0.0, 0.1),
     'L0_gnn_bskip': (0.0, 0.1),
     'L0_gnn_bout': (0.0, 0.1),
     'L0_gnn_ln1_w': (1.0, 0.2),
     'L0_gnn_ln1_b': (0.0, 0.1),
     'L0_gnn_b1': (0.0, 0.1),
     'L0_gnn_b2': (0.0, 0.1),
     'L0_gnn_ln2_w': (1.0, 0.2),
     'L0_gnn_ln2_b': (0.0, 0.1),
     'L1_gnn_mlp_b0': (0.0, 0.531),
     'L1_gnn_mlp_b1': (0.0, 0.314),
     'L1_gnn_mlp_b2': (0.0, 0.1)}
    factors = {}
    for name, (base, spread) in spreads.items():
        noise = np.random.default_rng([zlib.crc32(name.encode()), seed]).standard_normal(out[name].shape)
        drawn = base * np.exp(spread * noise) if base else spread * noise
        out[name] = jnp.asarray(drawn.astype(out[name].dtype))
    for name, factor in factors.items():
        out[name] = (out[name] * factor).astype(out[name].dtype)
    return out
```

```python
from contextlib import ExitStack

import concourse.bass as bass
from concourse import mybir
import numpy as np

P = 128
F32 = mybir.dt.float32
BF16 = mybir.dt.bfloat16
I32 = mybir.dt.int32
U32 = mybir.dt.uint32
ALU = mybir.AluOpType
ACT = mybir.ActivationFunctionType
AX = mybir.AxisListType
ET = mybir.EngineType

N, E, D, H, C, HID = 3125, 103125, 128, 4, 32, 512
EPS = 1e-5
NB = 8
QT = 4
SLOTS = 4
BODY = QT * SLOTS
ITERS = -(-E // (P * BODY))
NT = ITERS * BODY
TC = -(-NT // P)
TPAD = TC * P
NODE_TILES = -(-(N + P) // P)
NW = NODE_TILES * P
NCH = 7
CW = -(-N // (NCH * 2)) * 2
GE = NT * P // 16
BIG = 1e38
QC = QT * P
assert NCH * CW <= NW and CW <= 512 and NT * P >= E and TPAD >= NT

K_ID, K_IOTA, K_COL, K_NEGB, K_LN, K_EPS = 0, 128, 256, 257, 258, 259
K_N = 260
V_BSKIP, V_BOUT, V_L1W, V_L1B, V_L2W, V_L2B, V_B2, V_B1, V_MB0, V_MB1 = 0, 1, 2, 3, 4, 5, 6, 7, 11, 12
V_N = 13
W_SKIP, W_OUT, W_1, W_2, W_UP, W_M1, W_M2, W_OA, W_OB, W_M0 = 0, 128, 256, 768, 1280, 1408, 1536, 1664, 1792, 1920
W_N = 2048


def build(nc, a, out):
    with ExitStack() as ctx:
        def sb(name, shape, dt=F32):
            return ctx.enter_context(nc.sbuf_tensor(name, shape, dt))

        def sem(name):
            return ctx.enter_context(nc.semaphore(name))

        def slot_sems(name, n=SLOTS):
            return [sem(f"{name}{i}") for i in range(n)]

        def dram(name, shape, dt=F32):
            return nc.dram_tensor(name, shape, dt, kind="Internal").ap()

        q_tab = dram("q_tab", [NW, D])
        kv_tab = dram("kv_tab", [NW, 2 * D])
        up_tab = dram("up_tab", [NW, D])
        v_edges = dram("v_edges", [P, NT * D])
        emb_rows = dram("emb_rows", [NB, NT * P])
        carry_in = dram("carry_in", [2 * H * TC, P])
        carry_out = dram("carry_out", [2 * H * TC, P])

        consts = sb("consts", [P, K_N])
        vecs = sb("vecs", [P, V_N])
        weights = sb("weights", [P, W_N])
        wqkv = sb("wqkv", [P, 3 * D])
        bqkv = sb("bqkv", [P, 3 * D])
        xT = sb("xT", [P, NW])
        src_col = sb("src_col", [P, NT + BODY], I32)
        dst_i = sb("dst_i", [P, NT], I32)
        base_i = sb("base_i", [P, NT], I32)
        rel = sb("rel", [P, NT])
        win = sb("win", [P, NT])
        yvec = sb("yvec", [P, NT * 3])
        alpha = sb("alpha", [P, TPAD, H])
        acc = sb("acc", [P, 2, NW])
        idx = sb("idx", [P, SLOTS, QT], I32)
        nbr_i = sb("nbr_i", [P, 2 * TC], I32)
        nbr = sb("nbr", [P, 2, TC])
        flag = sb("flag", [P, 2])
        b2p = sb("b2p", [P, 3, D], BF16)
        b2rows = sb("b2rows", [P, D], BF16)
        rows = sb("rows", [P, SLOTS, QT, 2 * D])
        qwin = sb("qwin", [P, SLOTS, QT, D])
        dstb = sb("dstb", [P, SLOTS, QC], I32)
        hot = sb("hot", [P, 2, QT, P])
        work = sb("work", [P, 2, QC])
        arena = sb("arena", [P, 4 * NW])
        small = sb("small", [P, P + 2 * H * TC])
        ones_mean = sb("ones_mean", [P, P])
        b2f = sb("b2f", [P, 3, D])
        b2rep = sb("b2rep", [P, QT, D], BF16)
        ones3 = sb("ones3", [P, P], BF16)
        ps = ctx.enter_context(nc.psum_tensor("ps", [P, 8, 512], F32))

        ident = consts[:, K_ID:K_ID + P]
        iota = consts[:, K_IOTA:K_IOTA + P]

        def vec(j, n=1):
            return vecs[:, j:j + n]

        def wt(off, n=P):
            return weights[:, off:off + n]

        emb = arena[:, 0:GE]
        emb_m = arena[:, GE:2 * GE]
        sc_t = arena[:, 0:H * TPAD].rearrange("p (h n) -> p h n", h=H)
        fw_t = arena[:, H * TPAD:2 * H * TPAD].rearrange("p (h n) -> p h n", h=H)
        tot_t = arena[:, 2 * H * TPAD:3 * H * TPAD].rearrange("p (h n) -> p h n", h=H)
        mask_dst = arena[:, 3 * H * TPAD:3 * H * TPAD + TPAD].bitcast(I32)
        mback = arena[:, 3 * H * TPAD + TPAD:3 * H * TPAD + 2 * TPAD]
        accf = acc[:].rearrange("p m n -> p (m n)")
        masks = accf[:, 0:3 * TPAD].rearrange("p (k n) -> p k n", k=3)
        rowi = accf[0:H, 3 * TPAD:7 * TPAD].bitcast(I32).rearrange("p (k n) -> p k n", k=4)
        rel_tmp = acc[:, 0, 0:NT]
        nrel = win[:]
        rowbuf = qwin[:].rearrange("p a b c -> p (a b c)")[0:H, 0:2 * TPAD].rearrange("p (k n) -> p k n", k=2)
        rowsf = rows[:].rearrange("p a b c -> p (a b c)")
        rowout = rowsf[0:H, 0:2 * (TPAD + 1)].rearrange("p (k n) -> p k n", k=2)
        rowmask = rowsf[0:H, 2 * (TPAD + 1):4 * TPAD + 2].rearrange("p (k n) -> p k n", k=2)
        exb = arena[:, 0:2 * QC].rearrange("p (b t f) -> p b t f", b=2, t=QT)
        msg0 = arena[:, 2 * QC:4 * QC].rearrange("p (b t f) -> p b t f", b=2, t=QT)
        R = [arena[:, j * NW:(j + 1) * NW] for j in range(4)]
        hbuf = rows[:].rearrange("p a b c -> p (a b c)")
        MA = arena[:, 0:2 * QC].rearrange("p (b t f) -> p b t f", b=2, t=QT)
        MB = arena[:, 2 * QC:4 * QC].rearrange("p (b t f) -> p b t f", b=2, t=QT)
        h1s = arena[:, 4 * QC:6 * QC].rearrange("p (b n) -> p b n", b=2)
        h2s = arena[:, 6 * QC:8 * QC].rearrange("p (b n) -> p b n", b=2)
        embb = arena[:, 8 * QC:10 * QC].rearrange("p (b n) -> p b n", b=2)
        vy = arena[:, 10 * QC:10 * QC + 2 * 384].rearrange("p (b t f) -> p b t f", b=2, t=QT)
        ub = arena[:, 12 * QC:12 * QC + 256].rearrange("p (b t f) -> p b t f", b=2, t=QT)
        tb = arena[:, 13 * QC:13 * QC + 512].rearrange("p (b t f) -> p b t f", b=4, t=QT)

        ld = {k: sem("ld_" + k) for k in ("const", "graph", "attr", "x", "mask", "r")}
        idx_ready, base_ready = sem("idx_ready"), sem("base_ready")
        prep, yprep = sem("prep"), sem("yprep")
        qkv_mm, qkv_sb, qkv_out = sem("qkv_mm"), sem("qkv_sb"), slot_sems("qkv_out", 2)
        r_clip, r_sq, r_exp, emb_out = sem("r_clip"), sem("r_sq"), sem("r_exp"), sem("emb_out")
        kv_in, a_in, v_out = slot_sems("kv_in"), slot_sems("a_in"), slot_sems("v_out")
        hotT_ready, qe_ready, prod_ready, score_ready = sem("hotT_ready"), sem("qe_ready"), sem("prod_ready"), sem("score_ready")
        tr_mm, tr_sb, scan_f, scan_b = sem("tr_mm"), sem("tr_sb"), sem("scan_f"), sem("scan_b")
        edge_cols, c_tr, c_sb, c_dma, c_scan, c_back, c_mm, c_use = (
            sem("edge_cols"), sem("c_tr"), sem("c_sb"), sem("c_dma"), sem("c_scan"), sem("c_back"), sem("c_mm"), sem("c_use"))
        mask_ready, mx, shifted, exp_ready, back_mm, back_sb = (
            sem("mask_ready"), sem("mx"), sem("shifted"), sem("exp_ready"), sem("back_mm"), sem("back_sb"))
        v_in, exb_ready, hot_ready, msg_ready, sum_ready, acc_step = (
            slot_sems("v_in"), sem("exb_ready"), sem("hot_ready"), sem("msg_ready"), sem("sum_ready"), sem("acc_step"))
        acc_zero, pad_zero, b2_in = sem("acc_zero"), sem("pad_zero"), sem("b2_in")
        conv_a, conv_b, conv, skip_mm, skip_sb, out1_mm = sem("conv_a"), sem("conv_b"), sem("conv"), sem("skip_mm"), sem("skip_sb"), sem("out1_mm")
        ln_in, mean_mm, centred, squared, var_mm, std, inv, scaled, ln_out = (
            sem("ln_in"), sem("mean_mm"), sem("centred"), sem("squared"), sem("var_mm"), sem("std"), sem("inv"), sem("scaled"), sem("ln_out"))
        h_mm, h_sb, mlp_mm = sem("h_mm"), sem("h_sb"), sem("mlp_mm")
        up_mm, up_sb, up_out = sem("up_mm"), sem("up_sb"), slot_sems("up_out", 2)
        idx2_ready, g_in, e_in = sem("idx2_ready"), slot_sems("g_in"), slot_sems("e_in", 2)
        h1_mm, h1_sb, h2_mm, h2_sb, w_mm = sem("h1_mm"), sem("h1_sb"), sem("h2_mm"), sem("h2_sb"), sem("w_mm")
        hot2_ready, u_ready, vy_ready, t1_ready, t2_ready, w_used, msgs_ready, g_used = (
            sem("hot2_ready"), sem("u_ready"), sem("vy_ready"), sem("t1_ready"), sem("t2_ready"), sem("w_used"), sem("msgs_ready"), sem("g_used"))
        dist_ready = sem("dist_ready")
        sum2_ready, acc2_step, acc2_zero = sem("sum2_ready"), sem("acc2_step"), sem("acc2_zero")
        fin_mm, fin_out = sem("fin_mm"), sem("fin_out")

        def loop(eng, body):
            body(0, True)
            with eng.Fori(1, ITERS) as i:
                body(i, False)

        def loop_ahead(eng, body):
            body(0, True, False)
            with eng.Fori(1, ITERS - 1) as i:
                body(i, False, False)
            body(ITERS - 1, False, True)

        def node_cols(j):
            return slice(j * CW, (j + 1) * CW)

        dst_flat = a["dst_flat"]
        block = ctx.enter_context(nc.Block())

        @block.sync
        def _(sp):
            sp.dma_start(consts[:], a["consts"]).then_inc(ld["const"], 16)
            sp.dma_start(vecs[:], a["vecs"]).then_inc(ld["const"], 16)
            sp.dma_start(wqkv[:], a["wqkv"]).then_inc(ld["x"], 16)
            sp.dma_start(bqkv[:], a["bqkv"].partition_broadcast(P)).then_inc(ld["x"], 16)
            sp.dma_start(xT[:], a["xT"]).then_inc(ld["x"], 16)
            sp.dma_start(src_col[:], a["src_col"]).then_inc(ld["graph"], 16)
            sp.dma_start(dst_i[:], a["dst_col"]).then_inc(ld["graph"], 16)
            sp.dma_start(base_i[:], a["dst_first"].partition_broadcast(P)).then_inc(ld["graph"], 16)
            for g in range(16):
                sp.dma_start(emb[g * NB:(g + 1) * NB, :], a["r_flat"][g * GE:(g + 1) * GE].partition_broadcast(NB)).then_inc(ld["r"], 16)
            sp.dma_start(weights[:], a["weights"]).then_inc(ld["const"], 16)
            sp.dma_start(yvec[:], a["attr_col"]).then_inc(ld["attr"], 16)
            sp.dma_start(b2f[0:1, 0, :], a["mlp_b2"]).then_inc(ld["const"], 16)
            for t in range(NODE_TILES):
                sp.wait_ge(qkv_sb, t + 1)
                st = work[:, t % 2, 0:3 * D]
                sp.dma_start(q_tab[t * P:(t + 1) * P, :], st[:, 0:D]).then_inc(qkv_out[t % 2], 16)
                sp.dma_start(kv_tab[t * P:(t + 1) * P, :], st[:, D:3 * D]).then_inc(qkv_out[t % 2], 16)
            sp.wait_ge(r_exp, 1)
            for g in range(16):
                sp.dma_start(emb_rows[:, g * GE:(g + 1) * GE], emb[g * NB:(g + 1) * NB, :]).then_inc(emb_out, 16)
            for b in range(2):
                sp.wait_ge(qkv_out[b], 32 * (NODE_TILES // 2))

            sp.wait_ge(yprep, 13)
            for k in range(3):
                sp.dma_start(b2rows[k:k + 1, :], b2p[0:1, k, :]).then_inc(b2_in, 16)

            def loads(i, first):
                for s in range(SLOTS):
                    if not first:
                        sp.wait_ge(qe_ready, SLOTS * i + s - SLOTS + 1)
                    _, base = nc.values_load_multi_w_load_instructions(
                        base_i[0:1, bass.ds(i * BODY + s * QT, QT)], engines=(ET.SP,), min_val=0, max_val=N,
                        skip_runtime_bounds_check_because="destinations are node numbers")
                    sp.dma_start(dstb[:, s, :], dst_flat[bass.ds((i * BODY + s * QT) * P, QC)].partition_broadcast(P)).then_inc(a_in[s], 16)
                    for k in range(QT):
                        sp.dma_start(qwin[:, s, k, :], q_tab[bass.ds(base[k], P), :]).then_inc(a_in[s], 16)
            loop(sp, loads)

            sp.wait_ge(score_ready, SLOTS * ITERS)
            sp.dma_start(mask_dst.rearrange("p (c e) -> p c e", c=TC), dst_flat.rearrange("(c p e) -> p c e", p=P, e=P)).then_inc(ld["mask"], 16)
            sp.dma_start(nbr_i[:], a["neighbours"]).then_inc(ld["mask"], 16)
            sp.dma_start(rowi.rearrange("p k n -> p (k n)"), a["tile_ends"].partition_broadcast(H)).then_inc(ld["mask"], 16)
            sp.wait_ge(c_sb, 1)
            sp.dma_start(carry_in, small[0:2 * H * TC, 0:P]).then_inc(c_dma, 16)
            sp.wait_ge(c_dma, 16)
            sp.dma_start(rowbuf[:, :, 0:TPAD], carry_in.rearrange("(k h c) p -> h k (c p)", k=2, h=H)).then_inc(c_dma, 16)
            sp.wait_ge(c_scan, 2)
            sp.dma_start(carry_out[0:H * TC].rearrange("(h c) p -> h (c p)", h=H), rowout[:, 0, 0:TPAD]).then_inc(c_back, 16)
            sp.dma_start(carry_out[H * TC:].rearrange("(h c) p -> h (c p)", h=H), rowout[:, 1, 1:TPAD + 1]).then_inc(c_back, 16)
            sp.wait_ge(c_back, 32)
            sp.dma_start(small[0:2 * H * TC, 0:P], carry_out).then_inc(c_back, 16)

            sp.wait_ge(back_sb, TC)

            def loads_v(i, first):
                for s in range(SLOTS):
                    if not first:
                        sp.wait_ge(msg_ready, SLOTS * i + s - SLOTS + 1)
                    sp.dma_start(rows[:, s, :, 0:D], v_edges[:, bass.ds((i * BODY + s * QT) * D, QT * D)]
                                 .rearrange("p (t f) -> p t f", t=QT)).then_inc(v_in[s], 16)
            loop(sp, loads_v)

            for t in range(NODE_TILES):
                sp.wait_ge(up_sb, t + 1)
                sp.dma_start(up_tab[t * P:(t + 1) * P, :], work[:, t % 2, 0:D]).then_inc(up_out[t % 2], 16)

            sp.wait_ge(emb_out, 16 * 16)

            def loads_e(i, first):
                for u in range(2):
                    if not first:
                        sp.wait_ge(h1_mm, 2 * i + u - 1)
                    for half in range(2):
                        sp.dma_start(embb[half * NB:(half + 1) * NB, u, :],
                                     emb_rows[:, bass.ds((i * BODY + (2 * u + half) * QT) * P, QC)]).then_inc(e_in[u], 16)
            loop(sp, loads_e)

            for j in range(NCH):
                sp.wait_ge(ln_out, 3 * NCH + j + 1)
                w = min(CW, N - j * CW)
                sp.dma_start(out[:, j * CW:j * CW + w], R[1][:, j * CW:j * CW + w]).then_inc(fin_out, 16)
            sp.wait_ge(fin_out, 16 * NCH)

        def gather_loop(pool, table, width, landed, ready, release):
            limit, zero = pool.alloc_register(f"limit_{width}"), pool.alloc_register(f"zero_{width}")
            pool.reg_mov(limit, N)
            pool.reg_mov(zero, 0)
            def body(i, first):
                for s in range(SLOTS):
                    pool.wait_ge(ready, SLOTS * i + s + 1)
                    if not first:
                        release(i, s)
                    pool.reg_add(limit, limit, zero)
                    for k in range(QT):
                        nc.gpsimd.indirect_dma_start(
                            rows[:, s, k, 0:width], None, table,
                            bass.IndirectOffsetOnAxis(idx[:, s, k:k + 1].bitcast(U32), 0),
                            bounds_check=limit).then_inc(landed[s], 16)
            loop(pool, body)

        @block.gpsimd
        def _(pool):
            for b in range(2):
                pool.wait_ge(qkv_out[b], 32 * (NODE_TILES // 2))

            def release_kv(i, s):
                pool.wait_ge(prod_ready, SLOTS * i + s - SLOTS + 1)
                pool.wait_ge(v_out[s], 16 * i)
            gather_loop(pool, kv_tab, 2 * D, kv_in, idx_ready, release_kv)

            def weighted(i, first):
                for s in range(SLOTS):
                    q = SLOTS * i + s
                    pool.wait_ge(exb_ready, q + 1)
                    pool.wait_ge(v_in[s], 16 * (i + 1))
                    if not first or s >= 2:
                        pool.wait_ge(sum_ready, QT * (q - 1))
                    nc.gpsimd.tensor_tensor(msg0[:, s % 2], rows[:, s, :, 0:D], exb[:, s % 2], ALU.mult).then_inc(msg_ready, 1)
            loop(pool, weighted)

            for b in range(2):
                pool.wait_ge(up_out[b], 16 * (NODE_TILES // 2))

            def release_up(i, s):
                pool.wait_ge(g_used, SLOTS * i + s - SLOTS + 1)
            gather_loop(pool, up_tab, D, g_in, idx2_ready, release_up)

        @block.tensor
        def _(pe):
            pe.wait_ge(ld["x"], 48)
            for t in range(NODE_TILES):
                if t >= 2:
                    pe.wait_ge(qkv_sb, t - 1)
                pe.matmul(ps[:, t % 2, 0:3 * D], xT[:, t * P:(t + 1) * P], wqkv[:], start=True, stop=True).then_inc(qkv_mm, 1)
            pe.wait_ge(qkv_sb, NODE_TILES)

            def queries(i, first):
                for s in range(SLOTS):
                    pe.wait_ge(hotT_ready, SLOTS * i + s + 1)
                    if not first:
                        pe.wait_ge(prod_ready, SLOTS * i + s - SLOTS + 1)
                    for k in range(QT):
                        mm = pe.matmul(ps[:, s, k * P:(k + 1) * P], hot[:, s % 2, k, :], qwin[:, s, k, :], start=True, stop=True)
                    mm.then_inc(qe_ready, 1)
            loop(pe, queries)

            pe.wait_ge(ld["const"], 64)
            pe.wait_ge(score_ready, SLOTS * ITERS)
            if TPAD > NT:
                pe.wait_ge(pad_zero, 1)
            for c in range(TC):
                if c >= 4:
                    pe.wait_ge(tr_sb, c - 3)
                for h in range(H):
                    mm = pe.transpose(ps[:, c % 4, h * P:(h + 1) * P], alpha[:, c * P:(c + 1) * P, h], ident)
                mm.then_inc(tr_mm, 1)
            pe.wait_ge(edge_cols, 2)
            pe.transpose(ps[0:2 * H * TC, 4, 0:P], small[:, P:P + 2 * H * TC], ident).then_inc(c_tr, 1)
            pe.wait_ge(c_back, 48)
            pe.transpose(ps[:, 5, 0:2 * H * TC], small[0:2 * H * TC, 0:P], ident[0:2 * H * TC, 0:2 * H * TC]).then_inc(c_mm, 1)
            pe.wait_ge(exp_ready, H)
            pe.wait_ge(tr_sb, TC)
            for c in range(TC):
                if c >= 4:
                    pe.wait_ge(back_sb, c - 3)
                for h in range(H):
                    mm = pe.transpose(ps[:, c % 4, h * P:(h + 1) * P], sc_t[:, h, c * P:(c + 1) * P], ident)
                mm.then_inc(back_mm, 1)
            pe.wait_ge(back_sb, TC)

            def sums(i, first):
                for s in range(SLOTS):
                    pe.wait_ge(msg_ready, SLOTS * i + s + 1)
                    pe.wait_ge(hot_ready, SLOTS * i + s + 1)
                    if not first or s >= 2:
                        pe.wait_ge(acc_step, QT * (SLOTS * i + s - 1) + 1)
                    for k in range(QT):
                        for m, left in enumerate((msg0, exb)):
                            mm = pe.matmul(ps[:, 2 * (s % 2) + k // 2, (2 * (k % 2) + m) * P:(2 * (k % 2) + m + 1) * P],
                                           left[:, s % 2, k, :], hot[:, s % 2, k, :], start=True, stop=True)
                        mm.then_inc(sum_ready, 1)
            loop(pe, sums)

            def by_chunk(weight, x, wait, done, banks):
                for j in range(NCH):
                    wait(j)
                    pe.matmul(ps[:, banks[j % len(banks)], 0:CW], weight, x[:, node_cols(j)], start=True, stop=True).then_inc(done, 1)

            def skip_wait(j):
                if j == 0:
                    pe.wait_ge(acc_step, QT * SLOTS * ITERS + 1)
                if j >= 2:
                    pe.wait_ge(skip_sb, j - 1)
            by_chunk(wt(W_SKIP), xT, skip_wait, skip_mm, (0, 1))

            def out1_wait(j):
                pe.wait_ge(skip_sb, j + 1)
                if j >= 2:
                    pe.wait_ge(ln_in, j - 1)
            by_chunk(wt(W_OUT), R[0], out1_wait, out1_mm, (2, 3))

            def layer_norm(n):
                for j in range(NCH):
                    g = n * NCH + j
                    pe.wait_ge(ln_in, g + 1)
                    if g >= 2:
                        pe.wait_ge(centred, g - 1)
                    pe.matmul(ps[:, 4 + g % 2, 0:CW], ones_mean[:], R[1][:, node_cols(j)], start=True, stop=True).then_inc(mean_mm, 1)
                for j in range(NCH):
                    g = n * NCH + j
                    pe.wait_ge(squared, g + 1)
                    if g >= 2:
                        pe.wait_ge(std, g - 1)
                    pe.matmul(ps[:, 6 + g % 2, 0:CW], ones_mean[:], R[2][:, node_cols(j)], start=True, stop=True).then_inc(var_mm, 1)
            layer_norm(0)

            for j in range(NCH):
                pe.wait_ge(ln_out, j + 1)
                for m in range(HID // P):
                    n = j * 4 + m
                    if n >= 2:
                        pe.wait_ge(h_sb, n - 1)
                    pe.matmul(ps[:, n % 2, 0:CW], wt(W_1 + m * P), R[1][:, node_cols(j)], start=True, stop=True).then_inc(h_mm, 1)
                pe.wait_ge(h_sb, 4 * (j + 1))
                if j >= 2:
                    pe.wait_ge(ln_in, NCH + j - 1)
                for m in range(HID // P):
                    mm = pe.matmul(ps[:, 2 + j % 2, 0:CW], wt(W_2 + m * P), hbuf[:, ((j % 2) * 4 + m) * CW:((j % 2) * 4 + m + 1) * CW],
                                   start=(m == 0), stop=(m == HID // P - 1))
                mm.then_inc(mlp_mm, 1)
            layer_norm(1)
            layer_norm(2)

            pe.wait_ge(ln_out, 3 * NCH)
            for t in range(NODE_TILES):
                if t >= 2:
                    pe.wait_ge(up_sb, t - 1)
                pe.matmul(ps[:, t % 2, 0:D], xT[:, t * P:(t + 1) * P], wt(W_UP), start=True, stop=True).then_inc(up_mm, 1)
            pe.wait_ge(up_sb, NODE_TILES)

            def hidden1(i, u, n):
                pe.wait_ge(e_in[u], 32 * (i + 1))
                if not (isinstance(n, int) and n == 0):
                    pe.wait_ge(h1_sb, n)
                pe.matmul(ps[:, 0, :], weights[0:2 * NB, W_M0:W_M0 + P], embb[0:2 * NB, u, :], start=True, stop=True).then_inc(h1_mm, 1)

            def hidden2(u, n):
                pe.wait_ge(h1_sb, n + 1)
                if not (isinstance(n, int) and n == 0):
                    pe.wait_ge(h2_sb, n)
                pe.matmul(ps[:, 1, :], wt(W_M1), h1s[:, u, :], start=True, stop=True).then_inc(h2_mm, 1)

            def edge_weights(i, first, s):
                pe.wait_ge(h2_sb, 2 * i + s // 2 + 1)
                if not first or s >= 2:
                    pe.wait_ge(w_used, SLOTS * i + s - 1)
                half, u = s % 2, s // 2
                pe.matmul(ps[:, 2 + s % 2, :], ones3[0:3, :], b2rep[0:3].rearrange("p t f -> p (t f)"),
                          start=True, stop=False, skip_group_check=True)
                for k in range(QT):
                    mm = pe.matmul(ps[:, 2 + s % 2, k * P:(k + 1) * P], h2s[64 * half:64 * half + 64, u, k * P:(k + 1) * P],
                                   weights[64 * half:64 * half + 64, W_M2:W_M2 + P], start=False, stop=True, skip_group_check=True)
                mm.then_inc(w_mm, 1)

            def sum_quad(i, s, first):
                pe.wait_ge(msgs_ready, SLOTS * i + s + 1)
                pe.wait_ge(hot2_ready, SLOTS * i + s + 1)
                if not (first and s < 2):
                    pe.wait_ge(acc2_step, QT * (SLOTS * i + s - 1) + 1)
                for k in range(QT):
                    for m, left in enumerate((MA, MB)):
                        mm = pe.matmul(ps[:, 4 + 2 * (s % 2) + k // 2, (2 * (k % 2) + m) * P:(2 * (k % 2) + m + 1) * P],
                                       left[:, s % 2, k, :], hot[:, s % 2, k, :], start=True, stop=True)
                    mm.then_inc(sum2_ready, 1)

            def edge_units(i, first, last):
                for u in range(2):
                    n = 2 * i + u
                    ahead = not (last and u == 1)
                    if ahead:
                        hidden1(i + u, 1 - u, n + 1)
                    edge_weights(i, first, 2 * u)
                    if not (first and u == 0):
                        sum_quad(i if u else i - 1, (2 * u - 1) % SLOTS, first)
                    if ahead:
                        hidden2(1 - u, n + 1)
                    edge_weights(i, first, 2 * u + 1)
                    sum_quad(i, 2 * u, first)
            pe.wait_ge(prep, 6)
            hidden1(0, 0, 0)
            hidden2(0, 0)
            loop_ahead(pe, edge_units)
            sum_quad(ITERS - 1, SLOTS - 1, False)

            for j in range(NCH):
                if j == 0:
                    pe.wait_ge(acc2_step, QT * SLOTS * ITERS + 1)
                if j >= 2:
                    pe.wait_ge(ln_in, 3 * NCH + j - 1)
                pe.matmul(ps[:, j % 2, 0:CW], wt(W_OA), acc[:, 0, node_cols(j)], start=True, stop=False)
                pe.matmul(ps[:, j % 2, 0:CW], wt(W_OB), acc[:, 1, node_cols(j)], start=False, stop=True).then_inc(fin_mm, 1)
            layer_norm(3)

        @block.scalar
        def _(act):
            act.wait_ge(r_clip, 3)
            act.wait_ge(ld["const"], 64)
            nc.scalar.activation(emb, emb, ACT.Square, bias=consts[:, K_NEGB:K_NEGB + 1], scale=float(NB - 1)).then_inc(r_sq, 1)
            act.wait_ge(r_sq, 1)
            nc.scalar.activation(emb, emb, ACT.Exp, bias=consts[:, K_LN:K_LN + 1], scale=-0.5).then_inc(r_exp, 1)
            act.wait_ge(yprep, 3)
            nc.scalar.activation(rel_tmp, rel_tmp, ACT.Sqrt).then_inc(yprep, 1)

            def indices(i, s, ready):
                nc.scalar.copy(idx[:, s, :], src_col[:, bass.ds(i * BODY + s * QT, QT)]).then_inc(ready, 1)

            act.wait_ge(ld["graph"], 48)
            for s in range(SLOTS):
                indices(0, s, idx_ready)

            def store_values(i, first):
                for s in range(SLOTS):
                    act.wait_ge(kv_in[s], 16 * QT * (i + 1))
                    act.dma_start(v_edges[:, bass.ds((i * BODY + s * QT) * D, QT * D)].rearrange("p (t f) -> p t f", t=QT),
                                  rows[:, s, :, D:2 * D]).then_inc(v_out[s], 16)
                    indices(i + 1, s, idx_ready)
            loop(act, store_values)

            for c in range(TC):
                act.wait_ge(tr_mm, c + 1)
                nc.scalar.copy(sc_t[:, :, c * P:(c + 1) * P], ps[:, c % 4, :].rearrange("p (h e) -> p h e", h=H)).then_inc(tr_sb, 1)
            act.wait_ge(c_tr, 1)
            nc.scalar.copy(small[0:2 * H * TC, 0:P], ps[0:2 * H * TC, 4, 0:P]).then_inc(c_sb, 1)
            for h in range(H):
                act.wait_ge(shifted, h + 1)
                nc.scalar.activation(sc_t[:, h, :], sc_t[:, h, :], ACT.Exp, scale=1.0 / np.sqrt(C).item()).then_inc(exp_ready, 1)
            for c in range(TC):
                act.wait_ge(back_mm, c + 1)
                nc.scalar.copy(alpha[:, c * P:(c + 1) * P, :].rearrange("p t h -> p h t"),
                               ps[:, c % 4, :].rearrange("p (h e) -> p h e", h=H)).then_inc(back_sb, 1)
            act.wait_ge(back_sb, TC)
            for s in range(SLOTS):
                act.wait_ge(v_out[s], 16 * ITERS)

            def spread(i, first):
                for s in range(SLOTS):
                    if not first or s >= 2:
                        act.wait_ge(sum_ready, QT * (SLOTS * i + s - 1))
                    nc.scalar.copy(exb[:, s % 2].rearrange("p t (h c) -> p (t h) c", h=H),
                                   alpha[:, bass.ds(i * BODY + s * QT, QT), :].rearrange("p t h -> p (t h)").unsqueeze(2)
                                   .to_broadcast([P, QT * H, C])).then_inc(exb_ready, 1)
            loop(act, spread)

            def layer_norm(n):
                for j in range(NCH):
                    act.wait_ge(centred, n * NCH + j + 1)
                    nc.scalar.activation(R[2][:, node_cols(j)], R[1][:, node_cols(j)], ACT.Square).then_inc(squared, 1)
                for j in range(NCH):
                    g = n * NCH + j
                    act.wait_ge(var_mm, g + 1)
                    nc.scalar.activation(R[2][:, node_cols(j)], ps[:, 6 + g % 2, 0:CW], ACT.Sqrt,
                                         bias=consts[:, K_EPS:K_EPS + 1]).then_inc(std, 1)
            layer_norm(0)
            for j in range(NCH):
                if j >= 2:
                    act.wait_ge(mlp_mm, j - 1)
                for m in range(HID // P):
                    n = 4 * j + m
                    act.wait_ge(h_mm, n + 1)
                    nc.scalar.activation(hbuf[:, ((j % 2) * 4 + m) * CW:((j % 2) * 4 + m + 1) * CW], ps[:, n % 2, 0:CW], ACT.Relu,
                                         bias=vec(V_B1 + m)).then_inc(h_sb, 1)
            layer_norm(1)
            layer_norm(2)
            for t in range(NODE_TILES):
                act.wait_ge(up_mm, t + 1)
                if t >= 2:
                    act.wait_ge(up_out[t % 2], 16 * (t // 2))
                nc.scalar.mul(work[:, t % 2, 0:D], ps[:, t % 2, 0:D], 1.0 / np.sqrt(32).item()).then_inc(up_sb, 1)

            act.wait_ge(acc2_zero, 2)
            for s in range(SLOTS):
                indices(0, s, idx2_ready)

            def one_hots(i, first, s):
                q = SLOTS * i + s
                if not first or s >= 2:
                    act.wait_ge(sum2_ready, QT * (q - 1))
                for k in range(QT):
                    op = nc.scalar.activation(hot[:, s % 2, k, :], iota, ACT.Square,
                                              bias=nrel[:, bass.ds(i * BODY + s * QT + k, 1)])
                op.then_inc(dist_ready, 1)
                act.wait_ge(dist_ready, q + 1)
                nc.scalar.activation(hot[:, s % 2], hot[:, s % 2], ACT.Relu, bias=1.0, scale=-1.0).then_inc(hot2_ready, 1)

            def silu1(u, n):
                act.wait_ge(h1_mm, n + 1)
                if not (isinstance(n, int) and n < 2):
                    act.wait_ge(h2_mm, n - 1)
                nc.scalar.activation(h1s[:, u, :], ps[:, 0, :], ACT.Silu, bias=vec(V_MB0)).then_inc(h1_sb, 1)

            def silu2(u, n):
                act.wait_ge(h2_mm, n + 1)
                if not (isinstance(n, int) and n < 2):
                    act.wait_ge(w_mm, 2 * n - 2)
                nc.scalar.activation(h2s[:, u, :], ps[:, 1, :], ACT.Silu, bias=vec(V_MB1)).then_inc(h2_sb, 1)

            def edge_units(i, first, last):
                for u in range(2):
                    n = 2 * i + u
                    ahead = not (last and u == 1)
                    for half, silu in enumerate((silu1, silu2)):
                        s = 2 * u + half
                        if ahead:
                            silu(1 - u, n + 1)
                        one_hots(i, first, s)
                        if not last:
                            act.wait_ge(g_in[s], 16 * QT * (i + 1))
                            indices(i + 1, s, idx2_ready)
            silu1(0, 0)
            silu2(0, 0)
            loop_ahead(act, edge_units)
            layer_norm(3)

        @block.vector
        def _(dve):
            v = nc.vector
            yv = yvec[:].rearrange("p (t c) -> p t c", c=3)
            sq3 = acc[:, 1, 0:3 * NT].rearrange("p (t c) -> p t c", c=3)

            dve.wait_ge(ld["x"], 48)
            for t in range(NODE_TILES):
                dve.wait_ge(qkv_mm, t + 1)
                if t >= 2:
                    dve.wait_ge(qkv_out[t % 2], 32 * (t // 2))
                v.tensor_tensor(work[:, t % 2, 0:3 * D], ps[:, t % 2, 0:3 * D], bqkv[:], ALU.add).then_inc(qkv_sb, 1)
            dve.wait_ge(ld["graph"], 48)
            dve.wait_ge(ld["const"], 64)
            v.tensor_tensor(rel[:], dst_i[:], base_i[:], ALU.subtract).then_inc(prep, 1)
            v.tensor_scalar(win[:], base_i[:], consts[:, K_COL:K_COL + 1], None, ALU.add).then_inc(prep, 1)
            v.memset(ones_mean[:], 1.0 / D).then_inc(prep, 1)
            v.memset(ones3[:], 1.0).then_inc(prep, 1)
            dve.wait_ge(ld["r"], 16 * 16)
            v.tensor_scalar(emb_m, emb, 1.0, 1e4, ALU.is_gt, ALU.mult).then_inc(r_clip, 1)
            dve.wait_ge(r_clip, 1)
            v.tensor_scalar(emb, emb, 0.0, 1.0, ALU.max, ALU.min).then_inc(r_clip, 1)
            dve.wait_ge(r_clip, 2)
            v.tensor_tensor(emb, emb, emb_m, ALU.add).then_inc(r_clip, 1)
            dve.wait_ge(ld["attr"], 16)
            v.tensor_tensor(sq3, yv, yv, ALU.mult).then_inc(yprep, 1)
            dve.wait_ge(yprep, 1)
            v.tensor_reduce(rel_tmp, sq3, AX.X, ALU.add).then_inc(yprep, 2)
            dve.wait_ge(yprep, 4)
            v.tensor_scalar(rel_tmp, rel_tmp, 1e-12, None, ALU.add).then_inc(yprep, 1)
            dve.wait_ge(yprep, 5)
            v.reciprocal(rel_tmp, rel_tmp).then_inc(yprep, 1)
            dve.wait_ge(yprep, 6)
            v.scalar_tensor_tensor(out=yv, in0=yv, scalar=np.sqrt(3).item(),
                                   in1=rel_tmp.unsqueeze(2).to_broadcast([P, NT, 3]), op0=ALU.mult, op1=ALU.mult).then_inc(yprep, 1)
            dve.wait_ge(yprep, 7)
            v.tensor_scalar(weights[:, W_M2 + 96:W_M2 + 128], weights[:, W_M2 + 96:W_M2 + 128],
                            1.0 / np.sqrt(3).item(), None, ALU.mult).then_inc(prep, 1)
            v.tensor_scalar(b2f[0:1, 0, 96:128], b2f[0:1, 0, 96:128], 1.0 / np.sqrt(3).item(), None, ALU.mult).then_inc(yprep, 1)
            dve.wait_ge(yprep, 8)
            v.tensor_copy(b2p[0:1, 0, :], b2f[0:1, 0, :]).then_inc(yprep, 1)
            dve.wait_ge(yprep, 9)
            v.tensor_tensor(b2f[0:1, 1, :], b2f[0:1, 0, :], b2p[0:1, 0, :], ALU.subtract).then_inc(yprep, 1)
            dve.wait_ge(yprep, 10)
            v.tensor_copy(b2p[0:1, 1, :], b2f[0:1, 1, :]).then_inc(yprep, 1)
            dve.wait_ge(yprep, 11)
            v.tensor_tensor(b2f[0:1, 2, :], b2f[0:1, 1, :], b2p[0:1, 1, :], ALU.subtract).then_inc(yprep, 1)
            dve.wait_ge(yprep, 12)
            v.tensor_copy(b2p[0:1, 2, :], b2f[0:1, 2, :]).then_inc(yprep, 1)
            if TPAD > NT:
                v.memset(alpha[:, NT:TPAD, :], 0.0).then_inc(pad_zero, 1)
            dve.wait_ge(prep, 5)

            def product(i, s, first):
                q = SLOTS * i + s
                dve.wait_ge(qe_ready, q + 1)
                dve.wait_ge(kv_in[s], 16 * QT * (i + 1))
                if not first:
                    dve.wait_ge(score_ready, q - 1)
                v.tensor_tensor(work[:, s % 2, :].rearrange("p (t f) -> p t f", t=QT),
                                ps[:, s, :].rearrange("p (t f) -> p t f", t=QT), rows[:, s, :, 0:D], ALU.mult).then_inc(prod_ready, 1)
                dve.wait_ge(prod_ready, q + 1)
                v.tensor_reduce(alpha[:, bass.ds(i * BODY + s * QT, QT), :].rearrange("p t h -> p (t h)"),
                                work[:, s % 2, :].rearrange("p (g c) -> p g c", c=C), AX.X, ALU.add).then_inc(score_ready, 1)

            def scores(i, first):
                for s in range(SLOTS):
                    q = SLOTS * i + s
                    dve.wait_ge(a_in[s], 16 * (1 + QT) * (i + 1))
                    if not first or s >= 2:
                        dve.wait_ge(qe_ready, q - 1)
                    v.tensor_tensor(hot[:, s % 2], dstb[:, s, :].rearrange("p (t e) -> p t e", t=QT),
                                    win[:, bass.ds(i * BODY + s * QT, QT)].unsqueeze(2).to_broadcast([P, QT, P]),
                                    ALU.is_equal).then_inc(hotT_ready, 1)
                    if not (first and s == 0):
                        product(i if s else i - 1, (s - 1) % SLOTS, first and s < 3)
            loop(dve, scores)
            product(ITERS - 1, SLOTS - 1, False)

            dt = masks[:, 2, :].rearrange("p (c e) -> p c e", c=TC)
            mf = masks[:, 0, :].rearrange("p (c e) -> p c e", c=TC)
            m1 = masks[:, 1, :].rearrange("p (c e) -> p c e", c=TC)
            dve.wait_ge(ld["mask"], 16 * 3)
            v.tensor_copy(dt, mask_dst.rearrange("p (c e) -> p c e", c=TC)).then_inc(mask_ready, 1)
            v.tensor_copy(nbr[:], nbr_i[:].rearrange("p (k c) -> p k c", k=2)).then_inc(mask_ready, 1)
            dve.wait_ge(mask_ready, 2)
            v.tensor_tensor(mf[:, :, 1:P], dt[:, :, 1:P], dt[:, :, 0:P - 1], ALU.is_equal).then_inc(mask_ready, 1)
            v.memset(mf[:, :, 0:1], 0.0).then_inc(mask_ready, 1)
            v.tensor_tensor(m1, dt, nbr[:, 0, :].unsqueeze(2).to_broadcast([P, TC, P]), ALU.is_equal).then_inc(mask_ready, 1)
            dve.wait_ge(mask_ready, 5)
            v.tensor_tensor(dt, dt, nbr[:, 1, :].unsqueeze(2).to_broadcast([P, TC, P]), ALU.is_equal).then_inc(mask_ready, 1)
            dve.wait_ge(mask_ready, 6)
            v.tensor_scalar(masks, masks, 0.5, 2 * BIG, ALU.subtract, ALU.mult).then_inc(mask_ready, 1)
            dve.wait_ge(mask_ready, 7)
            dve.wait_ge(tr_sb, TC)
            for h in range(H):
                v.tensor_tensor_scan(fw_t[:, h, :], masks[:, 0, :], sc_t[:, h, :], -BIG, ALU.min, ALU.max).then_inc(scan_f, 1)
            v.memset(mback[:, TPAD - 1:TPAD], -BIG).then_inc(mask_ready, 1)
            v.tensor_copy(mback[:, 0:TPAD - 1], masks[:, 0, 1:TPAD]).then_inc(mask_ready, 1)
            dve.wait_ge(mask_ready, 9)
            for h in range(H):
                dve.wait_ge(scan_f, h + 1)
                v.tensor_tensor_scan(tot_t[:, h, ::-1], mback[:, ::-1], fw_t[:, h, ::-1], -BIG, ALU.min, ALU.max).then_inc(scan_b, 1)
            K = H * TC
            v.tensor_copy(small[:, P:P + K].rearrange("p (h c) -> p h c", h=H),
                          fw_t.rearrange("p h (c e) -> p h c e", c=TC)[:, :, :, P - 1]).then_inc(edge_cols, 1)
            dve.wait_ge(scan_b, H)
            v.tensor_copy(small[:, P + K:P + 2 * K].rearrange("p (h c) -> p h c", h=H),
                          tot_t.rearrange("p h (c e) -> p h c e", c=TC)[:, :, :, 0]).then_inc(edge_cols, 1)
            for s in range(SLOTS):
                dve.wait_ge(v_out[s], 16 * ITERS)
            for k in range(2):
                v.tensor_tensor(rowmask[:, k, :], rowi[:, 2 * k, :], rowi[:, 2 * k + 1, :], ALU.is_equal).then_inc(mask_ready, 1)
            dve.wait_ge(mask_ready, 11)
            v.tensor_scalar(rowmask, rowmask, 0.5, 2 * BIG, ALU.subtract, ALU.mult).then_inc(mask_ready, 1)
            v.memset(rowout[:, 0, 0:1], -BIG).then_inc(mask_ready, 1)
            v.memset(rowout[:, 1, TPAD:TPAD + 1], -BIG).then_inc(mask_ready, 1)
            dve.wait_ge(mask_ready, 14)
            dve.wait_ge(c_dma, 32)
            v.tensor_tensor_scan(rowout[:, 0, 1:TPAD + 1], rowmask[:, 0, :], rowbuf[:, 0, :], -BIG, ALU.min, ALU.max).then_inc(c_scan, 1)
            v.tensor_tensor_scan(rowout[:, 1, 0:TPAD][:, ::-1], rowmask[:, 1, ::-1], rowbuf[:, 1, ::-1], -BIG, ALU.min, ALU.max).then_inc(c_scan, 1)
            dve.wait_ge(c_mm, 1)
            v.tensor_copy(small[:, P:P + 2 * K], ps[:, 5, 0:2 * K]).then_inc(c_use, 1)
            dve.wait_ge(c_use, 1)
            n = 0
            for k in range(2):
                for h in range(H):
                    v.tensor_tensor(fw_t[:, h, :].rearrange("p (c e) -> p c e", c=TC),
                                    masks[:, 1 + k, :].rearrange("p (c e) -> p c e", c=TC),
                                    small[:, P + k * K + h * TC:P + k * K + (h + 1) * TC].unsqueeze(2).to_broadcast([P, TC, P]),
                                    ALU.min).then_inc(mx, 1)
                for h in range(H):
                    dve.wait_ge(mx, n + H)
                    v.tensor_tensor(tot_t[:, h, :], tot_t[:, h, :], fw_t[:, h, :], ALU.max).then_inc(mx, 1)
                    n += 1
                n += H
                dve.wait_ge(mx, n)
            for h in range(H):
                v.tensor_tensor(sc_t[:, h, :], sc_t[:, h, :], tot_t[:, h, :], ALU.subtract).then_inc(shifted, 1)
            dve.wait_ge(back_sb, TC)

            def bases(i, s):
                _, base = nc.values_load_multi_w_load_instructions(
                    base_i[0:1, bass.ds(i * BODY + s * QT, QT)], engines=(ET.DVE,), min_val=0, max_val=N,
                    skip_runtime_bounds_check_because="destinations are node numbers")
                return base

            def add_tile(i, s, k, base, bank0, ready, step):
                t = QT * (SLOTS * i + s) + k
                if k % 2 == 0:
                    dve.wait_ge(ready, t + 2)
                dve.wait_ge(step, t + 1)
                to = acc[:, :, bass.ds(base[k], P)]
                v.tensor_tensor(to, to, ps[:, bank0 + 2 * (s % 2) + k // 2, (k % 2) * 256:(k % 2) * 256 + 256]
                                .rearrange("p (m f) -> p m f", m=2), ALU.add).then_inc(step, 1)

            v.memset(acc[:], 0.0).then_inc(acc_zero, 1)
            v.memset(flag[:], 0.0).then_inc(acc_step, 1)
            dve.wait_ge(acc_zero, 1)
            dve.wait_ge(acc_step, 1)

            def sum_edges(i, first):
                for s in range(SLOTS):
                    q = SLOTS * i + s
                    before = None if first and s == 0 else (i if s else i - 1, (s - 1) % SLOTS)
                    if before:
                        base = bases(*before)
                    if not first or s >= 2:
                        dve.wait_ge(sum_ready, QT * (q - 1))
                    for k in range(QT):
                        op = v.tensor_scalar(hot[:, s % 2, k, :], iota, rel[:, bass.ds(i * BODY + s * QT + k, 1)], None, ALU.is_equal)
                        if k == QT - 1:
                            op.then_inc(hot_ready, 1)
                        if before:
                            add_tile(*before, k, base, 0, sum_ready, acc_step)
            loop(dve, sum_edges)
            base = bases(ITERS - 1, SLOTS - 1)
            for k in range(QT):
                add_tile(ITERS - 1, SLOTS - 1, k, base, 0, sum_ready, acc_step)

            dve.wait_ge(acc_step, QT * SLOTS * ITERS + 1)
            for j in range(NCH):
                cs = node_cols(j)
                v.tensor_scalar(R[3][:, cs], acc[:, 1, cs], 1e-30, None, ALU.max).then_inc(conv_a, 1)
            for j in range(NCH):
                cs = node_cols(j)
                dve.wait_ge(conv_a, j + 1)
                v.reciprocal(R[2][:, cs], R[3][:, cs]).then_inc(conv_b, 1)
                dve.wait_ge(conv_b, j + 1)
                v.tensor_tensor(R[0][:, cs], acc[:, 0, cs], R[2][:, cs], ALU.mult).then_inc(conv, 1)
            for j in range(NCH):
                cs = node_cols(j)
                dve.wait_ge(conv, j + 1)
                dve.wait_ge(skip_mm, j + 1)
                v.scalar_tensor_tensor(out=R[0][:, cs], in0=ps[:, j % 2, 0:CW], scalar=vec(V_BSKIP), in1=R[0][:, cs],
                                       op0=ALU.add, op1=ALU.add).then_inc(skip_sb, 1)
            for j in range(NCH):
                cs = node_cols(j)
                dve.wait_ge(out1_mm, j + 1)
                v.scalar_tensor_tensor(out=R[1][:, cs], in0=ps[:, 2 + j % 2, 0:CW], scalar=vec(V_BOUT), in1=xT[:, cs],
                                       op0=ALU.add, op1=ALU.add).then_inc(ln_in, 1)

            def layer_norm(n, affine=None):
                for j in range(NCH):
                    g, cs = n * NCH + j, node_cols(j)
                    dve.wait_ge(mean_mm, g + 1)
                    v.tensor_tensor(R[1][:, cs], R[1][:, cs], ps[:, 4 + g % 2, 0:CW], ALU.subtract).then_inc(centred, 1)
                for j in range(NCH):
                    g, cs = n * NCH + j, node_cols(j)
                    dve.wait_ge(std, g + 1)
                    v.reciprocal(R[2][:, cs], R[2][:, cs]).then_inc(inv, 1)
                    dve.wait_ge(inv, g + 1)
                    op = v.tensor_tensor(R[1][:, cs], R[1][:, cs], R[2][:, cs], ALU.mult)
                    if affine is None:
                        op.then_inc(ln_out, 1)
                    else:
                        op.then_inc(scaled, 1)
                        dve.wait_ge(scaled, g + 1)
                        v.tensor_scalar(R[1][:, cs], R[1][:, cs], vec(affine), vec(affine + 1), ALU.mult, ALU.add).then_inc(ln_out, 1)
            layer_norm(0, V_L1W)
            for j in range(NCH):
                cs = node_cols(j)
                dve.wait_ge(mlp_mm, j + 1)
                v.scalar_tensor_tensor(out=R[1][:, cs], in0=ps[:, 2 + j % 2, 0:CW], scalar=vec(V_B2), in1=R[1][:, cs],
                                       op0=ALU.add, op1=ALU.add).then_inc(ln_in, 1)
            layer_norm(1, V_L2W)
            for j in range(NCH):
                cs = node_cols(j)
                dve.wait_ge(ln_out, NCH + j + 1)
                v.tensor_tensor(R[1][:, cs], R[1][:, cs], xT[:, cs], ALU.add).then_inc(ln_in, 1)
            v.memset(acc[:], 0.0).then_inc(acc2_zero, 1)
            for j in range(NCH):
                g, cs = 2 * NCH + j, node_cols(j)
                dve.wait_ge(mean_mm, g + 1)
                v.tensor_tensor(R[1][:, cs], R[1][:, cs], ps[:, 4 + g % 2, 0:CW], ALU.subtract).then_inc(centred, 1)
            for j in range(NCH):
                g, cs = 2 * NCH + j, node_cols(j)
                dve.wait_ge(std, g + 1)
                v.reciprocal(R[2][:, cs], R[2][:, cs]).then_inc(inv, 1)
                dve.wait_ge(inv, g + 1)
                v.tensor_tensor(xT[:, cs], R[1][:, cs], R[2][:, cs], ALU.mult).then_inc(ln_out, 1)

            v.tensor_scalar(nrel, rel[:], -1.0, None, ALU.mult).then_inc(acc2_zero, 1)
            dve.wait_ge(b2_in, 48)
            v.tensor_copy(b2rep[0:3], b2rows[0:3].unsqueeze(1).to_broadcast([3, QT, D])).then_inc(prep, 1)
            v.memset(flag[:, 1:2], 0.0).then_inc(acc2_step, 1)
            dve.wait_ge(acc2_zero, 2)
            dve.wait_ge(acc2_step, 1)
            dve.wait_ge(ln_out, 3 * NCH)

            def messages(i, first):
                for s in range(SLOTS):
                    q = SLOTS * i + s
                    b = s % 2
                    before = None if first and s == 0 else (i if s else i - 1, (s - 1) % SLOTS)
                    if before:
                        base = bases(*before)

                    def add(k):
                        if before:
                            add_tile(*before, k, base, 4, sum2_ready, acc2_step)
                    g = rows[:, s, :, 0:D]
                    w = ps[:, 2 + b, :].rearrange("p (t f) -> p t f", t=QT)
                    ss = g[:, :, 0:32]
                    vv = g[:, :, 32:128].rearrange("p t (c m) -> p t c m", c=3)
                    y = yvec[:, bass.ds((i * BODY + s * QT) * 3, 3 * QT)].rearrange("p (t c) -> p t c", c=3) \
                        .unsqueeze(3).to_broadcast([P, QT, 3, 32])
                    vyb = vy[:, b].rearrange("p t (c m) -> p t c m", c=3)
                    dve.wait_ge(g_in[s], 16 * QT * (i + 1))
                    v.tensor_tensor(vyb, vv, y, ALU.mult).then_inc(vy_ready, 1)
                    dve.wait_ge(w_mm, q + 1)
                    v.tensor_tensor(ub[:, b], w[:, :, 32:64], ss, ALU.mult).then_inc(u_ready, 1)
                    dve.wait_ge(vy_ready, q + 1)
                    v.tensor_tensor(tb[:, 2 * b], vyb[:, :, 0], vyb[:, :, 1], ALU.add).then_inc(t1_ready, 1)
                    add(0)
                    if not first or s >= 2:
                        dve.wait_ge(sum2_ready, QT * (q - 1))
                    v.tensor_tensor(MA[:, b, :, 0:32], w[:, :, 0:32], ss, ALU.mult)
                    dve.wait_ge(t1_ready, q + 1)
                    v.tensor_tensor(tb[:, 2 * b + 1], tb[:, 2 * b], vyb[:, :, 2], ALU.add).then_inc(t2_ready, 1)
                    add(1)
                    v.tensor_tensor(MB[:, b, :, 32:128].rearrange("p t (c m) -> p t c m", c=3),
                                    w[:, :, 64:96].unsqueeze(2).to_broadcast([P, QT, 3, 32]), vv, ALU.mult).then_inc(g_used, 1)
                    add(2)
                    dve.wait_ge(t2_ready, q + 1)
                    v.tensor_tensor(MB[:, b, :, 0:32], w[:, :, 96:128], tb[:, 2 * b + 1], ALU.mult).then_inc(w_used, 1)
                    dve.wait_ge(u_ready, q + 1)
                    v.tensor_tensor(MA[:, b, :, 32:128].rearrange("p t (c m) -> p t c m", c=3),
                                    ub[:, b].unsqueeze(2).to_broadcast([P, QT, 3, 32]), y, ALU.mult).then_inc(msgs_ready, 1)
                    add(3)
            loop(dve, messages)
            base = bases(ITERS - 1, SLOTS - 1)
            for k in range(QT):
                add_tile(ITERS - 1, SLOTS - 1, k, base, 4, sum2_ready, acc2_step)

            for j in range(NCH):
                cs = node_cols(j)
                dve.wait_ge(fin_mm, j + 1)
                v.scalar_tensor_tensor(out=R[1][:, cs], in0=ps[:, j % 2, 0:CW], scalar=1.0 / (8.0 * 16.0), in1=xT[:, cs],
                                       op0=ALU.mult, op1=ALU.add).then_inc(ln_in, 1)
            layer_norm(3)


_SHAPES = {
    "consts": (P, K_N), "vecs": (P, V_N), "weights": (P, W_N), "wqkv": (P, 3 * D), "bqkv": (3 * D,), "xT": (P, NW),
    "src_col": (P, NT + BODY), "dst_col": (P, NT), "dst_first": (NT,), "dst_flat": (TPAD * P,), "neighbours": (P, 2 * TC),
    "tile_ends": (4 * TPAD,), "r_flat": (NT * P,), "attr_col": (P, 3 * NT), "mlp_b2": (1, D),
}


def layout(x):
    f = {k: np.asarray(v) for k, v in x.items()}

    def l0(n):
        return f["L0_gnn_" + n]

    def l1(n):
        return f["L1_gnn_" + n]

    a = {}
    c = np.zeros((P, K_N), np.float32)
    c[:, K_ID:K_ID + P] = np.eye(P)
    c[:, K_IOTA:K_IOTA + P] = np.arange(P)[None]
    c[:, K_COL] = np.arange(P)
    c[:, K_NEGB] = -(np.arange(P) % NB)
    c[:, K_LN] = 0.5 * np.log(NB)
    c[:, K_EPS] = EPS
    a["consts"] = c
    v = np.zeros((P, V_N), np.float32)
    for j, n in ((V_BSKIP, "bskip"), (V_BOUT, "bout"), (V_L1W, "ln1_w"), (V_L1B, "ln1_b"), (V_L2W, "ln2_w"), (V_L2B, "ln2_b"), (V_B2, "b2")):
        v[:, j] = l0(n)
    v[:, V_B1:V_B1 + 4] = l0("b1").reshape(4, P).T
    for h in range(2):
        v[64 * h:64 * h + 64, V_MB0] = l1("mlp_b0")
        v[64 * h:64 * h + 64, V_MB1] = l1("mlp_b1")
    a["vecs"] = v
    w = np.zeros((P, W_N), np.float32)
    w[:, W_SKIP:W_SKIP + D] = l0("Wskip").T
    w[:, W_OUT:W_OUT + D] = l0("Wout").T
    w[:, W_1:W_1 + HID] = l0("W1").T
    w[:, W_2:W_2 + HID] = l0("W2").T.reshape(4, P, D).transpose(1, 0, 2).reshape(P, HID)
    w[0:32, W_UP:W_UP + 32] = l1("W_up0")
    w[0:32, W_OA:W_OA + 32] = l1("W_out0")[0:32]
    w[0:32, W_OB:W_OB + 32] = l1("W_out0")[32:64]
    for q in range(3):
        w[32 + q:D:3, W_UP + 32 + 32 * q:W_UP + 64 + 32 * q] = l1("W_up1")
        w[32 + 32 * q:64 + 32 * q, W_OA + 32 + q:W_OA + D:3] = l1("W_out1")[0:32]
        w[32 + 32 * q:64 + 32 * q, W_OB + 32 + q:W_OB + D:3] = l1("W_out1")[32:64]
    for h in range(2):
        w[64 * h:64 * h + 64, W_M1 + 64 * h:W_M1 + 64 * h + 64] = l1("mlp_w1")
        w[64 * h:64 * h + 64, W_M2:W_M2 + D] = l1("mlp_w2")
        w[NB * h:NB * h + NB, W_M0 + 64 * h:W_M0 + 64 * h + 64] = l1("mlp_w0")
    a["weights"] = w
    a["wqkv"] = np.concatenate([l0("Wq").T, l0("Wk").T, l0("Wv").T], 1)
    a["bqkv"] = np.concatenate([l0("bq"), l0("bk"), l0("bv")])
    a["xT"] = np.zeros((P, NW), np.float32)
    a["xT"][:, :N] = f["x"].T
    src = np.zeros((NT + BODY) * P, np.int32)
    src[:E] = f["src"]
    dst = np.full(TPAD * P, N, np.int32)
    dst[:E] = f["dst"]
    a["src_col"] = src.reshape(-1, P).T
    tiles = dst.reshape(TPAD, P)
    a["dst_col"] = tiles[:NT].T
    a["dst_first"] = tiles[:NT, 0]
    a["dst_flat"] = dst
    first, last = tiles[:, 0], tiles[:, -1]
    before = np.concatenate([[-1], last[:-1]]).astype(np.int32)
    after = np.concatenate([first[1:], [-1]]).astype(np.int32)
    a["neighbours"] = np.concatenate([before.reshape(TC, P).T, after.reshape(TC, P).T], 1)
    a["tile_ends"] = np.concatenate([last, before, first, after])
    r = np.zeros(NT * P, np.float32)
    r[:E] = f["edge_weight"]
    a["r_flat"] = r
    e = np.zeros((NT * P, 3), np.float32)
    e[:E] = f["edge_attr_3"]
    a["attr_col"] = e.reshape(NT, P, 3).transpose(1, 0, 2).reshape(P, 3 * NT)
    a["mlp_b2"] = l1("mlp_b2").reshape(1, D)
    return {k: np.ascontiguousarray(t) for k, t in a.items()}


def kernel(**inputs):
    import concourse.bacc as bacc
    from concourse.bass_utils import run_bass_kernel_spmd as run

    nc = bacc.Bacc("TRN2", target_bir_lowering=False, num_devices=1)
    arrays = layout(inputs)
    aps = {}
    for k, shape in _SHAPES.items():
        assert arrays[k].shape == shape, (k, arrays[k].shape, shape)
        aps[k] = nc.dram_tensor("in_" + k, shape, mybir.dt.from_np(arrays[k].dtype), kind="ExternalInput").ap()
    out = nc.dram_tensor("out_t", (D, N), F32, kind="ExternalOutput").ap()
    build(nc, aps, out)
    r = run(nc, [{"in_" + k: t for k, t in arrays.items()}], core_ids=[0])
    return np.ascontiguousarray(r.results[0]["out_t"].T)
```

```python
from contextlib import ExitStack

import concourse.bass as bass
from concourse import mybir
import numpy as np

P = 128
F32 = mybir.dt.float32
BF16 = mybir.dt.bfloat16
I32 = mybir.dt.int32
U32 = mybir.dt.uint32
ALU = mybir.AluOpType
ACT = mybir.ActivationFunctionType
AX = mybir.AxisListType
ET = mybir.EngineType

N, E, D, H, C, HID = 3125, 103125, 128, 4, 32, 512
EPS = 1e-5
NB = 8
QT = 4
SLOTS = 4
BODY = QT * SLOTS
ITERS = -(-E // (P * BODY))
NT = ITERS * BODY
TC = -(-NT // P)
TPAD = TC * P
NODE_TILES = -(-(N + P) // P)
NW = NODE_TILES * P
NCH = 7
CW = -(-N // (NCH * 2)) * 2
GE = NT * P // 16
BIG = 1e38
QC = QT * P
assert NCH * CW <= NW and CW <= 512 and NT * P >= E and TPAD >= NT

K_ID, K_IOTA, K_COL, K_NEGB, K_LN, K_EPS = 0, 128, 256, 257, 258, 259
K_N = 260
V_BSKIP, V_BOUT, V_L1W, V_L1B, V_L2W, V_L2B, V_B2, V_B1, V_MB0, V_MB1 = 0, 1, 2, 3, 4, 5, 6, 7, 11, 12
V_N = 13
W_SKIP, W_OUT, W_1, W_2, W_UP, W_M1, W_M2, W_OA, W_OB, W_M0 = 0, 128, 256, 768, 1280, 1408, 1536, 1664, 1792, 1920
W_N = 2048


def build(nc, a, out):
    with ExitStack() as ctx:
        def sb(name, shape, dt=F32):
            return ctx.enter_context(nc.sbuf_tensor(name, shape, dt))

        def sem(name):
            return ctx.enter_context(nc.semaphore(name))

        def slot_sems(name, n=SLOTS):
            return [sem(f"{name}{i}") for i in range(n)]

        def dram(name, shape, dt=F32):
            return nc.dram_tensor(name, shape, dt, kind="Internal").ap()

        q_tab = dram("q_tab", [NW, D])
        kv_tab = dram("kv_tab", [NW, 2 * D])
        up_tab = dram("up_tab", [NW, D])
        v_edges = dram("v_edges", [P, NT * D])
        emb_rows = dram("emb_rows", [NB, NT * P])
        carry_in = dram("carry_in", [2 * H * TC, P])
        carry_out = dram("carry_out", [2 * H * TC, P])

        consts = sb("consts", [P, K_N])
        vecs = sb("vecs", [P, V_N])
        weights = sb("weights", [P, W_N])
        wqkv = sb("wqkv", [P, 3 * D])
        bqkv = sb("bqkv", [P, 3 * D])
        xT = sb("xT", [P, NW])
        src_col = sb("src_col", [P, NT + BODY], I32)
        dst_i = sb("dst_i", [P, NT], I32)
        base_i = sb("base_i", [P, NT], I32)
        rel = sb("rel", [P, NT])
        win = sb("win", [P, NT])
        yvec = sb("yvec", [P, NT * 3])
        alpha = sb("alpha", [P, TPAD, H])
        acc = sb("acc", [P, 2, NW])
        idx = sb("idx", [P, SLOTS, QT], I32)
        nbr_i = sb("nbr_i", [P, 2 * TC], I32)
        nbr = sb("nbr", [P, 2, TC])
        flag = sb("flag", [P, 2])
        b2p = sb("b2p", [P, 3, D], BF16)
        b2rows = sb("b2rows", [P, D], BF16)
        rows = sb("rows", [P, SLOTS, QT, 2 * D])
        qwin = sb("qwin", [P, SLOTS, QT, D])
        dstb = sb("dstb", [P, SLOTS, QC], I32)
        hot = sb("hot", [P, 2, QT, P])
        work = sb("work", [P, 2, QC])
        arena = sb("arena", [P, 4 * NW])
        small = sb("small", [P, P + 2 * H * TC])
        ones_mean = sb("ones_mean", [P, P])
        b2f = sb("b2f", [P, 3, D])
        b2rep = sb("b2rep", [P, QT, D], BF16)
        ones3 = sb("ones3", [P, P], BF16)
        ps = ctx.enter_context(nc.psum_tensor("ps", [P, 8, 512], F32))

        ident = consts[:, K_ID:K_ID + P]
        iota = consts[:, K_IOTA:K_IOTA + P]

        def vec(j, n=1):
            return vecs[:, j:j + n]

        def wt(off, n=P):
            return weights[:, off:off + n]

        emb = arena[:, 0:GE]
        emb_m = arena[:, GE:2 * GE]
        sc_t = arena[:, 0:H * TPAD].rearrange("p (h n) -> p h n", h=H)
        fw_t = arena[:, H * TPAD:2 * H * TPAD].rearrange("p (h n) -> p h n", h=H)
        tot_t = arena[:, 2 * H * TPAD:3 * H * TPAD].rearrange("p (h n) -> p h n", h=H)
        mask_dst = arena[:, 3 * H * TPAD:3 * H * TPAD + TPAD].bitcast(I32)
        mback = arena[:, 3 * H * TPAD + TPAD:3 * H * TPAD + 2 * TPAD]
        accf = acc[:].rearrange("p m n -> p (m n)")
        masks = accf[:, 0:3 * TPAD].rearrange("p (k n) -> p k n", k=3)
        rowi = accf[0:H, 3 * TPAD:7 * TPAD].bitcast(I32).rearrange("p (k n) -> p k n", k=4)
        ysq = [dstb[:].rearrange("p a b -> p (a b)")[:, j * NT:(j + 1) * NT].bitcast(F32) for j in range(2)]
        nrel = win[:]
        rowbuf = qwin[:].rearrange("p a b c -> p (a b c)")[0:H, 0:2 * TPAD].rearrange("p (k n) -> p k n", k=2)
        rowsf = rows[:].rearrange("p a b c -> p (a b c)")
        rowout = rowsf[0:H, 0:2 * (TPAD + 1)].rearrange("p (k n) -> p k n", k=2)
        rowmask = rowsf[0:H, 2 * (TPAD + 1):4 * TPAD + 2].rearrange("p (k n) -> p k n", k=2)
        exb, msg0, hot_b = [arena[:, j * SLOTS * QC:(j + 1) * SLOTS * QC].rearrange("p (s t f) -> p s t f", s=SLOTS, t=QT)
                            for j in range(3)]
        R = [arena[:, j * NW:(j + 1) * NW] for j in range(4)]
        hbuf = rows[:].rearrange("p a b c -> p (a b c)")
        MA = arena[:, 0:2 * QC].rearrange("p (b t f) -> p b t f", b=2, t=QT)
        MB = arena[:, 2 * QC:4 * QC].rearrange("p (b t f) -> p b t f", b=2, t=QT)
        h1s = arena[:, 4 * QC:6 * QC].rearrange("p (b n) -> p b n", b=2)
        h2s = arena[:, 6 * QC:8 * QC].rearrange("p (b n) -> p b n", b=2)
        embb = arena[:, 8 * QC:10 * QC].rearrange("p (b n) -> p b n", b=2)
        vy = arena[:, 10 * QC:10 * QC + 2 * 384].rearrange("p (b t f) -> p b t f", b=2, t=QT)
        ub = arena[:, 12 * QC:12 * QC + 256].rearrange("p (b t f) -> p b t f", b=2, t=QT)
        tb = arena[:, 13 * QC:13 * QC + 512].rearrange("p (b t f) -> p b t f", b=4, t=QT)

        ld = {k: sem("ld_" + k) for k in ("const", "graph", "attr", "x", "mask", "r", "src", "weights")}
        ld_x = slot_sems("ld_x", 2)
        idx_ready, base_ready = sem("idx_ready"), sem("base_ready")
        prep, yprep, bprep = sem("prep"), sem("yprep"), sem("bprep")
        qkv_mm, qkv_sb, qkv_out = sem("qkv_mm"), sem("qkv_sb"), slot_sems("qkv_out", 8)
        r_clip, r_sq, r_exp, emb_out = sem("r_clip"), sem("r_sq"), sem("r_exp"), sem("emb_out")
        kv_in, a_in, v_out = slot_sems("kv_in"), slot_sems("a_in"), slot_sems("v_out")
        hotT_ready, qe_ready, prod_ready, score_ready = sem("hotT_ready"), sem("qe_ready"), sem("prod_ready"), sem("score_ready")
        tr_mm, tr_sb, scan_f, scan_b = sem("tr_mm"), sem("tr_sb"), sem("scan_f"), sem("scan_b")
        edge_cols, c_tr, c_sb, c_dma, c_scan, c_back, c_mm, c_use = (
            sem("edge_cols"), sem("c_tr"), sem("c_sb"), sem("c_dma"), sem("c_scan"), sem("c_back"), sem("c_mm"), sem("c_use"))
        mask_ready, mx, shifted, exp_ready, back_mm, back_sb = (
            sem("mask_ready"), sem("mx"), sem("shifted"), sem("exp_ready"), sem("back_mm"), sem("back_sb"))
        v_in, exb_ready, hot_ready, msg_ready, sum_ready, acc_step = (
            slot_sems("v_in"), sem("exb_ready"), sem("hot_ready"), sem("msg_ready"), sem("sum_ready"), sem("acc_step"))
        acc_zero, pad_zero, b2_in = sem("acc_zero"), sem("pad_zero"), sem("b2_in")
        conv_a, conv_b, conv, skip_mm, skip_sb, out1_mm = sem("conv_a"), sem("conv_b"), sem("conv"), sem("skip_mm"), sem("skip_sb"), sem("out1_mm")
        ln_in, mean_mm, centred, squared, var_mm, std, inv, scaled, ln_out = (
            sem("ln_in"), sem("mean_mm"), sem("centred"), sem("squared"), sem("var_mm"), sem("std"), sem("inv"), sem("scaled"), sem("ln_out"))
        h_mm, h_sb, mlp_mm = sem("h_mm"), sem("h_sb"), sem("mlp_mm")
        up_mm, up_sb, up_out = sem("up_mm"), sem("up_sb"), slot_sems("up_out", 2)
        idx2_ready, g_in, e_in = sem("idx2_ready"), slot_sems("g_in"), slot_sems("e_in", 2)
        h1_mm, h1_sb, h2_mm, h2_sb, w_mm = sem("h1_mm"), sem("h1_sb"), sem("h2_mm"), sem("h2_sb"), sem("w_mm")
        hot2_ready, u_ready, vy_ready, t1_ready, t2_ready, w_used, msgs_ready, g_used = (
            sem("hot2_ready"), sem("u_ready"), sem("vy_ready"), sem("t1_ready"), sem("t2_ready"), sem("w_used"), sem("msgs_ready"), sem("g_used"))
        last_hot_ready = sem("last_hot_ready")
        square_ready, square2_ready, rel_ready, acc_step_z = sem("square_ready"), sem("square2_ready"), sem("rel_ready"), sem("acc_step_z")
        sum2_ready, acc2_step, acc2_zero = sem("sum2_ready"), sem("acc2_step"), sem("acc2_zero")
        fin_mm, fin_out = sem("fin_mm"), sem("fin_out")

        def loop(eng, body):
            body(0, True)
            with eng.Fori(1, ITERS) as i:
                body(i, False)

        def loop_ahead(eng, body):
            body(0, True, False)
            with eng.Fori(1, ITERS - 1) as i:
                body(i, False, False)
            body(ITERS - 1, False, True)

        STAGES = 8

        def stage(t):
            return rowsf[:, (t % STAGES) * 3 * D:(t % STAGES + 1) * 3 * D]

        def stages_of(b):
            return len(range(b, NODE_TILES, STAGES))

        def node_cols(j):
            return slice(j * CW, (j + 1) * CW)

        dst_flat = a["dst_flat"]
        block = ctx.enter_context(nc.Block())

        @block.sync
        def _(sp):
            sp.dma_start(wqkv[:], a["wqkv"]).then_inc(ld["x"], 16)
            sp.dma_start(bqkv[:], a["bqkv"].partition_broadcast(P)).then_inc(ld["x"], 16)
            for j in range(2):
                cs = slice(j * NW // 2, (j + 1) * NW // 2)
                sp.dma_start(xT[:, cs], a["xT"][:, cs]).then_inc(ld_x[j], 16)
            sp.dma_start(dst_i[:], a["dst_col"]).then_inc(ld["graph"], 16)
            sp.dma_start(base_i[:], a["dst_first"].partition_broadcast(P)).then_inc(ld["graph"], 16)
            sp.dma_start(consts[:], a["consts"]).then_inc(ld["const"], 16)
            sp.dma_start(vecs[:], a["vecs"]).then_inc(ld["const"], 16)
            sp.dma_start(src_col[:], a["src_col"]).then_inc(ld["src"], 16)
            for t in range(NODE_TILES):
                sp.wait_ge(qkv_sb, t + 1)
                st = stage(t)
                sp.dma_start(q_tab[t * P:(t + 1) * P, :], st[:, 0:D]).then_inc(qkv_out[t % STAGES], 16)
                sp.dma_start(kv_tab[t * P:(t + 1) * P, :], st[:, D:3 * D]).then_inc(qkv_out[t % STAGES], 16)
            for g in range(16):
                sp.dma_start(emb[g * NB:(g + 1) * NB, :], a["r_flat"][g * GE:(g + 1) * GE].partition_broadcast(NB)).then_inc(ld["r"], 16)
            sp.dma_start(weights[:], a["weights"]).then_inc(ld["weights"], 16)
            sp.dma_start(yvec[:], a["attr_col"]).then_inc(ld["attr"], 16)
            sp.dma_start(b2f[0:1, 0, :], a["mlp_b2"]).then_inc(ld["weights"], 16)
            for b in range(STAGES):
                sp.wait_ge(qkv_out[b], 32 * stages_of(b))

            def loads(i, first):
                for s in range(SLOTS):
                    if not first:
                        sp.wait_ge(qe_ready, SLOTS * i + s - SLOTS + 1)
                    _, base = nc.values_load_multi_w_load_instructions(
                        base_i[0:1, bass.ds(i * BODY + s * QT, QT)], engines=(ET.SP,), min_val=0, max_val=N,
                        skip_runtime_bounds_check_because="destinations are node numbers")
                    sp.dma_start(dstb[:, s, :], dst_flat[bass.ds((i * BODY + s * QT) * P, QC)].partition_broadcast(P)).then_inc(a_in[s], 16)
                    for k in range(QT):
                        sp.dma_start(qwin[:, s, k, :], q_tab[bass.ds(base[k], P), :]).then_inc(a_in[s], 16)
            loop(sp, loads)

            sp.wait_ge(r_exp, 1)
            for g in range(16):
                sp.dma_start(emb_rows[:, g * GE:(g + 1) * GE], emb[g * NB:(g + 1) * NB, :]).then_inc(emb_out, 16)

            sp.wait_ge(score_ready, SLOTS * ITERS)
            sp.dma_start(mask_dst.rearrange("p (c e) -> p c e", c=TC), dst_flat.rearrange("(c p e) -> p c e", p=P, e=P)).then_inc(ld["mask"], 16)
            sp.dma_start(nbr_i[:], a["neighbours"]).then_inc(ld["mask"], 16)
            sp.dma_start(rowi.rearrange("p k n -> p (k n)"), a["tile_ends"].partition_broadcast(H)).then_inc(ld["mask"], 16)
            sp.wait_ge(c_sb, 1)
            sp.dma_start(carry_in, small[0:2 * H * TC, 0:P]).then_inc(c_dma, 16)
            sp.wait_ge(c_dma, 16)
            sp.dma_start(rowbuf[:, :, 0:TPAD], carry_in.rearrange("(k h c) p -> h k (c p)", k=2, h=H)).then_inc(c_dma, 16)
            sp.wait_ge(c_scan, 2)
            sp.dma_start(carry_out[0:H * TC].rearrange("(h c) p -> h (c p)", h=H), rowout[:, 0, 0:TPAD]).then_inc(c_back, 16)
            sp.dma_start(carry_out[H * TC:].rearrange("(h c) p -> h (c p)", h=H), rowout[:, 1, 1:TPAD + 1]).then_inc(c_back, 16)
            sp.wait_ge(c_back, 32)
            sp.dma_start(small[0:2 * H * TC, 0:P], carry_out).then_inc(c_back, 16)

            sp.wait_ge(bprep, 6)
            for k in range(3):
                sp.dma_start(b2rows[k:k + 1, :], b2p[0:1, k, :]).then_inc(b2_in, 16)

            sp.wait_ge(back_sb, TC)

            def loads_v(i, first):
                for s in range(SLOTS):
                    if not first:
                        sp.wait_ge(msg_ready, SLOTS * i + s - SLOTS + 1)
                    sp.dma_start(rows[:, s, :, 0:D], v_edges[:, bass.ds((i * BODY + s * QT) * D, QT * D)]
                                 .rearrange("p (t f) -> p t f", t=QT)).then_inc(v_in[s], 16)
            loop(sp, loads_v)

            for t in range(NODE_TILES):
                sp.wait_ge(up_sb, t + 1)
                sp.dma_start(up_tab[t * P:(t + 1) * P, :], work[:, t % 2, 0:D]).then_inc(up_out[t % 2], 16)

            sp.wait_ge(emb_out, 16 * 16)

            def loads_e(i, first):
                for u in range(2):
                    if not first:
                        sp.wait_ge(h1_mm, 2 * i + u - 1)
                    for half in range(2):
                        sp.dma_start(embb[half * NB:(half + 1) * NB, u, :],
                                     emb_rows[:, bass.ds((i * BODY + (2 * u + half) * QT) * P, QC)]).then_inc(e_in[u], 16)
            loop(sp, loads_e)

            for j in range(NCH):
                sp.wait_ge(ln_out, 3 * NCH + j + 1)
                w = min(CW, N - j * CW)
                sp.dma_start(out[:, j * CW:j * CW + w], R[1][:, j * CW:j * CW + w]).then_inc(fin_out, 16)
            sp.wait_ge(fin_out, 16 * NCH)

        def gather_loop(pool, table, width, landed, ready, release):
            limit, zero = pool.alloc_register(f"limit_{width}"), pool.alloc_register(f"zero_{width}")
            pool.reg_mov(limit, N)
            pool.reg_mov(zero, 0)
            def body(i, first):
                for s in range(SLOTS):
                    pool.wait_ge(ready, SLOTS * i + s + 1)
                    if not first:
                        release(i, s)
                    pool.reg_add(limit, limit, zero)
                    for k in range(QT):
                        nc.gpsimd.indirect_dma_start(
                            rows[:, s, k, 0:width], None, table,
                            bass.IndirectOffsetOnAxis(idx[:, s, k:k + 1].bitcast(U32), 0),
                            bounds_check=limit).then_inc(landed[s], 16)
            loop(pool, body)

        @block.gpsimd
        def _(pool):
            for b in range(STAGES):
                pool.wait_ge(qkv_out[b], 32 * stages_of(b))

            def release_kv(i, s):
                pool.wait_ge(prod_ready, SLOTS * i + s - SLOTS + 1)
                pool.wait_ge(v_out[s], 16 * i)
            gather_loop(pool, kv_tab, 2 * D, kv_in, idx_ready, release_kv)

            def weighted(i, first):
                for s in range(SLOTS):
                    q = SLOTS * i + s
                    pool.wait_ge(exb_ready, q + 1)
                    pool.wait_ge(v_in[s], 16 * (i + 1))
                    if not first:
                        pool.wait_ge(sum_ready, QT * (q - SLOTS + 1))
                    nc.gpsimd.tensor_tensor(msg0[:, s], rows[:, s, :, 0:D], exb[:, s], ALU.mult).then_inc(msg_ready, 1)
            loop(pool, weighted)

            for b in range(2):
                pool.wait_ge(up_out[b], 16 * (NODE_TILES // 2))

            def release_up(i, s):
                pool.wait_ge(g_used, SLOTS * i + s - SLOTS + 1)
            gather_loop(pool, up_tab, D, g_in, idx2_ready, release_up)

        @block.tensor
        def _(pe):
            pe.wait_ge(ld["x"], 32)
            for t in range(NODE_TILES):
                if t % (NODE_TILES // 2) == 0:
                    pe.wait_ge(ld_x[t // (NODE_TILES // 2)], 16)
                if t >= 2:
                    pe.wait_ge(qkv_sb, t - 1)
                pe.matmul(ps[:, t % 2, 0:3 * D], xT[:, t * P:(t + 1) * P], wqkv[:], start=True, stop=True).then_inc(qkv_mm, 1)
            pe.wait_ge(qkv_sb, NODE_TILES)

            def queries(i, first):
                for s in range(SLOTS):
                    pe.wait_ge(hotT_ready, SLOTS * i + s + 1)
                    if not first:
                        pe.wait_ge(prod_ready, SLOTS * i + s - SLOTS + 1)
                    for k in range(QT):
                        mm = pe.matmul(ps[:, s, k * P:(k + 1) * P], hot[:, s % 2, k, :], qwin[:, s, k, :], start=True, stop=True)
                    mm.then_inc(qe_ready, 1)
            loop(pe, queries)

            pe.wait_ge(ld["const"], 32)
            pe.wait_ge(ld["weights"], 32)
            pe.wait_ge(score_ready, SLOTS * ITERS)
            if TPAD > NT:
                pe.wait_ge(pad_zero, 1)
            for c in range(TC):
                if c >= 4:
                    pe.wait_ge(tr_sb, c - 3)
                for h in range(H):
                    mm = pe.transpose(ps[:, c % 4, h * P:(h + 1) * P], alpha[:, c * P:(c + 1) * P, h], ident)
                mm.then_inc(tr_mm, 1)
            pe.wait_ge(edge_cols, 2)
            pe.transpose(ps[0:2 * H * TC, 4, 0:P], small[:, P:P + 2 * H * TC], ident).then_inc(c_tr, 1)
            pe.wait_ge(c_back, 48)
            pe.transpose(ps[:, 5, 0:2 * H * TC], small[0:2 * H * TC, 0:P], ident[0:2 * H * TC, 0:2 * H * TC]).then_inc(c_mm, 1)
            pe.wait_ge(exp_ready, H)
            pe.wait_ge(tr_sb, TC)
            for c in range(TC):
                if c >= 4:
                    pe.wait_ge(back_sb, c - 3)
                for h in range(H):
                    mm = pe.transpose(ps[:, c % 4, h * P:(h + 1) * P], sc_t[:, h, c * P:(c + 1) * P], ident)
                mm.then_inc(back_mm, 1)
            pe.wait_ge(back_sb, TC)

            def sums(i, first):
                for s in range(SLOTS):
                    pe.wait_ge(msg_ready, SLOTS * i + s + 1)
                    pe.wait_ge(hot_ready, SLOTS * i + s + 1)
                    pe.wait_ge(last_hot_ready, SLOTS * i + s + 1)
                    if not first:
                        pe.wait_ge(acc_step, QT * (SLOTS * (i - 1) + s + 1) + 1)
                        pe.wait_ge(acc_step_z, QT * (SLOTS * (i - 1) + s + 1) + 1)
                    for k in range(QT):
                        for m, left in enumerate((msg0, exb)):
                            mm = pe.matmul(ps[:, 2 * s + k // 2, (2 * (k % 2) + m) * P:(2 * (k % 2) + m + 1) * P],
                                           left[:, s, k, :], hot_b[:, s, k, :], start=True, stop=True)
                        mm.then_inc(sum_ready, 1)
            loop(pe, sums)

            def by_chunk(weight, x, wait, done, banks):
                for j in range(NCH):
                    wait(j)
                    pe.matmul(ps[:, banks[j % len(banks)], 0:CW], weight, x[:, node_cols(j)], start=True, stop=True).then_inc(done, 1)

            def skip_wait(j):
                if j == 0:
                    pe.wait_ge(acc_step, QT * SLOTS * ITERS + 1)
                if j >= 2:
                    pe.wait_ge(skip_sb, j - 1)
            by_chunk(wt(W_SKIP), xT, skip_wait, skip_mm, (0, 1))

            def out1_wait(j):
                pe.wait_ge(skip_sb, j + 1)
                if j >= 2:
                    pe.wait_ge(ln_in, j - 1)
            by_chunk(wt(W_OUT), R[0], out1_wait, out1_mm, (2, 3))

            def layer_norm(n):
                for j in range(NCH):
                    g = n * NCH + j
                    pe.wait_ge(ln_in, g + 1)
                    if g >= 2:
                        pe.wait_ge(centred, g - 1)
                    pe.matmul(ps[:, 4 + g % 2, 0:CW], ones_mean[:], R[1][:, node_cols(j)], start=True, stop=True).then_inc(mean_mm, 1)
                for j in range(NCH):
                    g = n * NCH + j
                    pe.wait_ge(squared, g + 1)
                    if g >= 2:
                        pe.wait_ge(std, g - 1)
                    pe.matmul(ps[:, 6 + g % 2, 0:CW], ones_mean[:], R[2][:, node_cols(j)], start=True, stop=True).then_inc(var_mm, 1)
            layer_norm(0)

            for j in range(NCH):
                pe.wait_ge(ln_out, j + 1)
                for m in range(HID // P):
                    n = j * 4 + m
                    if n >= 2:
                        pe.wait_ge(h_sb, n - 1)
                    pe.matmul(ps[:, n % 2, 0:CW], wt(W_1 + m * P), R[1][:, node_cols(j)], start=True, stop=True).then_inc(h_mm, 1)
                pe.wait_ge(h_sb, 4 * (j + 1))
                if j >= 2:
                    pe.wait_ge(ln_in, NCH + j - 1)
                for m in range(HID // P):
                    mm = pe.matmul(ps[:, 2 + j % 2, 0:CW], wt(W_2 + m * P), hbuf[:, ((j % 2) * 4 + m) * CW:((j % 2) * 4 + m + 1) * CW],
                                   start=(m == 0), stop=(m == HID // P - 1))
                mm.then_inc(mlp_mm, 1)
            layer_norm(1)
            layer_norm(2)

            pe.wait_ge(ln_out, 3 * NCH)
            for t in range(NODE_TILES):
                if t >= 2:
                    pe.wait_ge(up_sb, t - 1)
                pe.matmul(ps[:, t % 2, 0:D], xT[:, t * P:(t + 1) * P], wt(W_UP), start=True, stop=True).then_inc(up_mm, 1)
            pe.wait_ge(up_sb, NODE_TILES)

            def hidden1(i, u, n):
                pe.wait_ge(e_in[u], 32 * (i + 1))
                if not (isinstance(n, int) and n == 0):
                    pe.wait_ge(h1_sb, n)
                pe.matmul(ps[:, 0, :], weights[0:2 * NB, W_M0:W_M0 + P], embb[0:2 * NB, u, :], start=True, stop=True).then_inc(h1_mm, 1)

            def hidden2(u, n):
                pe.wait_ge(h1_sb, n + 1)
                if not (isinstance(n, int) and n == 0):
                    pe.wait_ge(h2_sb, n)
                pe.matmul(ps[:, 1, :], wt(W_M1), h1s[:, u, :], start=True, stop=True).then_inc(h2_mm, 1)

            def edge_weights(i, first, s):
                pe.wait_ge(h2_sb, 2 * i + s // 2 + 1)
                if not first or s >= 2:
                    pe.wait_ge(w_used, SLOTS * i + s - 1)
                half, u = s % 2, s // 2
                pe.matmul(ps[:, 2 + s % 2, :], ones3[0:3, :], b2rep[0:3].rearrange("p t f -> p (t f)"),
                          start=True, stop=False, skip_group_check=True)
                for k in range(QT):
                    mm = pe.matmul(ps[:, 2 + s % 2, k * P:(k + 1) * P], h2s[64 * half:64 * half + 64, u, k * P:(k + 1) * P],
                                   weights[64 * half:64 * half + 64, W_M2:W_M2 + P], start=False, stop=True, skip_group_check=True)
                mm.then_inc(w_mm, 1)

            def sum_quad(i, s, first):
                pe.wait_ge(msgs_ready, SLOTS * i + s + 1)
                pe.wait_ge(hot2_ready, SLOTS * i + s + 1)
                if not (first and s < 2):
                    pe.wait_ge(acc2_step, QT * (SLOTS * i + s - 1) + 1)
                for k in range(QT):
                    for m, left in enumerate((MA, MB)):
                        mm = pe.matmul(ps[:, 4 + 2 * (s % 2) + k // 2, (2 * (k % 2) + m) * P:(2 * (k % 2) + m + 1) * P],
                                       left[:, s % 2, k, :], hot[:, s % 2, k, :], start=True, stop=True)
                    mm.then_inc(sum2_ready, 1)

            def edge_units(i, first, last):
                for u in range(2):
                    n = 2 * i + u
                    ahead = not (last and u == 1)
                    if ahead:
                        hidden1(i + u, 1 - u, n + 1)
                    edge_weights(i, first, 2 * u)
                    if not (first and u == 0):
                        sum_quad(i if u else i - 1, (2 * u - 1) % SLOTS, first)
                    if ahead:
                        hidden2(1 - u, n + 1)
                    edge_weights(i, first, 2 * u + 1)
                    sum_quad(i, 2 * u, first)
            pe.wait_ge(prep, 6)
            hidden1(0, 0, 0)
            hidden2(0, 0)
            loop_ahead(pe, edge_units)
            sum_quad(ITERS - 1, SLOTS - 1, False)

            for j in range(NCH):
                if j == 0:
                    pe.wait_ge(acc2_step, QT * SLOTS * ITERS + 1)
                if j >= 2:
                    pe.wait_ge(ln_in, 3 * NCH + j - 1)
                pe.matmul(ps[:, j % 2, 0:CW], wt(W_OA), acc[:, 0, node_cols(j)], start=True, stop=False)
                pe.matmul(ps[:, j % 2, 0:CW], wt(W_OB), acc[:, 1, node_cols(j)], start=False, stop=True).then_inc(fin_mm, 1)
            layer_norm(3)

        @block.scalar
        def _(act):
            def indices(i, s, ready):
                nc.scalar.copy(idx[:, s, :], src_col[:, bass.ds(i * BODY + s * QT, QT)]).then_inc(ready, 1)

            act.wait_ge(ld["src"], 16)
            for s in range(SLOTS):
                indices(0, s, idx_ready)

            def store_values(i, first):
                for s in range(SLOTS):
                    act.wait_ge(kv_in[s], 16 * QT * (i + 1))
                    act.dma_start(v_edges[:, bass.ds((i * BODY + s * QT) * D, QT * D)].rearrange("p (t f) -> p t f", t=QT),
                                  rows[:, s, :, D:2 * D]).then_inc(v_out[s], 16)
                    indices(i + 1, s, idx_ready)
                if first:
                    act.wait_ge(r_clip, 3)
                    act.wait_ge(ld["const"], 32)
                    nc.scalar.activation(emb, emb, ACT.Square, bias=consts[:, K_NEGB:K_NEGB + 1], scale=float(NB - 1)).then_inc(r_sq, 1)
                    act.wait_ge(r_sq, 1)
                    nc.scalar.activation(emb, emb, ACT.Exp, bias=consts[:, K_LN:K_LN + 1], scale=-0.5).then_inc(r_exp, 1)
            loop(act, store_values)
            act.wait_ge(yprep, 5)
            nc.scalar.activation(ysq[0], ysq[0], ACT.Sqrt).then_inc(yprep, 1)
            act.wait_ge(emb_out, 16 * 16)

            for c in range(TC):
                act.wait_ge(tr_mm, c + 1)
                nc.scalar.copy(sc_t[:, :, c * P:(c + 1) * P], ps[:, c % 4, :].rearrange("p (h e) -> p h e", h=H)).then_inc(tr_sb, 1)
            act.wait_ge(c_tr, 1)
            nc.scalar.copy(small[0:2 * H * TC, 0:P], ps[0:2 * H * TC, 4, 0:P]).then_inc(c_sb, 1)
            for h in range(H):
                act.wait_ge(shifted, h + 1)
                nc.scalar.activation(sc_t[:, h, :], sc_t[:, h, :], ACT.Exp, scale=1.0 / np.sqrt(C).item()).then_inc(exp_ready, 1)
            for c in range(TC):
                act.wait_ge(back_mm, c + 1)
                nc.scalar.copy(alpha[:, c * P:(c + 1) * P, :].rearrange("p t h -> p h t"),
                               ps[:, c % 4, :].rearrange("p (h e) -> p h e", h=H)).then_inc(back_sb, 1)
            act.wait_ge(back_sb, TC)
            for s in range(SLOTS):
                act.wait_ge(v_out[s], 16 * ITERS)

            def one_hots(i, s, n, to, squares, ready):
                for k in range(n):
                    op = nc.scalar.activation(to[:, k, :], iota, ACT.Square, bias=nrel[:, bass.ds(i * BODY + s * QT + k, 1)])
                op.then_inc(squares, 1)
                act.wait_ge(squares, SLOTS * i + s + 1)
                nc.scalar.activation(to[:, 0:n, :], to[:, 0:n, :], ACT.Relu, bias=1.0, scale=-1.0).then_inc(ready, 1)

            act.wait_ge(rel_ready, 1)
            def spread(i, first):
                for s in range(SLOTS):
                    if not first:
                        act.wait_ge(sum_ready, QT * (SLOTS * (i - 1) + s + 1))
                    nc.scalar.copy(exb[:, s].rearrange("p t (h c) -> p (t h) c", h=H),
                                   alpha[:, bass.ds(i * BODY + s * QT, QT), :].rearrange("p t h -> p (t h)").unsqueeze(2)
                                   .to_broadcast([P, QT * H, C])).then_inc(exb_ready, 1)
                    one_hots(i, s, QT - 1, hot_b[:, s], square_ready, hot_ready)
            loop(act, spread)

            def layer_norm(n):
                for j in range(NCH):
                    act.wait_ge(centred, n * NCH + j + 1)
                    nc.scalar.activation(R[2][:, node_cols(j)], R[1][:, node_cols(j)], ACT.Square).then_inc(squared, 1)
                for j in range(NCH):
                    g = n * NCH + j
                    act.wait_ge(var_mm, g + 1)
                    nc.scalar.activation(R[2][:, node_cols(j)], ps[:, 6 + g % 2, 0:CW], ACT.Sqrt,
                                         bias=consts[:, K_EPS:K_EPS + 1]).then_inc(std, 1)
            layer_norm(0)
            for j in range(NCH):
                if j >= 2:
                    act.wait_ge(mlp_mm, j - 1)
                for m in range(HID // P):
                    n = 4 * j + m
                    act.wait_ge(h_mm, n + 1)
                    nc.scalar.activation(hbuf[:, ((j % 2) * 4 + m) * CW:((j % 2) * 4 + m + 1) * CW], ps[:, n % 2, 0:CW], ACT.Relu,
                                         bias=vec(V_B1 + m)).then_inc(h_sb, 1)
            layer_norm(1)
            layer_norm(2)
            for t in range(NODE_TILES):
                act.wait_ge(up_mm, t + 1)
                if t >= 2:
                    act.wait_ge(up_out[t % 2], 16 * (t // 2))
                nc.scalar.mul(work[:, t % 2, 0:D], ps[:, t % 2, 0:D], 1.0 / np.sqrt(32).item()).then_inc(up_sb, 1)

            act.wait_ge(acc2_zero, 1)
            for s in range(SLOTS):
                indices(0, s, idx2_ready)

            def silu1(u, n):
                act.wait_ge(h1_mm, n + 1)
                if not (isinstance(n, int) and n < 2):
                    act.wait_ge(h2_mm, n - 1)
                nc.scalar.activation(h1s[:, u, :], ps[:, 0, :], ACT.Silu, bias=vec(V_MB0)).then_inc(h1_sb, 1)

            def silu2(u, n):
                act.wait_ge(h2_mm, n + 1)
                if not (isinstance(n, int) and n < 2):
                    act.wait_ge(w_mm, 2 * n - 2)
                nc.scalar.activation(h2s[:, u, :], ps[:, 1, :], ACT.Silu, bias=vec(V_MB1)).then_inc(h2_sb, 1)

            def edge_units(i, first, last):
                for u in range(2):
                    n = 2 * i + u
                    ahead = not (last and u == 1)
                    for half, silu in enumerate((silu1, silu2)):
                        s = 2 * u + half
                        if ahead:
                            silu(1 - u, n + 1)
                        if not first or s >= 2:
                            act.wait_ge(sum2_ready, QT * (SLOTS * i + s - 1))
                        one_hots(i, s, QT, hot[:, s % 2], square2_ready, hot2_ready)
                        if not last:
                            act.wait_ge(g_in[s], 16 * QT * (i + 1))
                            indices(i + 1, s, idx2_ready)
            silu1(0, 0)
            silu2(0, 0)
            loop_ahead(act, edge_units)
            layer_norm(3)

        @block.vector
        def _(dve):
            v = nc.vector
            yv = yvec[:].rearrange("p (t c) -> p t c", c=3)

            dve.wait_ge(ld["x"], 32)
            for t in range(NODE_TILES):
                dve.wait_ge(qkv_mm, t + 1)
                if t >= STAGES:
                    dve.wait_ge(qkv_out[t % STAGES], 32 * (t // STAGES))
                v.tensor_tensor(stage(t), ps[:, t % 2, 0:3 * D], bqkv[:], ALU.add).then_inc(qkv_sb, 1)
            dve.wait_ge(ld["graph"], 32)
            dve.wait_ge(ld["const"], 32)
            v.tensor_tensor(rel[:], dst_i[:], base_i[:], ALU.subtract).then_inc(prep, 1)
            v.tensor_scalar(win[:], base_i[:], consts[:, K_COL:K_COL + 1], None, ALU.add).then_inc(prep, 1)
            v.memset(ones_mean[:], 1.0 / D).then_inc(prep, 1)
            v.memset(ones3[:], 1.0).then_inc(prep, 1)
            if TPAD > NT:
                v.memset(alpha[:, NT:TPAD, :], 0.0).then_inc(pad_zero, 1)
            dve.wait_ge(prep, 4)

            def radius():
                dve.wait_ge(ld["r"], 16 * 16)
                v.tensor_scalar(emb_m, emb, 1.0, 1e4, ALU.is_gt, ALU.mult).then_inc(r_clip, 1)
                dve.wait_ge(r_clip, 1)
                v.tensor_scalar(emb, emb, 0.0, 1.0, ALU.max, ALU.min).then_inc(r_clip, 1)
                dve.wait_ge(r_clip, 2)
                v.tensor_tensor(emb, emb, emb_m, ALU.add).then_inc(r_clip, 1)

            def product(i, s, first):
                q = SLOTS * i + s
                dve.wait_ge(qe_ready, q + 1)
                dve.wait_ge(kv_in[s], 16 * QT * (i + 1))
                if not first:
                    dve.wait_ge(score_ready, q - 1)
                v.tensor_tensor(work[:, s % 2, :].rearrange("p (t f) -> p t f", t=QT),
                                ps[:, s, :].rearrange("p (t f) -> p t f", t=QT), rows[:, s, :, 0:D], ALU.mult).then_inc(prod_ready, 1)
                dve.wait_ge(prod_ready, q + 1)
                v.tensor_reduce(alpha[:, bass.ds(i * BODY + s * QT, QT), :].rearrange("p t h -> p (t h)"),
                                work[:, s % 2, :].rearrange("p (g c) -> p g c", c=C), AX.X, ALU.add).then_inc(score_ready, 1)

            def scores(i, first):
                for s in range(SLOTS):
                    q = SLOTS * i + s
                    dve.wait_ge(a_in[s], 16 * (1 + QT) * (i + 1))
                    if not first or s >= 2:
                        dve.wait_ge(qe_ready, q - 1)
                    v.tensor_tensor(hot[:, s % 2], dstb[:, s, :].rearrange("p (t e) -> p t e", t=QT),
                                    win[:, bass.ds(i * BODY + s * QT, QT)].unsqueeze(2).to_broadcast([P, QT, P]),
                                    ALU.is_equal).then_inc(hotT_ready, 1)
                    if not (first and s == 0):
                        product(i if s else i - 1, (s - 1) % SLOTS, first and s < 3)
                if first:
                    radius()
            loop(dve, scores)
            product(ITERS - 1, SLOTS - 1, False)

            v.tensor_scalar(nrel, rel[:], -1.0, None, ALU.mult).then_inc(rel_ready, 1)
            dve.wait_ge(ld["attr"], 16)
            for n, c in enumerate(range(3)):
                if c:
                    dve.wait_ge(yprep, 2 * n - 1)
                v.tensor_tensor(ysq[min(c, 1)], yv[:, :, c], yv[:, :, c], ALU.mult).then_inc(yprep, 1)
                if c:
                    dve.wait_ge(yprep, 2 * n)
                    v.tensor_tensor(ysq[0], ysq[0], ysq[1], ALU.add).then_inc(yprep, 1)
            dt = masks[:, 2, :].rearrange("p (c e) -> p c e", c=TC)
            mf = masks[:, 0, :].rearrange("p (c e) -> p c e", c=TC)
            m1 = masks[:, 1, :].rearrange("p (c e) -> p c e", c=TC)
            dve.wait_ge(ld["mask"], 16 * 3)
            v.tensor_copy(dt, mask_dst.rearrange("p (c e) -> p c e", c=TC)).then_inc(mask_ready, 1)
            v.tensor_copy(nbr[:], nbr_i[:].rearrange("p (k c) -> p k c", k=2)).then_inc(mask_ready, 1)
            dve.wait_ge(mask_ready, 2)
            v.tensor_tensor(mf[:, :, 1:P], dt[:, :, 1:P], dt[:, :, 0:P - 1], ALU.is_equal).then_inc(mask_ready, 1)
            v.memset(mf[:, :, 0:1], 0.0).then_inc(mask_ready, 1)
            v.tensor_tensor(m1, dt, nbr[:, 0, :].unsqueeze(2).to_broadcast([P, TC, P]), ALU.is_equal).then_inc(mask_ready, 1)
            dve.wait_ge(mask_ready, 5)
            v.tensor_tensor(dt, dt, nbr[:, 1, :].unsqueeze(2).to_broadcast([P, TC, P]), ALU.is_equal).then_inc(mask_ready, 1)
            dve.wait_ge(mask_ready, 6)
            v.tensor_scalar(masks, masks, 0.5, 2 * BIG, ALU.subtract, ALU.mult).then_inc(mask_ready, 1)
            dve.wait_ge(mask_ready, 7)
            dve.wait_ge(tr_sb, TC)
            for h in range(H):
                v.tensor_tensor_scan(fw_t[:, h, :], masks[:, 0, :], sc_t[:, h, :], -BIG, ALU.min, ALU.max).then_inc(scan_f, 1)
            v.memset(mback[:, TPAD - 1:TPAD], -BIG).then_inc(mask_ready, 1)
            v.tensor_copy(mback[:, 0:TPAD - 1], masks[:, 0, 1:TPAD]).then_inc(mask_ready, 1)
            dve.wait_ge(mask_ready, 9)
            for h in range(H):
                dve.wait_ge(scan_f, h + 1)
                v.tensor_tensor_scan(tot_t[:, h, ::-1], mback[:, ::-1], fw_t[:, h, ::-1], -BIG, ALU.min, ALU.max).then_inc(scan_b, 1)
            K = H * TC
            v.tensor_copy(small[:, P:P + K].rearrange("p (h c) -> p h c", h=H),
                          fw_t.rearrange("p h (c e) -> p h c e", c=TC)[:, :, :, P - 1]).then_inc(edge_cols, 1)
            dve.wait_ge(scan_b, H)
            v.tensor_copy(small[:, P + K:P + 2 * K].rearrange("p (h c) -> p h c", h=H),
                          tot_t.rearrange("p h (c e) -> p h c e", c=TC)[:, :, :, 0]).then_inc(edge_cols, 1)
            for s in range(SLOTS):
                dve.wait_ge(v_out[s], 16 * ITERS)
            for k in range(2):
                v.tensor_tensor(rowmask[:, k, :], rowi[:, 2 * k, :], rowi[:, 2 * k + 1, :], ALU.is_equal).then_inc(mask_ready, 1)
            dve.wait_ge(mask_ready, 11)
            v.tensor_scalar(rowmask, rowmask, 0.5, 2 * BIG, ALU.subtract, ALU.mult).then_inc(mask_ready, 1)
            v.memset(rowout[:, 0, 0:1], -BIG).then_inc(mask_ready, 1)
            v.memset(rowout[:, 1, TPAD:TPAD + 1], -BIG).then_inc(mask_ready, 1)
            dve.wait_ge(mask_ready, 14)
            dve.wait_ge(c_dma, 32)
            v.tensor_tensor_scan(rowout[:, 0, 1:TPAD + 1], rowmask[:, 0, :], rowbuf[:, 0, :], -BIG, ALU.min, ALU.max).then_inc(c_scan, 1)
            v.tensor_tensor_scan(rowout[:, 1, 0:TPAD][:, ::-1], rowmask[:, 1, ::-1], rowbuf[:, 1, ::-1], -BIG, ALU.min, ALU.max).then_inc(c_scan, 1)
            dve.wait_ge(yprep, 6)
            v.tensor_scalar(ysq[0], ysq[0], 1e-12, None, ALU.add).then_inc(yprep, 1)
            dve.wait_ge(yprep, 7)
            v.reciprocal(ysq[1], ysq[0]).then_inc(yprep, 1)
            dve.wait_ge(yprep, 8)
            v.scalar_tensor_tensor(out=yv, in0=yv, scalar=np.sqrt(3).item(),
                                   in1=ysq[1].unsqueeze(2).to_broadcast([P, NT, 3]), op0=ALU.mult, op1=ALU.mult).then_inc(yprep, 1)
            dve.wait_ge(ld["weights"], 32)
            v.tensor_scalar(weights[:, W_M2 + 96:W_M2 + 128], weights[:, W_M2 + 96:W_M2 + 128],
                            1.0 / np.sqrt(3).item(), None, ALU.mult).then_inc(prep, 1)
            v.tensor_scalar(b2f[0:1, 0, 96:128], b2f[0:1, 0, 96:128], 1.0 / np.sqrt(3).item(), None, ALU.mult).then_inc(bprep, 1)
            for k in range(3):
                dve.wait_ge(bprep, 2 * k + 1)
                v.tensor_copy(b2p[0:1, k, :], b2f[0:1, k, :]).then_inc(bprep, 1)
                if k < 2:
                    dve.wait_ge(bprep, 2 * k + 2)
                    v.tensor_tensor(b2f[0:1, k + 1, :], b2f[0:1, k, :], b2p[0:1, k, :], ALU.subtract).then_inc(bprep, 1)
            dve.wait_ge(c_mm, 1)
            v.tensor_copy(small[:, P:P + 2 * K], ps[:, 5, 0:2 * K]).then_inc(c_use, 1)
            dve.wait_ge(c_use, 1)
            n = 0
            for k in range(2):
                for h in range(H):
                    v.tensor_tensor(fw_t[:, h, :].rearrange("p (c e) -> p c e", c=TC),
                                    masks[:, 1 + k, :].rearrange("p (c e) -> p c e", c=TC),
                                    small[:, P + k * K + h * TC:P + k * K + (h + 1) * TC].unsqueeze(2).to_broadcast([P, TC, P]),
                                    ALU.min).then_inc(mx, 1)
                for h in range(H):
                    dve.wait_ge(mx, n + H)
                    v.tensor_tensor(tot_t[:, h, :], tot_t[:, h, :], fw_t[:, h, :], ALU.max).then_inc(mx, 1)
                    n += 1
                n += H
                dve.wait_ge(mx, n)
            for h in range(H):
                v.tensor_tensor(sc_t[:, h, :], sc_t[:, h, :], tot_t[:, h, :], ALU.subtract).then_inc(shifted, 1)
            dve.wait_ge(back_sb, TC)

            def bases(i, s, n=QT):
                _, base = nc.values_load_multi_w_load_instructions(
                    base_i[0:1, bass.ds(i * BODY + s * QT, n)], engines=(ET.DVE,), min_val=0, max_val=N,
                    skip_runtime_bounds_check_because="destinations are node numbers")
                return base

            def add_tile(i, s, k, base, bank, ready, step):
                t = QT * (SLOTS * i + s) + k
                if k % 2 == 0:
                    dve.wait_ge(ready, t + 2)
                dve.wait_ge(step, t + 1)
                to = acc[:, :, bass.ds(base[k], P)]
                v.tensor_tensor(to, to, ps[:, bank + k // 2, (k % 2) * 256:(k % 2) * 256 + 256]
                                .rearrange("p (m f) -> p m f", m=2), ALU.add).then_inc(step, 1)

            def add_halves(i, s, k, base, bank, ready, steps):
                t = QT * (SLOTS * i + s) + k
                if k % 2 == 0:
                    dve.wait_ge(ready, t + 2)
                for m in range(2):
                    dve.wait_ge(steps[m], t + 1)
                    to = acc[:, m, bass.ds(base[k], P)]
                    v.tensor_tensor(to, to, ps[:, bank + k // 2, (2 * (k % 2) + m) * P:(2 * (k % 2) + m + 1) * P],
                                    ALU.add).then_inc(steps[m], 1)

            v.memset(acc[:], 0.0).then_inc(acc_zero, 1)
            v.memset(flag[:, 0:1], 0.0).then_inc(acc_step, 1)
            v.memset(flag[:, 1:2], 0.0).then_inc(acc_step_z, 1)
            dve.wait_ge(acc_zero, 1)
            dve.wait_ge(acc_step, 1)

            def last_hot(t, b):
                v.tensor_scalar(hot_b[:, b, QT - 1, :], iota, rel[:, bass.ds(t, 1)], None, ALU.is_equal).then_inc(last_hot_ready, 1)

            def sum_edges(i, first, last):
                base = bases(i, 0, BODY)
                for s in range(SLOTS):
                    q = SLOTS * i + s
                    if not (last and s == SLOTS - 1):
                        if not (first and s < SLOTS - 1):
                            dve.wait_ge(sum_ready, QT * (q - SLOTS + 2))
                        last_hot((q + 2) * QT - 1, (s + 1) % SLOTS)
                    for k in range(QT):
                        add_halves(i, s, k, base[s * QT:], 2 * s, sum_ready, (acc_step, acc_step_z))
            last_hot(QT - 1, 0)
            loop_ahead(dve, sum_edges)

            dve.wait_ge(acc_step, QT * SLOTS * ITERS + 1)
            dve.wait_ge(acc_step_z, QT * SLOTS * ITERS + 1)
            for j in range(NCH):
                cs = node_cols(j)
                v.tensor_scalar(R[3][:, cs], acc[:, 1, cs], 1e-30, None, ALU.max).then_inc(conv_a, 1)
            for j in range(NCH):
                cs = node_cols(j)
                dve.wait_ge(conv_a, j + 1)
                v.reciprocal(R[2][:, cs], R[3][:, cs]).then_inc(conv_b, 1)
                dve.wait_ge(conv_b, j + 1)
                v.tensor_tensor(R[0][:, cs], acc[:, 0, cs], R[2][:, cs], ALU.mult).then_inc(conv, 1)
            for j in range(NCH):
                cs = node_cols(j)
                dve.wait_ge(conv, j + 1)
                dve.wait_ge(skip_mm, j + 1)
                v.scalar_tensor_tensor(out=R[0][:, cs], in0=ps[:, j % 2, 0:CW], scalar=vec(V_BSKIP), in1=R[0][:, cs],
                                       op0=ALU.add, op1=ALU.add).then_inc(skip_sb, 1)
            for j in range(NCH):
                cs = node_cols(j)
                dve.wait_ge(out1_mm, j + 1)
                v.scalar_tensor_tensor(out=R[1][:, cs], in0=ps[:, 2 + j % 2, 0:CW], scalar=vec(V_BOUT), in1=xT[:, cs],
                                       op0=ALU.add, op1=ALU.add).then_inc(ln_in, 1)

            def layer_norm(n, affine=None):
                for j in range(NCH):
                    g, cs = n * NCH + j, node_cols(j)
                    dve.wait_ge(mean_mm, g + 1)
                    v.tensor_tensor(R[1][:, cs], R[1][:, cs], ps[:, 4 + g % 2, 0:CW], ALU.subtract).then_inc(centred, 1)
                for j in range(NCH):
                    g, cs = n * NCH + j, node_cols(j)
                    dve.wait_ge(std, g + 1)
                    v.reciprocal(R[2][:, cs], R[2][:, cs]).then_inc(inv, 1)
                    dve.wait_ge(inv, g + 1)
                    op = v.tensor_tensor(R[1][:, cs], R[1][:, cs], R[2][:, cs], ALU.mult)
                    if affine is None:
                        op.then_inc(ln_out, 1)
                    else:
                        op.then_inc(scaled, 1)
                        dve.wait_ge(scaled, g + 1)
                        v.tensor_scalar(R[1][:, cs], R[1][:, cs], vec(affine), vec(affine + 1), ALU.mult, ALU.add).then_inc(ln_out, 1)
            layer_norm(0, V_L1W)
            for j in range(NCH):
                cs = node_cols(j)
                dve.wait_ge(mlp_mm, j + 1)
                v.scalar_tensor_tensor(out=R[1][:, cs], in0=ps[:, 2 + j % 2, 0:CW], scalar=vec(V_B2), in1=R[1][:, cs],
                                       op0=ALU.add, op1=ALU.add).then_inc(ln_in, 1)
            layer_norm(1, V_L2W)
            for j in range(NCH):
                cs = node_cols(j)
                dve.wait_ge(ln_out, NCH + j + 1)
                v.tensor_tensor(R[1][:, cs], R[1][:, cs], xT[:, cs], ALU.add).then_inc(ln_in, 1)
            v.memset(acc[:], 0.0).then_inc(acc2_zero, 1)
            for j in range(NCH):
                g, cs = 2 * NCH + j, node_cols(j)
                dve.wait_ge(mean_mm, g + 1)
                v.tensor_tensor(R[1][:, cs], R[1][:, cs], ps[:, 4 + g % 2, 0:CW], ALU.subtract).then_inc(centred, 1)
            for j in range(NCH):
                g, cs = 2 * NCH + j, node_cols(j)
                dve.wait_ge(std, g + 1)
                v.reciprocal(R[2][:, cs], R[2][:, cs]).then_inc(inv, 1)
                dve.wait_ge(inv, g + 1)
                v.tensor_tensor(xT[:, cs], R[1][:, cs], R[2][:, cs], ALU.mult).then_inc(ln_out, 1)

            dve.wait_ge(b2_in, 48)
            v.tensor_copy(b2rep[0:3], b2rows[0:3].unsqueeze(1).to_broadcast([3, QT, D])).then_inc(prep, 1)
            v.memset(flag[:, 1:2], 0.0).then_inc(acc2_step, 1)
            dve.wait_ge(acc2_zero, 1)
            dve.wait_ge(acc2_step, 1)
            dve.wait_ge(ln_out, 3 * NCH)

            def messages(i, first):
                for s in range(SLOTS):
                    q = SLOTS * i + s
                    b = s % 2
                    before = None if first and s == 0 else (i if s else i - 1, (s - 1) % SLOTS)
                    if before:
                        base = bases(*before)

                    def add(k):
                        if before:
                            add_tile(*before, k, base, 4 + 2 * (before[1] % 2), sum2_ready, acc2_step)
                    g = rows[:, s, :, 0:D]
                    w = ps[:, 2 + b, :].rearrange("p (t f) -> p t f", t=QT)
                    ss = g[:, :, 0:32]
                    vv = g[:, :, 32:128].rearrange("p t (c m) -> p t c m", c=3)
                    y = yvec[:, bass.ds((i * BODY + s * QT) * 3, 3 * QT)].rearrange("p (t c) -> p t c", c=3) \
                        .unsqueeze(3).to_broadcast([P, QT, 3, 32])
                    vyb = vy[:, b].rearrange("p t (c m) -> p t c m", c=3)
                    dve.wait_ge(g_in[s], 16 * QT * (i + 1))
                    v.tensor_tensor(vyb, vv, y, ALU.mult).then_inc(vy_ready, 1)
                    dve.wait_ge(w_mm, q + 1)
                    v.tensor_tensor(ub[:, b], w[:, :, 32:64], ss, ALU.mult).then_inc(u_ready, 1)
                    dve.wait_ge(vy_ready, q + 1)
                    v.tensor_tensor(tb[:, 2 * b], vyb[:, :, 0], vyb[:, :, 1], ALU.add).then_inc(t1_ready, 1)
                    add(0)
                    if not first or s >= 2:
                        dve.wait_ge(sum2_ready, QT * (q - 1))
                    v.tensor_tensor(MA[:, b, :, 0:32], w[:, :, 0:32], ss, ALU.mult)
                    dve.wait_ge(t1_ready, q + 1)
                    v.tensor_tensor(tb[:, 2 * b + 1], tb[:, 2 * b], vyb[:, :, 2], ALU.add).then_inc(t2_ready, 1)
                    add(1)
                    v.tensor_tensor(MB[:, b, :, 32:128].rearrange("p t (c m) -> p t c m", c=3),
                                    w[:, :, 64:96].unsqueeze(2).to_broadcast([P, QT, 3, 32]), vv, ALU.mult).then_inc(g_used, 1)
                    add(2)
                    dve.wait_ge(t2_ready, q + 1)
                    v.tensor_tensor(MB[:, b, :, 0:32], w[:, :, 96:128], tb[:, 2 * b + 1], ALU.mult).then_inc(w_used, 1)
                    dve.wait_ge(u_ready, q + 1)
                    v.tensor_tensor(MA[:, b, :, 32:128].rearrange("p t (c m) -> p t c m", c=3),
                                    ub[:, b].unsqueeze(2).to_broadcast([P, QT, 3, 32]), y, ALU.mult).then_inc(msgs_ready, 1)
                    add(3)
            loop(dve, messages)
            base = bases(ITERS - 1, SLOTS - 1)
            for k in range(QT):
                add_tile(ITERS - 1, SLOTS - 1, k, base, 4 + 2 * ((SLOTS - 1) % 2), sum2_ready, acc2_step)

            for j in range(NCH):
                cs = node_cols(j)
                dve.wait_ge(fin_mm, j + 1)
                v.scalar_tensor_tensor(out=R[1][:, cs], in0=ps[:, j % 2, 0:CW], scalar=1.0 / (8.0 * 16.0), in1=xT[:, cs],
                                       op0=ALU.mult, op1=ALU.add).then_inc(ln_in, 1)
            layer_norm(3)


_SHAPES = {
    "consts": (P, K_N), "vecs": (P, V_N), "weights": (P, W_N), "wqkv": (P, 3 * D), "bqkv": (3 * D,), "xT": (P, NW),
    "src_col": (P, NT + BODY), "dst_col": (P, NT), "dst_first": (NT,), "dst_flat": (TPAD * P,), "neighbours": (P, 2 * TC),
    "tile_ends": (4 * TPAD,), "r_flat": (NT * P,), "attr_col": (P, 3 * NT), "mlp_b2": (1, D),
}


def layout(x):
    f = {k: np.asarray(v) for k, v in x.items()}

    def l0(n):
        return f["L0_gnn_" + n]

    def l1(n):
        return f["L1_gnn_" + n]

    a = {}
    c = np.zeros((P, K_N), np.float32)
    c[:, K_ID:K_ID + P] = np.eye(P)
    c[:, K_IOTA:K_IOTA + P] = np.arange(P)[None]
    c[:, K_COL] = np.arange(P)
    c[:, K_NEGB] = -(np.arange(P) % NB)
    c[:, K_LN] = 0.5 * np.log(NB)
    c[:, K_EPS] = EPS
    a["consts"] = c
    v = np.zeros((P, V_N), np.float32)
    for j, n in ((V_BSKIP, "bskip"), (V_BOUT, "bout"), (V_L1W, "ln1_w"), (V_L1B, "ln1_b"), (V_L2W, "ln2_w"), (V_L2B, "ln2_b"), (V_B2, "b2")):
        v[:, j] = l0(n)
    v[:, V_B1:V_B1 + 4] = l0("b1").reshape(4, P).T
    for h in range(2):
        v[64 * h:64 * h + 64, V_MB0] = l1("mlp_b0")
        v[64 * h:64 * h + 64, V_MB1] = l1("mlp_b1")
    a["vecs"] = v
    w = np.zeros((P, W_N), np.float32)
    w[:, W_SKIP:W_SKIP + D] = l0("Wskip").T
    w[:, W_OUT:W_OUT + D] = l0("Wout").T
    w[:, W_1:W_1 + HID] = l0("W1").T
    w[:, W_2:W_2 + HID] = l0("W2").T.reshape(4, P, D).transpose(1, 0, 2).reshape(P, HID)
    w[0:32, W_UP:W_UP + 32] = l1("W_up0")
    w[0:32, W_OA:W_OA + 32] = l1("W_out0")[0:32]
    w[0:32, W_OB:W_OB + 32] = l1("W_out0")[32:64]
    for q in range(3):
        w[32 + q:D:3, W_UP + 32 + 32 * q:W_UP + 64 + 32 * q] = l1("W_up1")
        w[32 + 32 * q:64 + 32 * q, W_OA + 32 + q:W_OA + D:3] = l1("W_out1")[0:32]
        w[32 + 32 * q:64 + 32 * q, W_OB + 32 + q:W_OB + D:3] = l1("W_out1")[32:64]
    for h in range(2):
        w[64 * h:64 * h + 64, W_M1 + 64 * h:W_M1 + 64 * h + 64] = l1("mlp_w1")
        w[64 * h:64 * h + 64, W_M2:W_M2 + D] = l1("mlp_w2")
        w[NB * h:NB * h + NB, W_M0 + 64 * h:W_M0 + 64 * h + 64] = l1("mlp_w0")
    a["weights"] = w
    a["wqkv"] = np.concatenate([l0("Wq").T, l0("Wk").T, l0("Wv").T], 1)
    a["bqkv"] = np.concatenate([l0("bq"), l0("bk"), l0("bv")])
    a["xT"] = np.zeros((P, NW), np.float32)
    a["xT"][:, :N] = f["x"].T
    src = np.zeros((NT + BODY) * P, np.int32)
    src[:E] = f["src"]
    dst = np.full(TPAD * P, N, np.int32)
    dst[:E] = f["dst"]
    a["src_col"] = src.reshape(-1, P).T
    tiles = dst.reshape(TPAD, P)
    a["dst_col"] = tiles[:NT].T
    a["dst_first"] = tiles[:NT, 0]
    a["dst_flat"] = dst
    first, last = tiles[:, 0], tiles[:, -1]
    before = np.concatenate([[-1], last[:-1]]).astype(np.int32)
    after = np.concatenate([first[1:], [-1]]).astype(np.int32)
    a["neighbours"] = np.concatenate([before.reshape(TC, P).T, after.reshape(TC, P).T], 1)
    a["tile_ends"] = np.concatenate([last, before, first, after])
    r = np.zeros(NT * P, np.float32)
    r[:E] = f["edge_weight"]
    a["r_flat"] = r
    e = np.zeros((NT * P, 3), np.float32)
    e[:E] = f["edge_attr_3"]
    a["attr_col"] = e.reshape(NT, P, 3).transpose(1, 0, 2).reshape(P, 3 * NT)
    a["mlp_b2"] = l1("mlp_b2").reshape(1, D)
    return {k: np.ascontiguousarray(t) for k, t in a.items()}


def kernel(**inputs):
    import concourse.bacc as bacc
    from concourse.bass_utils import run_bass_kernel_spmd as run

    nc = bacc.Bacc("TRN2", target_bir_lowering=False, num_devices=1)
    arrays = layout(inputs)
    aps = {}
    for k, shape in _SHAPES.items():
        assert arrays[k].shape == shape, (k, arrays[k].shape, shape)
        aps[k] = nc.dram_tensor("in_" + k, shape, mybir.dt.from_np(arrays[k].dtype), kind="ExternalInput").ap()
    out = nc.dram_tensor("out_t", (D, N), F32, kind="ExternalOutput").ap()
    build(nc, aps, out)
    r = run(nc, [{"in_" + k: t for k, t in arrays.items()}], core_ids=[0])
    return np.ascontiguousarray(r.results[0]["out_t"].T)
```

```python
from contextlib import ExitStack

import concourse.bass as bass
from concourse import mybir
import numpy as np

P = 128
F32 = mybir.dt.float32
BF16 = mybir.dt.bfloat16
I32 = mybir.dt.int32
U32 = mybir.dt.uint32
ALU = mybir.AluOpType
ACT = mybir.ActivationFunctionType
AX = mybir.AxisListType
ET = mybir.EngineType

N, E, D, H, C, HID = 3125, 103125, 128, 4, 32, 512
EPS = 1e-5
NB = 8
QT = 4
SLOTS = 4
BODY = QT * SLOTS
ITERS = -(-E // (P * BODY))
NT = ITERS * BODY
TC = -(-NT // P)
TPAD = TC * P
NODE_TILES = -(-(N + P) // P)
NW = NODE_TILES * P
CT = 4
CW = CT * P
NCH = -(-N // CW)
GE = NT * P // 16
BIG = 1e38
LATE = 2
QC = QT * P
assert 3 * SLOTS * QC + 2 * NW <= 4 * NW and CW <= 512 and NT * P >= E and TPAD >= NT

K_ID, K_IOTA, K_COL, K_NEGB, K_LN, K_EPS = 0, 128, 256, 257, 258, 259
K_N = 260
V_BSKIP, V_BOUT, V_L1W, V_L1B, V_L2W, V_L2B, V_B2, V_B1, V_MB0, V_MB1 = 0, 1, 2, 3, 4, 5, 6, 7, 11, 12
V_N = 13
W_SKIP, W_OUT, W_1, W_2, W_UP, W_M1, W_M2, W_OA, W_OB, W_M0 = 0, 128, 256, 768, 1280, 1408, 1536, 1664, 1792, 1920
W_N = 2048


def build(nc, a, out):
    with ExitStack() as ctx:
        def sb(name, shape, dt=F32):
            return ctx.enter_context(nc.sbuf_tensor(name, shape, dt))

        def sem(name):
            return ctx.enter_context(nc.semaphore(name))

        def slot_sems(name, n=SLOTS):
            return [sem(f"{name}{i}") for i in range(n)]

        def dram(name, shape, dt=F32):
            return nc.dram_tensor(name, shape, dt, kind="Internal").ap()

        q_tab = dram("q_tab", [NW, D])
        kv_tab = dram("kv_tab", [NW, 2 * D])
        up_tab = dram("up_tab", [-(-N // P) * P, D])
        v_edges = dram("v_edges", [P, NT * D])
        emb_rows = dram("emb_rows", [NB, NT * P])
        carry_in = dram("carry_in", [2 * H * TC, P])
        carry_out = dram("carry_out", [2 * H * TC, P])

        consts = sb("consts", [P, K_N])
        vecs = sb("vecs", [P, V_N])
        weights = sb("weights", [P, W_N])
        wqkv = sb("wqkv", [P, 3 * D])
        bqkv = sb("bqkv", [P, 3 * D])
        xT = sb("xT", [P, NW])
        src_col = sb("src_col", [P, NT + BODY], I32)
        dst_i = sb("dst_i", [P, NT], I32)
        base_i = sb("base_i", [P, NT], I32)
        rel = sb("rel", [P, NT])
        win = sb("win", [P, NT])
        yvec = sb("yvec", [P, NT * 3])
        alpha = sb("alpha", [P, TPAD, H])
        acc = sb("acc", [P, 2, NW])
        idx = sb("idx", [P, SLOTS, QT], I32)
        nbr_i = sb("nbr_i", [P, 2 * TC], I32)
        nbr = sb("nbr", [P, 2, TC])
        flag = sb("flag", [P, 2])
        b2p = sb("b2p", [P, 3, D], BF16)
        b2rows = sb("b2rows", [P, D], BF16)
        rows = sb("rows", [P, SLOTS, QT, 2 * D])
        qwin = sb("qwin", [P, SLOTS, QT, D])
        dstb = sb("dstb", [P, SLOTS, QC], I32)
        hot = sb("hot", [P, 2, QT, P])
        work = sb("work", [P, 2, QC])
        arena = sb("arena", [P, 4 * NW])
        small = sb("small", [P, P + 2 * H * TC])
        ones_mean = sb("ones_mean", [P, P])
        b2f = sb("b2f", [P, 3, D])
        b2rep = sb("b2rep", [P, QT, D], BF16)
        ones3 = sb("ones3", [P, P], BF16)
        ps = ctx.enter_context(nc.psum_tensor("ps", [P, 8, 512], F32))

        ident = consts[:, K_ID:K_ID + P]
        iota = consts[:, K_IOTA:K_IOTA + P]

        def vec(j, n=1):
            return vecs[:, j:j + n]

        def wt(off, n=P):
            return weights[:, off:off + n]

        emb = arena[:, 0:GE]
        emb_m = arena[:, GE:2 * GE]
        sc_t = arena[:, 0:H * TPAD].rearrange("p (h n) -> p h n", h=H)
        fw_t = arena[:, H * TPAD:2 * H * TPAD].rearrange("p (h n) -> p h n", h=H)
        tot_t = arena[:, 2 * H * TPAD:3 * H * TPAD].rearrange("p (h n) -> p h n", h=H)
        mask_dst = arena[:, 3 * H * TPAD:3 * H * TPAD + TPAD].bitcast(I32)
        mback = arena[:, 3 * H * TPAD + TPAD:3 * H * TPAD + 2 * TPAD]
        accf = acc[:].rearrange("p m n -> p (m n)")
        masks = accf[:, 0:3 * TPAD].rearrange("p (k n) -> p k n", k=3)
        rowi = accf[0:H, 3 * TPAD:7 * TPAD].bitcast(I32).rearrange("p (k n) -> p k n", k=4)
        ysq = [dstb[:].rearrange("p a b -> p (a b)")[:, j * NT:(j + 1) * NT].bitcast(F32) for j in range(2)]
        nrel = win[:]
        rowbuf = qwin[:].rearrange("p a b c -> p (a b c)")[0:H, 0:2 * TPAD].rearrange("p (k n) -> p k n", k=2)
        rowsf = rows[:].rearrange("p a b c -> p (a b c)")
        rowout = rowsf[0:H, 0:2 * (TPAD + 1)].rearrange("p (k n) -> p k n", k=2)
        rowmask = rowsf[0:H, 2 * (TPAD + 1):4 * TPAD + 2].rearrange("p (k n) -> p k n", k=2)
        exb, msg0, hot_b = [arena[:, j * SLOTS * QC:(j + 1) * SLOTS * QC].rearrange("p (s t f) -> p s t f", s=SLOTS, t=QT)
                            for j in range(3)]
        acc_odd = arena[:, 3 * SLOTS * QC:3 * SLOTS * QC + 2 * NW].rearrange("p (m n) -> p m n", m=2)
        R = [arena[:, j * NW:(j + 1) * NW] for j in range(4)]
        den = small[:, 0:CT * NCH * H].rearrange("p (t h) -> p t h", h=H)
        dev = small[:, CT * NCH * H:CT * NCH * (H + 1)]
        hbuf = rows[:].rearrange("p a b c -> p (a b c)")
        MA = arena[:, 0:2 * QC].rearrange("p (b t f) -> p b t f", b=2, t=QT)
        MB = arena[:, 2 * QC:4 * QC].rearrange("p (b t f) -> p b t f", b=2, t=QT)
        h1s = arena[:, 4 * QC:6 * QC].rearrange("p (b n) -> p b n", b=2)
        h2s = arena[:, 6 * QC:8 * QC].rearrange("p (b n) -> p b n", b=2)
        embb = arena[:, 8 * QC:10 * QC].rearrange("p (b n) -> p b n", b=2)
        vy = arena[:, 10 * QC:10 * QC + 2 * 384].rearrange("p (b t f) -> p b t f", b=2, t=QT)
        ub = arena[:, 12 * QC:12 * QC + 256].rearrange("p (b t f) -> p b t f", b=2, t=QT)
        tb = arena[:, 13 * QC:13 * QC + 512].rearrange("p (b t f) -> p b t f", b=4, t=QT)

        ld = {k: sem("ld_" + k) for k in ("const", "graph", "attr", "x", "mask", "r", "src", "weights")}
        ld_x = slot_sems("ld_x", 2)
        idx_ready = sem("idx_ready")
        prep, yprep, bprep = sem("prep"), sem("yprep"), sem("bprep")
        qkv_mm, qkv_sb, qkv_out = sem("qkv_mm"), sem("qkv_sb"), slot_sems("qkv_out", 8)
        r_clip, r_sq, r_exp, emb_out = sem("r_clip"), sem("r_sq"), sem("r_exp"), sem("emb_out")
        kv_in, a_in, v_out = slot_sems("kv_in"), slot_sems("a_in"), slot_sems("v_out")
        hotT_ready, qe_ready, prod_ready, score_ready = sem("hotT_ready"), sem("qe_ready"), sem("prod_ready"), sem("score_ready")
        tr_mm, tr_sb, scan_f, scan_b = sem("tr_mm"), sem("tr_sb"), sem("scan_f"), sem("scan_b")
        edge_cols, c_tr, c_sb, c_dma, c_scan, c_back, c_mm, c_use = (
            sem("edge_cols"), sem("c_tr"), sem("c_sb"), sem("c_dma"), sem("c_scan"), sem("c_back"), sem("c_mm"), sem("c_use"))
        mask_ready, mx, shifted, exp_ready, back_mm, back_sb = (
            sem("mask_ready"), sem("mx"), sem("shifted"), sem("exp_ready"), sem("back_mm"), sem("back_sb"))
        v_in, exb_ready, hot_ready, msg_ready, sum_ready, acc_step = (
            slot_sems("v_in"), sem("exb_ready"), sem("hot_ready"), sem("msg_ready"), sem("sum_ready"), sem("acc_step"))
        acc_zero, odd_zero, merged, pad_zero, b2_in = sem("acc_zero"), sem("odd_zero"), sem("merged"), sem("pad_zero"), sem("b2_in")
        conv_a, conv_b, conv, skip_mm, skip_sb, out1_mm = sem("conv_a"), sem("conv_b"), sem("conv"), sem("skip_mm"), sem("skip_sb"), sem("out1_mm")
        den_mm, den_wide, inv_mm, inv_spread = sem("den_mm"), sem("den_wide"), sem("inv_mm"), sem("inv_spread")
        ln_in, mean_mm, centred, squared, var_mm, std, inv, scaled, ln_out = (
            sem("ln_in"), sem("mean_mm"), sem("centred"), sem("squared"), sem("var_mm"), sem("std"), sem("inv"), sem("scaled"), sem("ln_out"))
        h_mm, h_sb, mlp_mm = sem("h_mm"), sem("h_sb"), sem("mlp_mm")
        up_mm, up_sb, up_out = sem("up_mm"), sem("up_sb"), slot_sems("up_out", 2)
        idx2_ready, g_in, e_in = sem("idx2_ready"), slot_sems("g_in"), slot_sems("e_in", 2)
        h1_mm, h1_sb, h2_mm, h2_sb, w_mm = sem("h1_mm"), sem("h1_sb"), sem("h2_mm"), sem("h2_sb"), sem("w_mm")
        hot2_ready, u_ready, vy_ready, t1_ready, t2_ready, w_used, msgs_ready, g_used = (
            sem("hot2_ready"), sem("u_ready"), sem("vy_ready"), sem("t1_ready"), sem("t2_ready"), sem("w_used"), sem("msgs_ready"), sem("g_used"))
        late_hots_ready = sem("late_hots_ready")
        square_ready, square2_ready, rel_ready, odd_step = sem("square_ready"), sem("square2_ready"), sem("rel_ready"), sem("odd_step")
        sum2_ready, acc2_step, acc2_zero = sem("sum2_ready"), sem("acc2_step"), sem("acc2_zero")
        fin_mm, fin_out = sem("fin_mm"), sem("fin_out")

        def loop(eng, body):
            body(0, True)
            with eng.Fori(1, ITERS) as i:
                body(i, False)

        def loop_ahead(eng, body):
            body(0, True, False)
            with eng.Fori(1, ITERS - 1) as i:
                body(i, False, False)
            body(ITERS - 1, False, True)

        STAGES = 8

        def stage(t):
            return rowsf[:, (t % STAGES) * 3 * D:(t % STAGES + 1) * 3 * D]

        def stages_of(b):
            return len(range(b, NODE_TILES, STAGES))

        node_tiles = -(-N // P)

        def chunk_tiles(j):
            return range(CT * j, min(CT * (j + 1), node_tiles))

        def width(j):
            return len(chunk_tiles(j)) * P

        def node_cols(j):
            return slice(j * CW, j * CW + width(j))

        def hidden(j, m):
            at = ((j % 2) * (HID // P) + m) * CW
            return hbuf[:, at:at + width(j)]

        def tile_cols(t):
            return slice(t * P, (t + 1) * P)

        dst_flat = a["dst_flat"]
        block = ctx.enter_context(nc.Block())

        @block.sync
        def _(sp):
            sp.dma_start(wqkv[:], a["wqkv"]).then_inc(ld["x"], 16)
            sp.dma_start(bqkv[:], a["bqkv"].partition_broadcast(P)).then_inc(ld["x"], 16)
            for j in range(2):
                cs = slice(j * NW // 2, (j + 1) * NW // 2)
                sp.dma_start(xT[:, cs], a["xT"][:, cs]).then_inc(ld_x[j], 16)
            sp.dma_start(dst_i[:], a["dst_col"]).then_inc(ld["graph"], 16)
            sp.dma_start(base_i[:], a["dst_first"].partition_broadcast(P)).then_inc(ld["graph"], 16)
            sp.dma_start(consts[:], a["consts"]).then_inc(ld["const"], 16)
            sp.dma_start(vecs[:], a["vecs"]).then_inc(ld["const"], 16)
            sp.dma_start(src_col[:], a["src_col"]).then_inc(ld["src"], 16)
            for t in range(NODE_TILES):
                sp.wait_ge(qkv_sb, t + 1)
                st = stage(t)
                sp.dma_start(q_tab[t * P:(t + 1) * P, :], st[:, 0:D]).then_inc(qkv_out[t % STAGES], 16)
                sp.dma_start(kv_tab[t * P:(t + 1) * P, :], st[:, D:3 * D]).then_inc(qkv_out[t % STAGES], 16)
            for g in range(16):
                sp.dma_start(emb[g * NB:(g + 1) * NB, :], a["r_flat"][g * GE:(g + 1) * GE].partition_broadcast(NB)).then_inc(ld["r"], 16)
            sp.dma_start(weights[:], a["weights"]).then_inc(ld["weights"], 16)
            sp.dma_start(yvec[:], a["attr_col"]).then_inc(ld["attr"], 16)
            sp.dma_start(b2f[0:1, 0, :], a["mlp_b2"]).then_inc(ld["weights"], 16)
            for b in range(STAGES):
                sp.wait_ge(qkv_out[b], 32 * stages_of(b))

            def loads(i, first):
                for s in range(SLOTS):
                    if not first:
                        sp.wait_ge(qe_ready, SLOTS * i + s - SLOTS + 1)
                    _, base = nc.values_load_multi_w_load_instructions(
                        base_i[0:1, bass.ds(i * BODY + s * QT, QT)], engines=(ET.SP,), min_val=0, max_val=N,
                        skip_runtime_bounds_check_because="destinations are node numbers")
                    sp.dma_start(dstb[:, s, :], dst_flat[bass.ds((i * BODY + s * QT) * P, QC)].partition_broadcast(P)).then_inc(a_in[s], 16)
                    for k in range(QT):
                        sp.dma_start(qwin[:, s, k, :], q_tab[bass.ds(base[k], P), :]).then_inc(a_in[s], 16)
            loop(sp, loads)

            sp.wait_ge(r_exp, 1)
            for g in range(16):
                sp.dma_start(emb_rows[:, g * GE:(g + 1) * GE], emb[g * NB:(g + 1) * NB, :]).then_inc(emb_out, 16)

            sp.wait_ge(score_ready, SLOTS * ITERS)
            sp.dma_start(mask_dst.rearrange("p (c e) -> p c e", c=TC), dst_flat.rearrange("(c p e) -> p c e", p=P, e=P)).then_inc(ld["mask"], 16)
            sp.dma_start(nbr_i[:], a["neighbours"]).then_inc(ld["mask"], 16)
            sp.dma_start(rowi.rearrange("p k n -> p (k n)"), a["tile_ends"].partition_broadcast(H)).then_inc(ld["mask"], 16)
            sp.wait_ge(c_sb, 1)
            sp.dma_start(carry_in, small[0:2 * H * TC, 0:P]).then_inc(c_dma, 16)
            sp.wait_ge(c_dma, 16)
            sp.dma_start(rowbuf[:, :, 0:TPAD], carry_in.rearrange("(k h c) p -> h k (c p)", k=2, h=H)).then_inc(c_dma, 16)
            sp.wait_ge(c_scan, 2)
            sp.dma_start(carry_out[0:H * TC].rearrange("(h c) p -> h (c p)", h=H), rowout[:, 0, 0:TPAD]).then_inc(c_back, 16)
            sp.dma_start(carry_out[H * TC:].rearrange("(h c) p -> h (c p)", h=H), rowout[:, 1, 1:TPAD + 1]).then_inc(c_back, 16)
            sp.wait_ge(c_back, 32)
            sp.dma_start(small[0:2 * H * TC, 0:P], carry_out).then_inc(c_back, 16)

            sp.wait_ge(bprep, 6)
            for k in range(3):
                sp.dma_start(b2rows[k:k + 1, :], b2p[0:1, k, :]).then_inc(b2_in, 16)

            sp.wait_ge(back_sb, TC)

            def loads_v(i, first):
                for s in range(SLOTS):
                    if not first:
                        sp.wait_ge(msg_ready, SLOTS * i + s - SLOTS + 1)
                    sp.dma_start(rows[:, s, :, 0:D], v_edges[:, bass.ds((i * BODY + s * QT) * D, QT * D)]
                                 .rearrange("p (t f) -> p t f", t=QT)).then_inc(v_in[s], 16)
            loop(sp, loads_v)

            for j in range(NCH):
                sp.wait_ge(up_sb, j + 1)
                sp.dma_start(up_tab[node_cols(j), :].rearrange("(t p) f -> p t f", p=P),
                             work[:, j % 2, 0:width(j)].rearrange("p (t f) -> p t f", f=D)).then_inc(up_out[j % 2], 16)

            sp.wait_ge(emb_out, 16 * 16)

            def loads_e(i, first):
                for u in range(2):
                    if not first:
                        sp.wait_ge(h1_mm, 2 * i + u - 1)
                    for half in range(2):
                        sp.dma_start(embb[half * NB:(half + 1) * NB, u, :],
                                     emb_rows[:, bass.ds((i * BODY + (2 * u + half) * QT) * P, QC)]).then_inc(e_in[u], 16)
            loop(sp, loads_e)

            for j in range(NCH):
                sp.wait_ge(scaled, 3 * NCH + j + 1)
                w = min(CW, N - j * CW)
                sp.dma_start(out[:, j * CW:j * CW + w], R[1][:, j * CW:j * CW + w]).then_inc(fin_out, 16)
            sp.wait_ge(fin_out, 16 * NCH)

        def gather_loop(pool, table, width, landed, ready, release):
            limit, zero = pool.alloc_register(f"limit_{width}"), pool.alloc_register(f"zero_{width}")
            pool.reg_mov(limit, N)
            pool.reg_mov(zero, 0)
            def body(i, first):
                for s in range(SLOTS):
                    pool.wait_ge(ready, SLOTS * i + s + 1)
                    if not first:
                        release(i, s)
                    pool.reg_add(limit, limit, zero)
                    for k in range(QT):
                        nc.gpsimd.indirect_dma_start(
                            rows[:, s, k, 0:width], None, table,
                            bass.IndirectOffsetOnAxis(idx[:, s, k:k + 1].bitcast(U32), 0),
                            bounds_check=limit).then_inc(landed[s], 16)
            loop(pool, body)

        @block.gpsimd
        def _(pool):
            for b in range(STAGES):
                pool.wait_ge(qkv_out[b], 32 * stages_of(b))

            def release_kv(i, s):
                pool.wait_ge(prod_ready, SLOTS * i + s - SLOTS + 1)
                pool.wait_ge(v_out[s], 16 * i)
            gather_loop(pool, kv_tab, 2 * D, kv_in, idx_ready, release_kv)

            pool.wait_ge(back_sb, TC)
            nc.gpsimd.memset(acc_odd, 0.0).then_inc(odd_zero, 1)

            def weighted(i, first):
                for s in range(SLOTS):
                    q = SLOTS * i + s
                    pool.wait_ge(exb_ready, q + 1)
                    pool.wait_ge(v_in[s], 16 * (i + 1))
                    if not first:
                        pool.wait_ge(sum_ready, QT * (q - SLOTS + 1))
                    nc.gpsimd.tensor_tensor(msg0[:, s], rows[:, s, :, 0:D], exb[:, s], ALU.mult).then_inc(msg_ready, 1)
            loop(pool, weighted)

            pool.wait_ge(conv, NCH)
            nc.gpsimd.memset(acc[:], 0.0).then_inc(acc2_zero, 1)
            for b in range(2):
                pool.wait_ge(up_out[b], 16 * len(range(b, NCH, 2)))

            def release_up(i, s):
                pool.wait_ge(g_used, SLOTS * i + s - SLOTS + 1)
            gather_loop(pool, up_tab, D, g_in, idx2_ready, release_up)

        @block.tensor
        def _(pe):
            pe.wait_ge(ld["x"], 32)
            for t in range(NODE_TILES):
                if t % (NODE_TILES // 2) == 0:
                    pe.wait_ge(ld_x[t // (NODE_TILES // 2)], 16)
                if t >= 2:
                    pe.wait_ge(qkv_sb, t - 1)
                pe.matmul(ps[:, t % 2, 0:3 * D], xT[:, t * P:(t + 1) * P], wqkv[:], start=True, stop=True).then_inc(qkv_mm, 1)
            pe.wait_ge(qkv_sb, NODE_TILES)

            def queries(i, first):
                for s in range(SLOTS):
                    pe.wait_ge(hotT_ready, SLOTS * i + s + 1)
                    if not first:
                        pe.wait_ge(prod_ready, SLOTS * i + s - SLOTS + 1)
                    for k in range(QT):
                        mm = pe.matmul(ps[:, s, k * P:(k + 1) * P], hot[:, s % 2, k, :], qwin[:, s, k, :], start=True, stop=True)
                    mm.then_inc(qe_ready, 1)
            loop(pe, queries)

            pe.wait_ge(ld["const"], 32)
            pe.wait_ge(ld["weights"], 32)
            pe.wait_ge(score_ready, SLOTS * ITERS)
            if TPAD > NT:
                pe.wait_ge(pad_zero, 1)
            for c in range(TC):
                if c >= 4:
                    pe.wait_ge(tr_sb, c - 3)
                for h in range(H):
                    mm = pe.transpose(ps[:, c % 4, h * P:(h + 1) * P], alpha[:, c * P:(c + 1) * P, h], ident)
                mm.then_inc(tr_mm, 1)
            pe.wait_ge(edge_cols, 2)
            pe.transpose(ps[0:2 * H * TC, 4, 0:P], small[:, P:P + 2 * H * TC], ident).then_inc(c_tr, 1)
            pe.wait_ge(c_back, 48)
            pe.transpose(ps[:, 5, 0:2 * H * TC], small[0:2 * H * TC, 0:P], ident[0:2 * H * TC, 0:2 * H * TC]).then_inc(c_mm, 1)
            pe.wait_ge(exp_ready, H)
            pe.wait_ge(tr_sb, TC)
            for c in range(TC):
                if c >= 4:
                    pe.wait_ge(back_sb, c - 3)
                for h in range(H):
                    mm = pe.transpose(ps[:, c % 4, h * P:(h + 1) * P], sc_t[:, h, c * P:(c + 1) * P], ident)
                mm.then_inc(back_mm, 1)
            pe.wait_ge(back_sb, TC)

            def sums(i, first):
                for s in range(SLOTS):
                    pe.wait_ge(msg_ready, SLOTS * i + s + 1)
                    pe.wait_ge(hot_ready, SLOTS * i + s + 1)
                    pe.wait_ge(late_hots_ready, SLOTS * i + s + 1)
                    if not first:
                        pe.wait_ge(acc_step, 2 * (SLOTS * (i - 1) + s + 1) + 1)
                        pe.wait_ge(odd_step, 2 * (SLOTS * (i - 1) + s + 1) + 1)
                    for k in range(QT):
                        for m, left in enumerate((msg0, exb)):
                            mm = pe.matmul(ps[:, 2 * s + k // 2, (2 * (k % 2) + m) * P:(2 * (k % 2) + m + 1) * P],
                                           left[:, s, k, :], hot_b[:, s, k, :], start=True, stop=True)
                        mm.then_inc(sum_ready, 1)
            loop(pe, sums)

            pe.wait_ge(acc_step, 2 * SLOTS * ITERS + 1)
            pe.wait_ge(odd_step, 2 * SLOTS * ITERS + 1)

            def denominators(j):
                pe.wait_ge(merged, j + 1)
                if j >= 2:
                    pe.wait_ge(conv_a, j - 1)
                for k, t in enumerate(chunk_tiles(j)):
                    mm = pe.matmul(ps[:, 4 + j % 2, k * H:(k + 1) * H], acc[:, 1, tile_cols(t)], ident[:, 0:P:C], start=True, stop=True)
                mm.then_inc(den_mm, 1)

            def inverses(j):
                pe.wait_ge(den_wide, j + 1)
                if j >= 2:
                    pe.wait_ge(conv, j - 1)
                for k, t in enumerate(chunk_tiles(j)):
                    mm = pe.matmul(ps[:, 6 + j % 2, k * P:(k + 1) * P], work[:, j % 2, k * P:(k + 1) * P],
                                   ident, start=True, stop=True)
                mm.then_inc(inv_mm, 1)

            def skip(j):
                if j >= 4:
                    pe.wait_ge(skip_sb, j - 3)
                pe.matmul(ps[:, j % 4, 0:width(j)], wt(W_SKIP), xT[:, node_cols(j)], start=True, stop=True).then_inc(skip_mm, 1)
            for j in range(NCH + 2):
                if j < NCH:
                    denominators(j)
                if j >= 2:
                    inverses(j - 2)
                if j < 4:
                    skip(j)
            for j in range(4, NCH):
                skip(j)
            for j in range(NCH):
                pe.wait_ge(skip_sb, min(j + 5, NCH))
                if j >= 4:
                    pe.wait_ge(ln_in, j - 3)
                pe.matmul(ps[:, j % 4, 0:width(j)], wt(W_OUT), R[0][:, node_cols(j)], start=True, stop=True).then_inc(out1_mm, 1)

            def layer_norm(n):
                for j in range(NCH):
                    g = n * NCH + j
                    pe.wait_ge(ln_in, g + 1)
                    if j >= 2:
                        pe.wait_ge(centred, g - 1)
                    pe.matmul(ps[:, 4 + j % 2, 0:width(j)], ones_mean[:], R[1][:, node_cols(j)], start=True, stop=True).then_inc(mean_mm, 1)

                def variance(j):
                    g = n * NCH + j
                    pe.wait_ge(squared, g + 1)
                    if j >= 2:
                        pe.wait_ge(std, g - 1)
                    for k, t in enumerate(chunk_tiles(j)):
                        mm = pe.matmul(ps[:, 2 + j % 2, k:k + 1], R[2][:, tile_cols(t)], ones_mean[:, 0:1], start=True, stop=True)
                    mm.then_inc(var_mm, 1)

                def to_features(j):
                    g = n * NCH + j
                    pe.wait_ge(inv, g + 1)
                    if j >= 2:
                        pe.wait_ge(scaled, g - 1)
                    for k, t in enumerate(chunk_tiles(j)):
                        mm = pe.matmul(ps[:, 6 + j % 2, k * P:(k + 1) * P], dev[:, t:t + 1].to_broadcast([P, P]), ident, start=True, stop=True)
                    mm.then_inc(inv_spread, 1)
                for j in range(NCH + 2):
                    if j < NCH:
                        variance(j)
                    if j >= 2:
                        to_features(j - 2)
            layer_norm(0)

            for j in range(NCH):
                pe.wait_ge(ln_out, j + 1)
                for m in range(HID // P):
                    n = j * 4 + m
                    if n >= 2:
                        pe.wait_ge(h_sb, n - 1)
                    pe.matmul(ps[:, n % 2, 0:width(j)], wt(W_1 + m * P), R[1][:, node_cols(j)], start=True, stop=True).then_inc(h_mm, 1)
                pe.wait_ge(h_sb, 4 * (j + 1))
                if j >= 2:
                    pe.wait_ge(ln_in, NCH + j - 1)
                for m in range(HID // P):
                    mm = pe.matmul(ps[:, 2 + j % 2, 0:width(j)], wt(W_2 + m * P), hidden(j, m),
                                   start=(m == 0), stop=(m == HID // P - 1))
                mm.then_inc(mlp_mm, 1)
            layer_norm(1)
            layer_norm(2)

            for j in range(NCH):
                pe.wait_ge(scaled, 2 * NCH + j + 1)
                if j >= 2:
                    pe.wait_ge(up_sb, j - 1)
                for k, t in enumerate(chunk_tiles(j)):
                    mm = pe.matmul(ps[:, j % 2, k * P:(k + 1) * P], xT[:, tile_cols(t)], wt(W_UP), start=True, stop=True)
                mm.then_inc(up_mm, 1)
            pe.wait_ge(up_sb, NCH)
            pe.wait_ge(scaled, 3 * NCH)

            def hidden1(i, u, n):
                pe.wait_ge(e_in[u], 32 * (i + 1))
                if not (isinstance(n, int) and n == 0):
                    pe.wait_ge(h1_sb, n)
                pe.matmul(ps[:, 0, :], weights[0:2 * NB, W_M0:W_M0 + P], embb[0:2 * NB, u, :], start=True, stop=True).then_inc(h1_mm, 1)

            def hidden2(u, n):
                pe.wait_ge(h1_sb, n + 1)
                if not (isinstance(n, int) and n == 0):
                    pe.wait_ge(h2_sb, n)
                pe.matmul(ps[:, 1, :], wt(W_M1), h1s[:, u, :], start=True, stop=True).then_inc(h2_mm, 1)

            def edge_weights(i, first, s):
                pe.wait_ge(h2_sb, 2 * i + s // 2 + 1)
                if not first or s >= 2:
                    pe.wait_ge(w_used, SLOTS * i + s - 1)
                half, u = s % 2, s // 2
                pe.matmul(ps[:, 2 + s % 2, :], ones3[0:3, :], b2rep[0:3].rearrange("p t f -> p (t f)"),
                          start=True, stop=False, skip_group_check=True)
                for k in range(QT):
                    mm = pe.matmul(ps[:, 2 + s % 2, k * P:(k + 1) * P], h2s[64 * half:64 * half + 64, u, k * P:(k + 1) * P],
                                   weights[64 * half:64 * half + 64, W_M2:W_M2 + P], start=False, stop=True, skip_group_check=True)
                mm.then_inc(w_mm, 1)

            def sum_quad(i, s, first):
                pe.wait_ge(msgs_ready, SLOTS * i + s + 1)
                pe.wait_ge(hot2_ready, SLOTS * i + s + 1)
                if not (first and s < 2):
                    pe.wait_ge(acc2_step, QT * (SLOTS * i + s - 1) + 1)
                for k in range(QT):
                    for m, left in enumerate((MA, MB)):
                        mm = pe.matmul(ps[:, 4 + 2 * (s % 2) + k // 2, (2 * (k % 2) + m) * P:(2 * (k % 2) + m + 1) * P],
                                       left[:, s % 2, k, :], hot[:, s % 2, k, :], start=True, stop=True)
                    mm.then_inc(sum2_ready, 1)

            def edge_units(i, first, last):
                for u in range(2):
                    n = 2 * i + u
                    ahead = not (last and u == 1)
                    if ahead:
                        hidden1(i + u, 1 - u, n + 1)
                    edge_weights(i, first, 2 * u)
                    if not (first and u == 0):
                        sum_quad(i if u else i - 1, (2 * u - 1) % SLOTS, first)
                    if ahead:
                        hidden2(1 - u, n + 1)
                    edge_weights(i, first, 2 * u + 1)
                    sum_quad(i, 2 * u, first)
            pe.wait_ge(prep, 6)
            hidden1(0, 0, 0)
            hidden2(0, 0)
            loop_ahead(pe, edge_units)
            sum_quad(ITERS - 1, SLOTS - 1, False)

            for j in range(NCH):
                if j == 0:
                    pe.wait_ge(acc2_step, QT * SLOTS * ITERS + 1)
                if j >= 2:
                    pe.wait_ge(ln_in, 3 * NCH + j - 1)
                pe.matmul(ps[:, j % 2, 0:width(j)], wt(W_OA), acc[:, 0, node_cols(j)], start=True, stop=False)
                pe.matmul(ps[:, j % 2, 0:width(j)], wt(W_OB), acc[:, 1, node_cols(j)], start=False, stop=True).then_inc(fin_mm, 1)
            layer_norm(3)

        @block.scalar
        def _(act):
            def indices(i, s, ready):
                nc.scalar.copy(idx[:, s, :], src_col[:, bass.ds(i * BODY + s * QT, QT)]).then_inc(ready, 1)

            act.wait_ge(ld["src"], 16)
            for s in range(SLOTS):
                indices(0, s, idx_ready)

            def store_values(i, first):
                for s in range(SLOTS):
                    act.wait_ge(kv_in[s], 16 * QT * (i + 1))
                    act.dma_start(v_edges[:, bass.ds((i * BODY + s * QT) * D, QT * D)].rearrange("p (t f) -> p t f", t=QT),
                                  rows[:, s, :, D:2 * D]).then_inc(v_out[s], 16)
                    indices(i + 1, s, idx_ready)
                if first:
                    act.wait_ge(r_clip, 3)
                    act.wait_ge(ld["const"], 32)
                    nc.scalar.activation(emb, emb, ACT.Square, bias=consts[:, K_NEGB:K_NEGB + 1], scale=float(NB - 1)).then_inc(r_sq, 1)
                    act.wait_ge(r_sq, 1)
                    nc.scalar.activation(emb, emb, ACT.Exp, bias=consts[:, K_LN:K_LN + 1], scale=-0.5).then_inc(r_exp, 1)
            loop(act, store_values)
            act.wait_ge(yprep, 5)
            nc.scalar.activation(ysq[0], ysq[0], ACT.Sqrt).then_inc(yprep, 1)
            act.wait_ge(emb_out, 16 * 16)

            for c in range(TC):
                act.wait_ge(tr_mm, c + 1)
                nc.scalar.copy(sc_t[:, :, c * P:(c + 1) * P], ps[:, c % 4, :].rearrange("p (h e) -> p h e", h=H)).then_inc(tr_sb, 1)
            act.wait_ge(c_tr, 1)
            nc.scalar.copy(small[0:2 * H * TC, 0:P], ps[0:2 * H * TC, 4, 0:P]).then_inc(c_sb, 1)
            for h in range(H):
                act.wait_ge(shifted, h + 1)
                nc.scalar.activation(sc_t[:, h, :], sc_t[:, h, :], ACT.Exp, scale=1.0 / np.sqrt(C).item()).then_inc(exp_ready, 1)
            for c in range(TC):
                act.wait_ge(back_mm, c + 1)
                nc.scalar.copy(alpha[:, c * P:(c + 1) * P, :].rearrange("p t h -> p h t"),
                               ps[:, c % 4, :].rearrange("p (h e) -> p h e", h=H)).then_inc(back_sb, 1)
            act.wait_ge(back_sb, TC)
            for s in range(SLOTS):
                act.wait_ge(v_out[s], 16 * ITERS)

            def one_hots(i, s, n, to, squares, ready):
                for k in range(n):
                    op = nc.scalar.activation(to[:, k, :], iota, ACT.Square, bias=nrel[:, bass.ds(i * BODY + s * QT + k, 1)])
                op.then_inc(squares, 1)
                act.wait_ge(squares, SLOTS * i + s + 1)
                nc.scalar.activation(to[:, 0:n, :], to[:, 0:n, :], ACT.Relu, bias=1.0, scale=-1.0).then_inc(ready, 1)

            act.wait_ge(rel_ready, 1)
            def spread(i, first):
                for s in range(SLOTS):
                    if not first:
                        act.wait_ge(sum_ready, QT * (SLOTS * (i - 1) + s + 1))
                    nc.scalar.copy(exb[:, s].rearrange("p t (h c) -> p (t h) c", h=H),
                                   alpha[:, bass.ds(i * BODY + s * QT, QT), :].rearrange("p t h -> p (t h)").unsqueeze(2)
                                   .to_broadcast([P, QT * H, C])).then_inc(exb_ready, 1)
                    one_hots(i, s, QT - LATE, hot_b[:, s], square_ready, hot_ready)
            loop(act, spread)

            def layer_norm(n, affine=None):
                for j in range(NCH):
                    act.wait_ge(centred, n * NCH + j + 1)
                    nc.scalar.activation(R[2][:, node_cols(j)], R[1][:, node_cols(j)], ACT.Square).then_inc(squared, 1)
                for j in range(NCH):
                    tiles = chunk_tiles(j)
                    act.wait_ge(var_mm, n * NCH + j + 1)
                    nc.scalar.activation(dev[:, tiles[0]:tiles[-1] + 1], ps[:, 2 + j % 2, 0:len(tiles)], ACT.Sqrt,
                                         bias=consts[:, K_EPS:K_EPS + 1]).then_inc(std, 1)
                if affine is not None:
                    for j in range(NCH):
                        act.wait_ge(scaled, n * NCH + j + 1)
                        nc.scalar.activation(R[1][:, node_cols(j)], R[1][:, node_cols(j)], ACT.Identity, bias=vec(affine + 1)).then_inc(ln_out, 1)
            for j in range(NCH):
                tiles = chunk_tiles(j)
                act.wait_ge(conv_b, j + 1)
                if j >= 2:
                    act.wait_ge(inv_mm, j - 1)
                nc.scalar.copy(work[:, j % 2, 0:width(j)].rearrange("p (g c) -> p g c", c=C),
                               den[:, tiles[0]:tiles[-1] + 1, :].rearrange("p t h -> p (t h)").unsqueeze(2)
                               .to_broadcast([P, len(tiles) * H, C])).then_inc(den_wide, 1)
            layer_norm(0, V_L1W)
            for j in range(NCH):
                if j >= 2:
                    act.wait_ge(mlp_mm, j - 1)
                for m in range(HID // P):
                    n = 4 * j + m
                    act.wait_ge(h_mm, n + 1)
                    nc.scalar.activation(hidden(j, m), ps[:, n % 2, 0:width(j)], ACT.Relu, bias=vec(V_B1 + m)).then_inc(h_sb, 1)
            layer_norm(1, V_L2W)
            layer_norm(2)
            for j in range(NCH):
                act.wait_ge(up_mm, j + 1)
                if j >= 2:
                    act.wait_ge(up_out[j % 2], 16 * (j // 2))
                nc.scalar.mul(work[:, j % 2, 0:width(j)], ps[:, j % 2, 0:width(j)], 1.0 / np.sqrt(32).item()).then_inc(up_sb, 1)

            act.wait_ge(acc2_zero, 1)
            for s in range(SLOTS):
                indices(0, s, idx2_ready)

            def silu1(u, n):
                act.wait_ge(h1_mm, n + 1)
                if not (isinstance(n, int) and n < 2):
                    act.wait_ge(h2_mm, n - 1)
                nc.scalar.activation(h1s[:, u, :], ps[:, 0, :], ACT.Silu, bias=vec(V_MB0)).then_inc(h1_sb, 1)

            def silu2(u, n):
                act.wait_ge(h2_mm, n + 1)
                if not (isinstance(n, int) and n < 2):
                    act.wait_ge(w_mm, 2 * n - 2)
                nc.scalar.activation(h2s[:, u, :], ps[:, 1, :], ACT.Silu, bias=vec(V_MB1)).then_inc(h2_sb, 1)

            def edge_units(i, first, last):
                for u in range(2):
                    n = 2 * i + u
                    ahead = not (last and u == 1)
                    for half, silu in enumerate((silu1, silu2)):
                        s = 2 * u + half
                        if ahead:
                            silu(1 - u, n + 1)
                        if not first or s >= 2:
                            act.wait_ge(sum2_ready, QT * (SLOTS * i + s - 1))
                        one_hots(i, s, QT, hot[:, s % 2], square2_ready, hot2_ready)
                        if not last:
                            act.wait_ge(g_in[s], 16 * QT * (i + 1))
                            indices(i + 1, s, idx2_ready)
            silu1(0, 0)
            silu2(0, 0)
            loop_ahead(act, edge_units)
            layer_norm(3)

        @block.vector
        def _(dve):
            v = nc.vector
            yv = yvec[:].rearrange("p (t c) -> p t c", c=3)

            dve.wait_ge(ld["x"], 32)
            for t in range(NODE_TILES):
                dve.wait_ge(qkv_mm, t + 1)
                if t >= STAGES:
                    dve.wait_ge(qkv_out[t % STAGES], 32 * (t // STAGES))
                v.tensor_tensor(stage(t), ps[:, t % 2, 0:3 * D], bqkv[:], ALU.add).then_inc(qkv_sb, 1)
            dve.wait_ge(ld["graph"], 32)
            dve.wait_ge(ld["const"], 32)
            v.tensor_tensor(rel[:], dst_i[:], base_i[:], ALU.subtract).then_inc(prep, 1)
            v.tensor_scalar(win[:], base_i[:], consts[:, K_COL:K_COL + 1], None, ALU.add).then_inc(prep, 1)
            v.memset(ones_mean[:], 1.0 / D).then_inc(prep, 1)
            v.memset(ones3[:], 1.0).then_inc(prep, 1)
            if TPAD > NT:
                v.memset(alpha[:, NT:TPAD, :], 0.0).then_inc(pad_zero, 1)
            dve.wait_ge(prep, 4)

            def radius():
                dve.wait_ge(ld["r"], 16 * 16)
                v.tensor_scalar(emb_m, emb, 1.0, 1e4, ALU.is_gt, ALU.mult).then_inc(r_clip, 1)
                dve.wait_ge(r_clip, 1)
                v.tensor_scalar(emb, emb, 0.0, 1.0, ALU.max, ALU.min).then_inc(r_clip, 1)
                dve.wait_ge(r_clip, 2)
                v.tensor_tensor(emb, emb, emb_m, ALU.add).then_inc(r_clip, 1)

            def product(i, s, first):
                q = SLOTS * i + s
                dve.wait_ge(qe_ready, q + 1)
                dve.wait_ge(kv_in[s], 16 * QT * (i + 1))
                if not first:
                    dve.wait_ge(score_ready, q - 1)
                v.tensor_tensor(work[:, s % 2, :].rearrange("p (t f) -> p t f", t=QT),
                                ps[:, s, :].rearrange("p (t f) -> p t f", t=QT), rows[:, s, :, 0:D], ALU.mult).then_inc(prod_ready, 1)
                dve.wait_ge(prod_ready, q + 1)
                v.tensor_reduce(alpha[:, bass.ds(i * BODY + s * QT, QT), :].rearrange("p t h -> p (t h)"),
                                work[:, s % 2, :].rearrange("p (g c) -> p g c", c=C), AX.X, ALU.add).then_inc(score_ready, 1)

            def scores(i, first):
                for s in range(SLOTS):
                    q = SLOTS * i + s
                    dve.wait_ge(a_in[s], 16 * (1 + QT) * (i + 1))
                    if not first or s >= 2:
                        dve.wait_ge(qe_ready, q - 1)
                    v.tensor_tensor(hot[:, s % 2], dstb[:, s, :].rearrange("p (t e) -> p t e", t=QT),
                                    win[:, bass.ds(i * BODY + s * QT, QT)].unsqueeze(2).to_broadcast([P, QT, P]),
                                    ALU.is_equal).then_inc(hotT_ready, 1)
                    if not (first and s == 0):
                        product(i if s else i - 1, (s - 1) % SLOTS, first and s < 3)
                if first:
                    radius()
            loop(dve, scores)
            product(ITERS - 1, SLOTS - 1, False)

            v.tensor_scalar(nrel, rel[:], -1.0, None, ALU.mult).then_inc(rel_ready, 1)
            dve.wait_ge(ld["attr"], 16)
            for n, c in enumerate(range(3)):
                if c:
                    dve.wait_ge(yprep, 2 * n - 1)
                v.tensor_tensor(ysq[min(c, 1)], yv[:, :, c], yv[:, :, c], ALU.mult).then_inc(yprep, 1)
                if c:
                    dve.wait_ge(yprep, 2 * n)
                    v.tensor_tensor(ysq[0], ysq[0], ysq[1], ALU.add).then_inc(yprep, 1)
            dt = masks[:, 2, :].rearrange("p (c e) -> p c e", c=TC)
            mf = masks[:, 0, :].rearrange("p (c e) -> p c e", c=TC)
            m1 = masks[:, 1, :].rearrange("p (c e) -> p c e", c=TC)
            dve.wait_ge(ld["mask"], 16 * 3)
            v.tensor_copy(dt, mask_dst.rearrange("p (c e) -> p c e", c=TC)).then_inc(mask_ready, 1)
            v.tensor_copy(nbr[:], nbr_i[:].rearrange("p (k c) -> p k c", k=2)).then_inc(mask_ready, 1)
            dve.wait_ge(mask_ready, 2)
            v.tensor_tensor(mf[:, :, 1:P], dt[:, :, 1:P], dt[:, :, 0:P - 1], ALU.is_equal).then_inc(mask_ready, 1)
            v.memset(mf[:, :, 0:1], 0.0).then_inc(mask_ready, 1)
            v.tensor_tensor(m1, dt, nbr[:, 0, :].unsqueeze(2).to_broadcast([P, TC, P]), ALU.is_equal).then_inc(mask_ready, 1)
            dve.wait_ge(mask_ready, 5)
            v.tensor_tensor(dt, dt, nbr[:, 1, :].unsqueeze(2).to_broadcast([P, TC, P]), ALU.is_equal).then_inc(mask_ready, 1)
            dve.wait_ge(mask_ready, 6)
            v.tensor_scalar(masks, masks, 0.5, 2 * BIG, ALU.subtract, ALU.mult).then_inc(mask_ready, 1)
            dve.wait_ge(mask_ready, 7)
            dve.wait_ge(tr_sb, TC)
            for h in range(H):
                v.tensor_tensor_scan(fw_t[:, h, :], masks[:, 0, :], sc_t[:, h, :], -BIG, ALU.min, ALU.max).then_inc(scan_f, 1)
            v.memset(mback[:, TPAD - 1:TPAD], -BIG).then_inc(mask_ready, 1)
            v.tensor_copy(mback[:, 0:TPAD - 1], masks[:, 0, 1:TPAD]).then_inc(mask_ready, 1)
            dve.wait_ge(mask_ready, 9)
            for h in range(H):
                dve.wait_ge(scan_f, h + 1)
                v.tensor_tensor_scan(tot_t[:, h, ::-1], mback[:, ::-1], fw_t[:, h, ::-1], -BIG, ALU.min, ALU.max).then_inc(scan_b, 1)
            K = H * TC
            v.tensor_copy(small[:, P:P + K].rearrange("p (h c) -> p h c", h=H),
                          fw_t.rearrange("p h (c e) -> p h c e", c=TC)[:, :, :, P - 1]).then_inc(edge_cols, 1)
            dve.wait_ge(scan_b, H)
            v.tensor_copy(small[:, P + K:P + 2 * K].rearrange("p (h c) -> p h c", h=H),
                          tot_t.rearrange("p h (c e) -> p h c e", c=TC)[:, :, :, 0]).then_inc(edge_cols, 1)
            for s in range(SLOTS):
                dve.wait_ge(v_out[s], 16 * ITERS)
            for k in range(2):
                v.tensor_tensor(rowmask[:, k, :], rowi[:, 2 * k, :], rowi[:, 2 * k + 1, :], ALU.is_equal).then_inc(mask_ready, 1)
            dve.wait_ge(mask_ready, 11)
            v.tensor_scalar(rowmask, rowmask, 0.5, 2 * BIG, ALU.subtract, ALU.mult).then_inc(mask_ready, 1)
            v.memset(rowout[:, 0, 0:1], -BIG).then_inc(mask_ready, 1)
            v.memset(rowout[:, 1, TPAD:TPAD + 1], -BIG).then_inc(mask_ready, 1)
            dve.wait_ge(mask_ready, 14)
            dve.wait_ge(c_dma, 32)
            v.tensor_tensor_scan(rowout[:, 0, 1:TPAD + 1], rowmask[:, 0, :], rowbuf[:, 0, :], -BIG, ALU.min, ALU.max).then_inc(c_scan, 1)
            v.tensor_tensor_scan(rowout[:, 1, 0:TPAD][:, ::-1], rowmask[:, 1, ::-1], rowbuf[:, 1, ::-1], -BIG, ALU.min, ALU.max).then_inc(c_scan, 1)
            dve.wait_ge(yprep, 6)
            v.tensor_scalar(ysq[0], ysq[0], 1e-12, None, ALU.add).then_inc(yprep, 1)
            dve.wait_ge(yprep, 7)
            v.reciprocal(ysq[1], ysq[0]).then_inc(yprep, 1)
            dve.wait_ge(yprep, 8)
            v.scalar_tensor_tensor(out=yv, in0=yv, scalar=np.sqrt(3).item(),
                                   in1=ysq[1].unsqueeze(2).to_broadcast([P, NT, 3]), op0=ALU.mult, op1=ALU.mult).then_inc(yprep, 1)
            dve.wait_ge(ld["weights"], 32)
            v.tensor_scalar(weights[:, W_M2 + 96:W_M2 + 128], weights[:, W_M2 + 96:W_M2 + 128],
                            1.0 / np.sqrt(3).item(), None, ALU.mult).then_inc(prep, 1)
            v.tensor_scalar(b2f[0:1, 0, 96:128], b2f[0:1, 0, 96:128], 1.0 / np.sqrt(3).item(), None, ALU.mult).then_inc(bprep, 1)
            for k in range(3):
                dve.wait_ge(bprep, 2 * k + 1)
                v.tensor_copy(b2p[0:1, k, :], b2f[0:1, k, :]).then_inc(bprep, 1)
                if k < 2:
                    dve.wait_ge(bprep, 2 * k + 2)
                    v.tensor_tensor(b2f[0:1, k + 1, :], b2f[0:1, k, :], b2p[0:1, k, :], ALU.subtract).then_inc(bprep, 1)
            dve.wait_ge(c_mm, 1)
            v.tensor_copy(small[:, P:P + 2 * K], ps[:, 5, 0:2 * K]).then_inc(c_use, 1)
            dve.wait_ge(c_use, 1)
            n = 0
            for k in range(2):
                for h in range(H):
                    v.tensor_tensor(fw_t[:, h, :].rearrange("p (c e) -> p c e", c=TC),
                                    masks[:, 1 + k, :].rearrange("p (c e) -> p c e", c=TC),
                                    small[:, P + k * K + h * TC:P + k * K + (h + 1) * TC].unsqueeze(2).to_broadcast([P, TC, P]),
                                    ALU.min).then_inc(mx, 1)
                for h in range(H):
                    dve.wait_ge(mx, n + H)
                    v.tensor_tensor(tot_t[:, h, :], tot_t[:, h, :], fw_t[:, h, :], ALU.max).then_inc(mx, 1)
                    n += 1
                n += H
                dve.wait_ge(mx, n)
            for h in range(H):
                v.tensor_tensor(sc_t[:, h, :], sc_t[:, h, :], tot_t[:, h, :], ALU.subtract).then_inc(shifted, 1)
            v.memset(acc[:], 0.0).then_inc(acc_zero, 1)
            dve.wait_ge(mx, 4 * H)
            dve.wait_ge(back_sb, TC)

            def bases(i, s, n=QT):
                _, base = nc.values_load_multi_w_load_instructions(
                    base_i[0:1, bass.ds(i * BODY + s * QT, n)], engines=(ET.DVE,), min_val=0, max_val=N,
                    skip_runtime_bounds_check_because="destinations are node numbers")
                return base

            def add_tile(i, s, k, base, bank, ready, step):
                t = QT * (SLOTS * i + s) + k
                if k % 2 == 0:
                    dve.wait_ge(ready, t + 2)
                dve.wait_ge(step, t + 1)
                to = acc[:, :, bass.ds(base[k], P)]
                v.tensor_tensor(to, to, ps[:, bank + k // 2, (k % 2) * 256:(k % 2) * 256 + 256]
                                .rearrange("p (m f) -> p m f", m=2), ALU.add).then_inc(step, 1)

            def add_to_pair(i, s, k, base):
                q = SLOTS * i + s
                if k % 2 == 0:
                    dve.wait_ge(sum_ready, QT * q + k + 2)
                total, step = ((acc, acc_step), (acc_odd, odd_step))[k % 2]
                dve.wait_ge(step, 2 * q + k // 2 + 1)
                to = total[:, :, bass.ds(base[k], P)]
                v.tensor_tensor(to, to, ps[:, 2 * s + k // 2, (k % 2) * 256:(k % 2) * 256 + 256]
                                .rearrange("p (m f) -> p m f", m=2), ALU.add).then_inc(step, 1)

            v.memset(flag[:, 0:1], 0.0).then_inc(acc_step, 1)
            v.memset(flag[:, 1:2], 0.0).then_inc(odd_step, 1)
            dve.wait_ge(acc_zero, 1)
            dve.wait_ge(odd_zero, 1)

            def late_hots(q, b):
                v.tensor_tensor(hot_b[:, b, QT - LATE:QT, :], iota.unsqueeze(1).to_broadcast([P, LATE, P]),
                                rel[:, bass.ds(q * QT + QT - LATE, LATE)].unsqueeze(2).to_broadcast([P, LATE, P]),
                                ALU.is_equal).then_inc(late_hots_ready, 1)

            def sum_edges(i, first, last):
                base = bases(i, 0, BODY)
                for s in range(SLOTS):
                    q = SLOTS * i + s
                    if not (last and s == SLOTS - 1):
                        if not (first and s < SLOTS - 1):
                            dve.wait_ge(sum_ready, QT * (q - SLOTS + 2))
                        late_hots(q + 1, (s + 1) % SLOTS)
                    for k in range(QT):
                        add_to_pair(i, s, k, base[s * QT:])
            late_hots(0, 0)
            loop_ahead(dve, sum_edges)

            dve.wait_ge(acc_step, 2 * SLOTS * ITERS + 1)
            dve.wait_ge(odd_step, 2 * SLOTS * ITERS + 1)
            for j in range(NCH):
                cs = node_cols(j)
                v.tensor_tensor(acc[:, :, cs], acc[:, :, cs], acc_odd[:, :, cs], ALU.add).then_inc(merged, 1)
            def invert_sums(j):
                tiles = chunk_tiles(j)
                d = den[:, tiles[0]:tiles[-1] + 1, :].rearrange("p t h -> p (t h)")
                dve.wait_ge(den_mm, j + 1)
                v.tensor_scalar(d, ps[:, 4 + j % 2, 0:len(tiles) * H], 1e-30, None, ALU.max).then_inc(conv_a, 1)
                dve.wait_ge(conv_a, j + 1)
                v.reciprocal(d, d).then_inc(conv_b, 1)

            def divide(j):
                cs = node_cols(j)
                dve.wait_ge(inv_mm, j + 1)
                dve.wait_ge(merged, NCH)
                v.tensor_tensor(R[0][:, cs], acc[:, 0, cs], ps[:, 6 + j % 2, 0:width(j)], ALU.mult).then_inc(conv, 1)
            for j in range(NCH + 3):
                if j < NCH:
                    invert_sums(j)
                if j >= 3:
                    divide(j - 3)
            for j in range(NCH):
                cs = node_cols(j)
                dve.wait_ge(conv, j + 1)
                dve.wait_ge(skip_mm, j + 1)
                v.scalar_tensor_tensor(out=R[0][:, cs], in0=ps[:, j % 4, 0:width(j)], scalar=vec(V_BSKIP), in1=R[0][:, cs],
                                       op0=ALU.add, op1=ALU.add).then_inc(skip_sb, 1)
            for j in range(NCH):
                cs = node_cols(j)
                dve.wait_ge(out1_mm, j + 1)
                v.scalar_tensor_tensor(out=R[1][:, cs], in0=ps[:, j % 4, 0:width(j)], scalar=vec(V_BOUT), in1=xT[:, cs],
                                       op0=ALU.add, op1=ALU.add).then_inc(ln_in, 1)

            def layer_norm(n, to=None, affine=None):
                to = R[1] if to is None else to
                for j in range(NCH):
                    g, cs = n * NCH + j, node_cols(j)
                    dve.wait_ge(mean_mm, g + 1)
                    v.tensor_tensor(R[1][:, cs], R[1][:, cs], ps[:, 4 + j % 2, 0:width(j)], ALU.subtract).then_inc(centred, 1)

                def invert(j):
                    tiles = chunk_tiles(j)
                    d = dev[:, tiles[0]:tiles[-1] + 1]
                    dve.wait_ge(std, n * NCH + j + 1)
                    v.reciprocal(d, d).then_inc(inv, 1)

                def scale(j):
                    cs, spread = node_cols(j), ps[:, 6 + j % 2, 0:width(j)]
                    dve.wait_ge(inv_spread, n * NCH + j + 1)
                    if affine is None:
                        v.tensor_tensor(to[:, cs], R[1][:, cs], spread, ALU.mult).then_inc(scaled, 1)
                    else:
                        v.scalar_tensor_tensor(out=to[:, cs], in0=R[1][:, cs], scalar=vec(affine), in1=spread,
                                               op0=ALU.mult, op1=ALU.mult).then_inc(scaled, 1)
                for j in range(NCH + 3):
                    if j < NCH:
                        invert(j)
                    if j >= 3:
                        scale(j - 3)
            layer_norm(0, affine=V_L1W)
            for j in range(NCH):
                cs = node_cols(j)
                dve.wait_ge(mlp_mm, j + 1)
                v.scalar_tensor_tensor(out=R[1][:, cs], in0=ps[:, 2 + j % 2, 0:width(j)], scalar=vec(V_B2), in1=R[1][:, cs],
                                       op0=ALU.add, op1=ALU.add).then_inc(ln_in, 1)
            layer_norm(1, affine=V_L2W)
            for j in range(NCH):
                cs = node_cols(j)
                dve.wait_ge(ln_out, NCH + j + 1)
                v.tensor_tensor(R[1][:, cs], R[1][:, cs], xT[:, cs], ALU.add).then_inc(ln_in, 1)
            layer_norm(2, to=xT)

            dve.wait_ge(b2_in, 48)
            v.tensor_copy(b2rep[0:3], b2rows[0:3].unsqueeze(1).to_broadcast([3, QT, D])).then_inc(prep, 1)
            v.memset(flag[:, 1:2], 0.0).then_inc(acc2_step, 1)
            dve.wait_ge(acc2_zero, 1)
            dve.wait_ge(acc2_step, 1)
            dve.wait_ge(scaled, 3 * NCH)

            def messages(i, first):
                for s in range(SLOTS):
                    q = SLOTS * i + s
                    b = s % 2
                    before = None if first and s == 0 else (i if s else i - 1, (s - 1) % SLOTS)
                    if before:
                        base = bases(*before)

                    def add(k):
                        if before:
                            add_tile(*before, k, base, 4 + 2 * (before[1] % 2), sum2_ready, acc2_step)
                    g = rows[:, s, :, 0:D]
                    w = ps[:, 2 + b, :].rearrange("p (t f) -> p t f", t=QT)
                    ss = g[:, :, 0:32]
                    vv = g[:, :, 32:128].rearrange("p t (c m) -> p t c m", c=3)
                    y = yvec[:, bass.ds((i * BODY + s * QT) * 3, 3 * QT)].rearrange("p (t c) -> p t c", c=3) \
                        .unsqueeze(3).to_broadcast([P, QT, 3, 32])
                    vyb = vy[:, b].rearrange("p t (c m) -> p t c m", c=3)
                    dve.wait_ge(g_in[s], 16 * QT * (i + 1))
                    v.tensor_tensor(vyb, vv, y, ALU.mult).then_inc(vy_ready, 1)
                    dve.wait_ge(w_mm, q + 1)
                    v.tensor_tensor(ub[:, b], w[:, :, 32:64], ss, ALU.mult).then_inc(u_ready, 1)
                    dve.wait_ge(vy_ready, q + 1)
                    v.tensor_tensor(tb[:, 2 * b], vyb[:, :, 0], vyb[:, :, 1], ALU.add).then_inc(t1_ready, 1)
                    add(0)
                    if not first or s >= 2:
                        dve.wait_ge(sum2_ready, QT * (q - 1))
                    v.tensor_tensor(MA[:, b, :, 0:32], w[:, :, 0:32], ss, ALU.mult)
                    dve.wait_ge(t1_ready, q + 1)
                    v.tensor_tensor(tb[:, 2 * b + 1], tb[:, 2 * b], vyb[:, :, 2], ALU.add).then_inc(t2_ready, 1)
                    add(1)
                    v.tensor_tensor(MB[:, b, :, 32:128].rearrange("p t (c m) -> p t c m", c=3),
                                    w[:, :, 64:96].unsqueeze(2).to_broadcast([P, QT, 3, 32]), vv, ALU.mult).then_inc(g_used, 1)
                    add(2)
                    dve.wait_ge(t2_ready, q + 1)
                    v.tensor_tensor(MB[:, b, :, 0:32], w[:, :, 96:128], tb[:, 2 * b + 1], ALU.mult).then_inc(w_used, 1)
                    dve.wait_ge(u_ready, q + 1)
                    v.tensor_tensor(MA[:, b, :, 32:128].rearrange("p t (c m) -> p t c m", c=3),
                                    ub[:, b].unsqueeze(2).to_broadcast([P, QT, 3, 32]), y, ALU.mult).then_inc(msgs_ready, 1)
                    add(3)
            loop(dve, messages)
            base = bases(ITERS - 1, SLOTS - 1)
            for k in range(QT):
                add_tile(ITERS - 1, SLOTS - 1, k, base, 4 + 2 * ((SLOTS - 1) % 2), sum2_ready, acc2_step)

            for j in range(NCH):
                cs = node_cols(j)
                dve.wait_ge(fin_mm, j + 1)
                v.scalar_tensor_tensor(out=R[1][:, cs], in0=ps[:, j % 2, 0:width(j)], scalar=1.0 / (8.0 * 16.0), in1=xT[:, cs],
                                       op0=ALU.mult, op1=ALU.add).then_inc(ln_in, 1)
            layer_norm(3)


_SHAPES = {
    "consts": (P, K_N), "vecs": (P, V_N), "weights": (P, W_N), "wqkv": (P, 3 * D), "bqkv": (3 * D,), "xT": (P, NW),
    "src_col": (P, NT + BODY), "dst_col": (P, NT), "dst_first": (NT,), "dst_flat": (TPAD * P,), "neighbours": (P, 2 * TC),
    "tile_ends": (4 * TPAD,), "r_flat": (NT * P,), "attr_col": (P, 3 * NT), "mlp_b2": (1, D),
}


def layout(x):
    f = {k: np.asarray(v) for k, v in x.items()}

    def l0(n):
        return f["L0_gnn_" + n]

    def l1(n):
        return f["L1_gnn_" + n]

    a = {}
    c = np.zeros((P, K_N), np.float32)
    c[:, K_ID:K_ID + P] = np.eye(P)
    c[:, K_IOTA:K_IOTA + P] = np.arange(P)[None]
    c[:, K_COL] = np.arange(P)
    c[:, K_NEGB] = -(np.arange(P) % NB)
    c[:, K_LN] = 0.5 * np.log(NB)
    c[:, K_EPS] = EPS
    a["consts"] = c
    v = np.zeros((P, V_N), np.float32)
    for j, n in ((V_BSKIP, "bskip"), (V_BOUT, "bout"), (V_L1W, "ln1_w"), (V_L1B, "ln1_b"), (V_L2W, "ln2_w"), (V_L2B, "ln2_b"), (V_B2, "b2")):
        v[:, j] = l0(n)
    v[:, V_B1:V_B1 + 4] = l0("b1").reshape(4, P).T
    for h in range(2):
        v[64 * h:64 * h + 64, V_MB0] = l1("mlp_b0")
        v[64 * h:64 * h + 64, V_MB1] = l1("mlp_b1")
    a["vecs"] = v
    w = np.zeros((P, W_N), np.float32)
    w[:, W_SKIP:W_SKIP + D] = l0("Wskip").T
    w[:, W_OUT:W_OUT + D] = l0("Wout").T
    w[:, W_1:W_1 + HID] = l0("W1").T
    w[:, W_2:W_2 + HID] = l0("W2").T.reshape(4, P, D).transpose(1, 0, 2).reshape(P, HID)
    w[0:32, W_UP:W_UP + 32] = l1("W_up0")
    w[0:32, W_OA:W_OA + 32] = l1("W_out0")[0:32]
    w[0:32, W_OB:W_OB + 32] = l1("W_out0")[32:64]
    for q in range(3):
        w[32 + q:D:3, W_UP + 32 + 32 * q:W_UP + 64 + 32 * q] = l1("W_up1")
        w[32 + 32 * q:64 + 32 * q, W_OA + 32 + q:W_OA + D:3] = l1("W_out1")[0:32]
        w[32 + 32 * q:64 + 32 * q, W_OB + 32 + q:W_OB + D:3] = l1("W_out1")[32:64]
    for h in range(2):
        w[64 * h:64 * h + 64, W_M1 + 64 * h:W_M1 + 64 * h + 64] = l1("mlp_w1")
        w[64 * h:64 * h + 64, W_M2:W_M2 + D] = l1("mlp_w2")
        w[NB * h:NB * h + NB, W_M0 + 64 * h:W_M0 + 64 * h + 64] = l1("mlp_w0")
    a["weights"] = w
    a["wqkv"] = np.concatenate([l0("Wq").T, l0("Wk").T, l0("Wv").T], 1)
    a["bqkv"] = np.concatenate([l0("bq"), l0("bk"), l0("bv")])
    a["xT"] = np.zeros((P, NW), np.float32)
    a["xT"][:, :N] = f["x"].T
    src = np.zeros((NT + BODY) * P, np.int32)
    src[:E] = f["src"]
    dst = np.full(TPAD * P, N, np.int32)
    dst[:E] = f["dst"]
    a["src_col"] = src.reshape(-1, P).T
    tiles = dst.reshape(TPAD, P)
    a["dst_col"] = tiles[:NT].T
    a["dst_first"] = tiles[:NT, 0]
    a["dst_flat"] = dst
    first, last = tiles[:, 0], tiles[:, -1]
    before = np.concatenate([[-1], last[:-1]]).astype(np.int32)
    after = np.concatenate([first[1:], [-1]]).astype(np.int32)
    a["neighbours"] = np.concatenate([before.reshape(TC, P).T, after.reshape(TC, P).T], 1)
    a["tile_ends"] = np.concatenate([last, before, first, after])
    r = np.zeros(NT * P, np.float32)
    r[:E] = f["edge_weight"]
    a["r_flat"] = r
    e = np.zeros((NT * P, 3), np.float32)
    e[:E] = f["edge_attr_3"]
    a["attr_col"] = e.reshape(NT, P, 3).transpose(1, 0, 2).reshape(P, 3 * NT)
    a["mlp_b2"] = l1("mlp_b2").reshape(1, D)
    return {k: np.ascontiguousarray(t) for k, t in a.items()}


def kernel(**inputs):
    import concourse.bacc as bacc
    from concourse.bass_utils import run_bass_kernel_spmd as run

    nc = bacc.Bacc("TRN2", target_bir_lowering=False, num_devices=1)
    arrays = layout(inputs)
    aps = {}
    for k, shape in _SHAPES.items():
        assert arrays[k].shape == shape, (k, arrays[k].shape, shape)
        aps[k] = nc.dram_tensor("in_" + k, shape, mybir.dt.from_np(arrays[k].dtype), kind="ExternalInput").ap()
    out = nc.dram_tensor("out_t", (D, N), F32, kind="ExternalOutput").ap()
    build(nc, aps, out)
    r = run(nc, [{"in_" + k: t for k, t in arrays.items()}], core_ids=[0])
    return np.ascontiguousarray(r.results[0]["out_t"].T)
```
